# Optimizing a Trainium2 kernel written in Bass

```python
import numpy as np
import jax
import jax.numpy as jnp

def _softmax(x, axis=-1):
    return jax.nn.softmax(x, axis=axis)

def _gelu(x):
    return jax.nn.gelu(x, approximate=True)

def _silu(x):
    return jax.nn.silu(x)

def _sigmoid(x):
    return jax.nn.sigmoid(x)

def _layernorm(x, axis=-1, eps=1e-05):
    m = jnp.mean(x, axis=axis, keepdims=True)
    v = jnp.var(x, axis=axis, keepdims=True)
    return (x - m) / jnp.sqrt(v + eps)

def _scatter_add(tgt, idx, src, axis=0):
    return tgt.at[idx].add(src)

def _segment_sum(src, seg, n):
    return jax.ops.segment_sum(src, seg, n)
kernel_name = 'mk_seq_preln_d1_jaxref_r4_9b5737'

def setup_inputs(seed: int=0):
    np.random.seed(seed)
    _w = jnp.asarray

    def _L0_attn_setup():
        import jax, jax.numpy as jnp
        import numpy as np
        DIM = 256
        HID = 1024
        NUM_HEADS = 4
        WINDOW = 128
        NUM_PM = 64
        NEG = -1e+30

        def _swa(x_in, wq, wk, wv, wo):
            B, S, D = x_in.shape
            h, dh = (NUM_HEADS, D // NUM_HEADS)
            q = (x_in @ wq.T).reshape(B, S, h, dh).transpose(0, 2, 1, 3)
            k = (x_in @ wk.T).reshape(B, S, h, dh).transpose(0, 2, 1, 3)
            v = (x_in @ wv.T).reshape(B, S, h, dh).transpose(0, 2, 1, 3)
            i = jnp.arange(S)[:, None]
            j = jnp.arange(S)[None, :]
            mask = (j <= i) & (j > i - WINDOW)
            logits = jnp.einsum('bhqd,bhkd->bhqk', q, k) / np.sqrt(dh).astype(np.float32)
            logits = jnp.where(mask, logits, NEG)
            attn = jax.nn.softmax(logits, axis=-1)
            out = jnp.einsum('bhqk,bhkd->bhqd', attn, v)
            out = out.transpose(0, 2, 1, 3).reshape(B, S, D)
            return out @ wo.T

        def _mlp(w1, b1, w2, b2, x):
            return jax.nn.silu(x @ w1.T + b1) @ w2.T + b2
        key = jax.random.key(seed)
        ks = jax.random.split(key, 12)
        B, S = (2, 512)
        sc = 0.02
        n = lambda k, shape, s=sc: jax.random.normal(k, shape, jnp.float32) * s
        return {'x': n(ks[0], (B, S, DIM), 1.0), 'mem': n(ks[1], (NUM_PM, DIM), 1.0), 'wq': n(ks[2], (DIM, DIM)), 'wk': n(ks[3], (DIM, DIM)), 'wv': n(ks[4], (DIM, DIM)), 'wo': n(ks[5], (DIM, DIM)), 'w1': n(ks[6], (HID, DIM)), 'b1': jnp.zeros((HID,), jnp.float32), 'w2': n(ks[7], (DIM, HID)), 'b2': jnp.zeros((DIM,), jnp.float32), 'lin1': n(ks[8], (DIM, DIM)), 'lin2': n(ks[9], (DIM, DIM)), 'alpha': jnp.float32(0.0001), 'theta': jnp.float32(0.0001)}
    _L0_attn_in = _L0_attn_setup()

    def _L0_ffn_setup():
        import math
        import jax, jax.numpy as jnp
        import numpy as np
        B, L, D, FF, E, K = (4, 512, 256, 1024, 8, 2)
        CAPACITY_FACTOR = 1.25
        T = B * L
        CAP = math.ceil(CAPACITY_FACTOR * T * K / E)
        key = jax.random.key(seed)
        ks = jax.random.split(key, 7)
        return {'h': jax.random.normal(ks[0], (B, L, D), dtype=jnp.float32), 'gate_w': 0.02 * jax.random.normal(ks[1], (E, D), dtype=jnp.float32), 'gate_b': jnp.zeros((E,), dtype=jnp.float32), 'W1': 0.02 * jax.random.normal(ks[2], (E, D, FF), dtype=jnp.float32), 'b1': jnp.zeros((E, FF), dtype=jnp.float32), 'W2': 0.02 * jax.random.normal(ks[3], (E, FF, D), dtype=jnp.float32), 'b2': jnp.zeros((E, D), dtype=jnp.float32)}
    _L0_ffn_in = _L0_ffn_setup()
    _d = {'L0_attn_x': _L0_attn_in['x'], 'L0_attn_mem': _L0_attn_in['mem'], 'L0_attn_wq': _L0_attn_in['wq'], 'L0_attn_wk': _L0_attn_in['wk'], 'L0_attn_wv': _L0_attn_in['wv'], 'L0_attn_wo': _L0_attn_in['wo'], 'L0_attn_w1': _L0_attn_in['w1'], 'L0_attn_b1': _L0_attn_in['b1'], 'L0_attn_w2': _L0_attn_in['w2'], 'L0_attn_b2': _L0_attn_in['b2'], 'L0_attn_lin1': _L0_attn_in['lin1'], 'L0_attn_lin2': _L0_attn_in['lin2'], 'L0_attn_alpha': _L0_attn_in['alpha'], 'L0_attn_theta': _L0_attn_in['theta'], 'L0_ffn_gate_w': _L0_ffn_in['gate_w'], 'L0_ffn_gate_b': _L0_ffn_in['gate_b'], 'L0_ffn_W1': _L0_ffn_in['W1'], 'L0_ffn_b1': _L0_ffn_in['b1'], 'L0_ffn_W2': _L0_ffn_in['W2'], 'L0_ffn_b2': _L0_ffn_in['b2']}
    _x0 = _d['L0_attn_x']
    _d['L0_attn_x'] = jax.random.normal(jax.random.fold_in(jax.random.key(seed), 1), (8, 1024, 256), dtype=_x0.dtype)
    del _x0
    return _d

def reference(L0_attn_x, L0_attn_mem, L0_attn_wq, L0_attn_wk, L0_attn_wv, L0_attn_wo, L0_attn_w1, L0_attn_b1, L0_attn_w2, L0_attn_b2, L0_attn_lin1, L0_attn_lin2, L0_attn_alpha, L0_attn_theta, L0_ffn_gate_w, L0_ffn_gate_b, L0_ffn_W1, L0_ffn_b1, L0_ffn_W2, L0_ffn_b2):

    def _L0_attn_ref(x, mem, wq, wk, wv, wo, w1, b1, w2, b2, lin1, lin2, alpha, theta):
        import jax, jax.numpy as jnp
        import numpy as np
        DIM = 256
        HID = 1024
        NUM_HEADS = 4
        WINDOW = 128
        NUM_PM = 64
        NEG = -1e+30

        def _swa(x_in, wq, wk, wv, wo):
            B, S, D = x_in.shape
            h, dh = (NUM_HEADS, D // NUM_HEADS)
            q = (x_in @ wq.T).reshape(B, S, h, dh).transpose(0, 2, 1, 3)
            k = (x_in @ wk.T).reshape(B, S, h, dh).transpose(0, 2, 1, 3)
            v = (x_in @ wv.T).reshape(B, S, h, dh).transpose(0, 2, 1, 3)
            i = jnp.arange(S)[:, None]
            j = jnp.arange(S)[None, :]
            mask = (j <= i) & (j > i - WINDOW)
            logits = jnp.einsum('bhqd,bhkd->bhqk', q, k) / np.sqrt(dh).astype(np.float32)
            logits = jnp.where(mask, logits, NEG)
            attn = jax.nn.softmax(logits, axis=-1)
            out = jnp.einsum('bhqk,bhkd->bhqd', attn, v)
            out = out.transpose(0, 2, 1, 3).reshape(B, S, D)
            return out @ wo.T

        def _mlp(w1, b1, w2, b2, x):
            return jax.nn.silu(x @ w1.T + b1) @ w2.T + b2
        B, S, D = x.shape
        pm = jnp.broadcast_to(mem[None], (B, NUM_PM, D))
        x_in = jnp.concatenate([pm, x], axis=1)
        out_swa = _swa(x_in, wq, wk, wv, wo)
        k_flat = x_in.reshape(-1, D)
        v_flat = out_swa.reshape(-1, D)

        def loss_fn(params):
            pred = _mlp(*params, k_flat)
            return 0.5 * jnp.sum((pred - v_flat) ** 2)
        grads = jax.grad(loss_fn)((w1, b1, w2, b2))
        upd = jax.tree_util.tree_map(lambda p, g: (1.0 - alpha) * p - theta * g, (w1, b1, w2, b2), grads)
        out_mem = _mlp(*upd, k_flat).reshape(x_in.shape)
        g1 = jax.nn.sigmoid(out_swa @ lin1.T)
        g2 = jax.nn.sigmoid(out_mem @ lin2.T)
        out_merged = g1 * out_swa + g2 * out_mem
        return out_merged[:, NUM_PM:, :]

    def _L0_ffn_ref(h, gate_w, gate_b, W1, b1, W2, b2):
        import math
        import jax, jax.numpy as jnp
        import numpy as np
        B, L, D, FF, E, K = (4, 512, 256, 1024, 8, 2)
        CAPACITY_FACTOR = 1.25
        T = B * L
        CAP = math.ceil(CAPACITY_FACTOR * T * K / E)
        Bb, Ll, Dm = h.shape
        Tt = Bb * Ll
        x = h.reshape(Tt, Dm)
        logits = x @ gate_w.T + gate_b
        probs = jax.nn.softmax(logits, axis=-1)
        topk_prob, topk_idx = jax.lax.top_k(probs, K)
        y = jnp.zeros((Tt, Dm), dtype=h.dtype)
        n_slots = E * CAP
        for c in range(K):
            idx = topk_idx[:, c]
            prb = topk_prob[:, c]
            oh = jax.nn.one_hot(idx, E, dtype=jnp.int32)
            pos = jnp.take_along_axis(jnp.cumsum(oh, axis=0) - 1, idx[:, None], axis=1)[:, 0]
            keep = pos < CAP
            buf_idx = jnp.where(keep, idx * CAP + pos, n_slots)
            xbuf = jnp.zeros((n_slots, Dm), x.dtype).at[buf_idx].set(x, mode='drop')
            xb = xbuf.reshape(E, CAP, Dm)
            hmid = jax.nn.relu(jnp.einsum('ecd,edf->ecf', xb, W1) + b1[:, None, :])
            yb = jnp.einsum('ecf,efd->ecd', hmid, W2) + b2[:, None, :]
            ytok = yb.reshape(n_slots, Dm)[jnp.clip(buf_idx, 0, n_slots - 1)]
            y = y + ytok * (prb * keep.astype(prb.dtype))[:, None]
        return y.reshape(Bb, Ll, Dm)
    x = L0_attn_x
    x = x + _L0_attn_ref(_layernorm(x, axis=-1), L0_attn_mem, L0_attn_wq, L0_attn_wk, L0_attn_wv, L0_attn_wo, L0_attn_w1, L0_attn_b1, L0_attn_w2, L0_attn_b2, L0_attn_lin1, L0_attn_lin2, L0_attn_alpha, L0_attn_theta)
    x = x + _L0_ffn_ref(_layernorm(x, axis=-1), L0_ffn_gate_w, L0_ffn_gate_b, L0_ffn_W1, L0_ffn_b1, L0_ffn_W2, L0_ffn_b2)
    return x

_drawn_inputs = setup_inputs


def setup_inputs(seed=0):
    import zlib

    import numpy as np

    out = dict(_drawn_inputs(seed))
    spreads = {'L0_attn_b1': (0.0, 0.1),
     'L0_attn_b2': (0.0, 0.1),
     'L0_ffn_gate_b': (0.0, 0.1),
     'L0_ffn_b1': (0.0, 0.1),
     'L0_ffn_b2': (0.0, 0.1)}
    factors = {}
    for name, (base, spread) in spreads.items():
        noise = np.random.default_rng([zlib.crc32(name.encode()), seed]).standard_normal(out[name].shape)
        drawn = base * np.exp(spread * noise) if base else spread * noise
        out[name] = jnp.asarray(drawn.astype(out[name].dtype))
    for name, factor in factors.items():
        out[name] = (out[name] * factor).astype(out[name].dtype)
    return out
```

```python
import numpy as np
import concourse.bass as bass
from concourse import mybir
from concourse.alu_op_type import AluOpType as ALU
from contextlib import ExitStack

F32 = mybir.dt.float32
F32R = mybir.dt.float32r
I32 = mybir.dt.int32
ACTF = mybir.ActivationFunctionType
AX = mybir.AxisListType

P = 128
B, S, D = 8, 1024, 256
HID = 1024
HEADS, DH = 4, 64
NMEM = 64
NT = B * S
NBLK = NT // P
GRP = 4
NGRP = NBLK // GRP
NPAIR = NBLK // 2
KC = D // P
HC = HID // P
E, TOPK, CAP = 8, 2, 640
NSLOT = E * CAP
EPS = 1e-5


class Step:

    def __init__(self, queue, emit, after, sem=None, value=None):
        self.queue, self.emit, self.after = queue, emit, [s for s in after if s is not None]
        self.sem, self.value, self.awaited = sem, value, sem is not None


class Queue:

    def __init__(self, engine, done):
        self.engine, self.done, self.steps = engine, done, []

    def __call__(self, emit, after=()):
        step = Step(self, emit, after)
        for s in step.after:
            s.awaited = True
        self.steps.append(step)
        return step

    def number(self):
        for s in self.steps:
            if s.awaited and s.sem is None:
                self.done.count += 1
                s.sem, s.value = self.done, self.done.count

    def drain(self, handle):
        for s in self.steps:
            for w in s.after:
                if self.passed.get(w.sem.name, 0) < w.value:
                    handle.wait_ge(w.sem.sem, w.value)
                    self.passed[w.sem.name] = w.value
            last = s.emit(self.engine)
            if s.sem is not None:
                last.then_inc(s.sem.sem, 16 if s.sem.dma else 1)
        self.steps = []

    passed = None


class Sem:
    def __init__(self, sem, name, dma=False):
        self.sem, self.name, self.dma, self.count = sem, name, dma, 0


class Core:

    def __init__(self, nc, ctx):
        self.nc, self.ctx = nc, ctx
        self.sems = {}
        self.pe = Queue(nc.tensor, self.sem("pe_done"))
        self.act = Queue(nc.scalar, self.sem("act_done"))
        self.dve = Queue(nc.vector, self.sem("dve_done"))
        self.pool = Queue(nc.gpsimd, self.sem("pool_done"))
        self.sync = Queue(nc.sync, self.sem("sync_done"))
        for q in self.queues():
            q.passed = {}

    def queues(self):
        return [self.pe, self.act, self.dve, self.pool, self.sync]

    def sem(self, name, dma=False):
        if name not in self.sems:
            self.sems[name] = Sem(self.ctx.enter_context(self.nc.semaphore(name)), name, dma)
        return self.sems[name]

    def dma(self, queue, buffer, out, in_, after=()):
        sem = self.sem("dma_" + buffer, dma=True)
        sem.count += 16
        step = Step(queue, lambda e: e.dma_start(out, in_), after, sem, sem.count)
        for s in step.after:
            s.awaited = True
        queue.steps.append(step)
        return step

    def run(self):
        for q in self.queues():
            q.number()
        with self.nc.Block() as block:
            block.tensor(self.pe.drain)
            block.scalar(self.act.drain)
            block.vector(self.dve.drain)
            block.gpsimd(self.pool.drain)
            block.sync(self.sync.drain)


def matmul_split(out, lhs, rhs, first=True, last=True):
    terms = []
    for (ah, al), (bh, bl) in zip(lhs, rhs):
        terms += [(al, bh), (ah, bl), (ah, bh)]

    def emit(e):
        for n, (a, b) in enumerate(terms):
            i = e.matmul(out, a, b, start=first and n == 0, stop=last and n == len(terms) - 1)
        return i
    return emit


def copy(out, in_):
    return lambda e: e.tensor_copy(out, in_)


def act_copy(out, in_):
    return lambda e: e.activation(out, in_, ACTF.Copy)


def sub(out, a, b):
    return lambda e: e.tensor_tensor(out, a, b, ALU.subtract)


def add(out, a, b):
    return lambda e: e.tensor_tensor(out, a, b, ALU.add)


def attention_phase(c, io):
    nc = c.nc
    with ExitStack() as ctx:
        def sb(name, shape, dt=F32):
            return ctx.enter_context(nc.sbuf_tensor(name, shape, dt))

        def ps(name, shape, dt=F32):
            return ctx.enter_context(nc.psum_tensor(name, shape, dt))

        w = {}
        ws = []
        full_w = sb("a_wfull", [P, 4, KC, D])
        for n, k in enumerate(("wq", "wk", "wv", "wo")):
            hi, lo = sb(k + "_h", [P, KC, D], F32R), sb(k + "_l", [P, KC, D], F32R)
            ld = c.dma(c.sync, k, full_w[:, n], io[k + "T"].rearrange("(c p) n -> p c n", p=P))
            h = c.dve(copy(hi[:], full_w[:, n]), [ld])
            ws.append(c.dve(sub(lo[:], full_w[:, n], hi[:]), [h]))
            w[k] = (hi, lo)
        ident, masks = sb("a_ident", [P, P]), sb("a_masks", [P, 3, 2 * P])
        ld_ident = c.dma(c.sync, "a_ident", ident[:], io["ident"])
        ld_masks = c.dma(c.sync, "a_masks", masks[:], io["masks"].rearrange("m p k -> p m k"))
        neg_half = sb("neg_half", [P, GRP])
        set_half = c.pool(lambda e: e.memset(neg_half[:], -0.5))

        x_g = [sb(f"x_g{i}", [P, GRP, D]) for i in range(3)]
        xn = [sb(f"xn{i}", [P, GRP, D]) for i in range(2)]
        stats = [sb(f"ln_stats{i}", [P, GRP, 6]) for i in range(2)]
        mv = [sb(f"ln_mv{i}", [P, GRP, 2]) for i in range(2)]
        rstd = [sb(f"ln_rstd{i}", [P, 2, GRP]) for i in range(2)]
        xT = [sb(f"xT{i}", [P, KC, GRP * P]) for i in range(2)]
        xTh = [sb(f"xTh{i}", [P, KC, GRP * P], F32R) for i in range(2)]
        xTl = [sb(f"xTl{i}", [P, KC, GRP * P], F32R) for i in range(2)]
        qh = [sb(f"qh{i}", [P, KC, GRP * P if i < 3 else P], F32R) for i in range(4)]
        ql = [sb(f"ql{i}", [P, KC, GRP * P if i < 3 else P], F32R) for i in range(4)]
        kh = [sb(f"kh{i}", [P, KC, 9 * P], F32R) for i in range(2)]
        kl = [sb(f"kl{i}", [P, KC, 9 * P], F32R) for i in range(2)]
        vh = [sb(f"vh{i}", [P, 9, D], F32R) for i in range(2)]
        vl = [sb(f"vl{i}", [P, 9, D], F32R) for i in range(2)]
        pr = [sb(f"prob{i}", [P, HEADS, 2 * P]) for i in range(2)]
        small = [sb(f"softmax_small{i}", [P, 4, HEADS]) for i in range(2)]
        pth = [sb(f"probT_h{i}", [P, 2, HEADS, P], F32R) for i in range(2)]
        ptl = [sb(f"probT_l{i}", [P, 2, HEADS, P], F32R) for i in range(2)]
        ah = sb("attnT_h", [P, KC, GRP * P], F32R)
        al = sb("attnT_l", [P, KC, GRP * P], F32R)
        oT = sb("outT", [P, KC, GRP * P])

        ps_s = ps("ps_scores", [P, 2, 2, 2 * P])
        ps_pt = ps("ps_probT", [P, 2, HEADS, P])
        ps_av = ps("ps_av", [P, KC, 2 * P])
        ps_j = ps("ps_proj", [P, GRP * P])
        ps_x = ps("ps_xT", [P, KC, 2 * P])
        ps_v = ps("ps_v", [P, 2, D])

        x_v = io["x"].rearrange("(g j p) d -> g p j d", j=GRP, p=P)
        last = {}
        xn_ready, xT_stored, qk_ready, v_ready = {}, {}, {}, {}
        xT_pair = {}

        def order(G):
            return -1 if G == NGRP else G

        def blocks(G):
            return GRP if G < NGRP else 1

        def load_x(G):
            if G < NGRP:
                last["x", G] = c.dma(c.sync, f"x{G % 3}", x_g[G % 3][:], x_v[G], [last.get(("ln", G - 3))])

        def store_pairs(name, G, tile_of, dram, steps):
            for h in range((blocks(G) + 1) // 2):
                pair, n = 2 * G + h, min(2, blocks(G))
                out, in_ = tile_of(h, n, dram[pair])
                last[name, order(G)] = c.dma(c.sync, f"{name}{order(G) % 2}", out, in_, steps[h])

        def norm(G):
            o = order(G)
            s, t = o % 2, xn[o % 2]
            free = [last.get(("xn_st", o - 2)), last.get(("tx_pe", o - 2))]
            if G == NGRP:
                done = c.dma(c.sync, "mem", t[:, 0, :], io["memp"], free)
                xn_ready[G] = [done]
            else:
                ld, src = last["x", G], x_g[G % 3]
                for j in range(GRP):
                    st = c.dve(lambda e, j=j: e.bn_stats(stats[s][:, j], src[:, j]), [ld, last.get(("ln_ag", o - 2))])
                for j in range(GRP):
                    ag = c.dve(lambda e, j=j: e.bn_aggr(mv[s][:, j], stats[s][:, j]), [st, last.get(("ln", o - 2))])
                last["ln_ag", o] = ag
                ve = c.dve(lambda e: e.tensor_scalar(rstd[s][:, 0], mv[s][:, :, 1], EPS, None, ALU.add), [ag, last.get(("ln_r", o - 2))])
                r = c.pool(lambda e: e.tensor_tensor(rstd[s][:, 1], rstd[s][:, 0], neg_half[:], ALU.pow), [ve, set_half, last.get(("ln", o - 2))])
                last["ln_r", o] = r
                for j in range(GRP):
                    a = c.dve(lambda e, j=j: e.tensor_scalar(t[:, j], src[:, j], mv[s][:, j, 0:1], rstd[s][:, 1, j:j + 1],
                                                              ALU.subtract, ALU.mult), [r] + free)
                last["ln", G] = a
                xn_ready[G] = [a]
            store_pairs("xn_st", G, lambda h, n, d: (d[:, 0:n, :], t[:, 2 * h:2 * h + n, :]), io["xn_d"], [xn_ready[G]] * 2)

        def transpose_x(G, h):
            o = order(G)
            s, n = o % 2, min(2, blocks(G))
            cols = slice(2 * h * P, (2 * h + n) * P)

            def emit(e):
                for k in range(KC):
                    for j in range(n):
                        i = e.transpose(ps_x[:, k, j * P:(j + 1) * P], xn[s][:, 2 * h + j, k * P:(k + 1) * P], ident[:])
                return i
            t = c.pe(emit, xn_ready[G] + [ld_ident, last.get("ps_x")])
            last["tx_pe", o] = t
            f = c.act(act_copy(xT[s][:, :, cols], ps_x[:, :, 0:n * P]), [t, last.get(("xT_st", o - 2)), last.get(("xTl", o - 2))])
            last["ps_x"] = f
            hi = c.dve(copy(xTh[s][:, :, cols], xT[s][:, :, cols]), [f, last.get(("xT_use", o - 2))])
            lo = c.pool(sub(xTl[s][:, :, cols], xT[s][:, :, cols], xTh[s][:, :, cols]), [hi, last.get(("xT_use", o - 2))])
            last["xTl", o] = lo
            xT_pair[G, h] = lo
            d = io["xT_d"][2 * G + h]
            last["xT_st", o] = c.dma(c.sync, f"xT_st{s}", d[:, :, 0:n * P], xT[s][:, :, cols], [f])

        def q_slot(G, low):
            return (ql if low else qh)[3 if G == NGRP else G % 3]

        def project_qk(G, t):
            s, n, m = order(G) % 2, blocks(G) * P, t % 2
            wh, wl = w["wq" if t < 2 else "wk"]
            lhs = [(wh[:, k, m * P:(m + 1) * P], wl[:, k, m * P:(m + 1) * P]) for k in range(KC)]
            rhs = [(xTh[s][:, k, 0:n], xTl[s][:, k, 0:n]) for k in range(KC)]
            mm = c.pe(matmul_split(ps_j[:, 0:n], lhs, rhs), [xT_pair[G, 0], xT_pair.get((G, 1)), last.get("ps_j"), ws[0], ws[1]])
            last["xT_use", order(G)] = mm
            if t < 2:
                free = [last.get(("score", g)) for g in range(GRP * (G - 3), GRP * (G - 3) + GRP)] if 3 <= G < NGRP else []
                dst = [(q_slot(G, 0)[:, m, 0:n], q_slot(G, 1)[:, m, 0:n])]
            elif G < NGRP:
                b = G // 2
                free = [last.get(("score", 8 * (b - 2) + 7))] if b >= 2 else []
                cols = slice(P + (G % 2) * GRP * P, P + (G % 2 + 1) * GRP * P)
                dst = [(kh[b % 2][:, m, cols], kl[b % 2][:, m, cols])]
            else:
                free, dst = [], [(kh[b][:, m, 0:P], kl[b][:, m, 0:P]) for b in range(2)]
            for hi_t, _ in dst:
                hi = c.act(act_copy(hi_t, ps_j[:, 0:n]), [mm] + free)
            for hi_t, lo_t in dst:
                lo = c.dve(sub(lo_t, ps_j[:, 0:n], hi_t), [hi] + free)
                qk_ready[G, t] = qk_ready.get((G, t), []) + [lo]
                last["ps_j"] = lo

        def project_v(G, h):
            s, n = order(G) % 2, min(2, blocks(G))
            wh, wl = w["wv"]

            def emit(e):
                for j in range(n):
                    cols = slice((2 * h + j) * P, (2 * h + j + 1) * P)
                    i = matmul_split(ps_v[:, j], [(xTh[s][:, k, cols], xTl[s][:, k, cols]) for k in range(KC)],
                                     [(wh[:, k], wl[:, k]) for k in range(KC)])(e)
                return i
            mm = c.pe(emit, [xT_pair[G, h], last.get("ps_v"), ws[2]])
            last["xT_use", order(G)] = mm
            if G < NGRP:
                b = G // 2
                free = [last.get(("av", 8 * (b - 2) + 7))] if b >= 2 else []
                at = 1 + (G % 2) * GRP + 2 * h
                dst = [(vh[b % 2][:, at:at + 2], vl[b % 2][:, at:at + 2])]
            else:
                free, dst = [], [(vh[b][:, 0:1], vl[b][:, 0:1]) for b in range(2)]
            for hi_t, _ in dst:
                hi = c.act(act_copy(hi_t, ps_v[:, 0:n]), [mm] + free)
            for hi_t, lo_t in dst:
                lo = c.dve(sub(lo_t, ps_v[:, 0:n], hi_t), [hi] + free)
                v_ready[G, h] = v_ready.get((G, h), []) + [lo]
                last["ps_v"] = lo

        def place(g):
            if g == NBLK:
                return (B - 1) % 2, 0, 2
            return (g // 8) % 2, g % 8, 1 if g % 8 == 0 else 0

        def scores(g):
            G, (par, i, mask) = g // GRP, place(g)
            qc, kcols = slice((g % GRP) * P, (g % GRP + 1) * P), slice(i * P, (i + 2) * P)

            def emit(e):
                for c2 in range(2):
                    for n in range(3):
                        for half in range(2):
                            r = slice(half * DH, (half + 1) * DH)
                            a = q_slot(G, n == 0)[r, c2, qc]
                            b = (kl if n == 1 else kh)[par][r, c2, kcols]
                            x = e.matmul(ps_s[:, half, c2], a, b, start=n == 0, stop=n == 2)
                return x
            need = [s for t in range(4) for s in qk_ready[G, t]]
            need += [s for t in (2, 3) for s in qk_ready[NGRP, t]]
            if g % GRP == 0 and g % 8 and g < NBLK:
                need += [s for t in (2, 3) for s in qk_ready[G - 1, t]]
            sc = c.pe(emit, need + [last.get("ps_s")])
            last["score", g] = sc
            p, sm = pr[g % 2], small[g % 2]
            for h in range(HEADS):
                mx = c.dve(lambda e, h=h: e.tensor_tensor_reduce(
                    out=p[:, h], in0=ps_s[:, h % 2, h // 2], in1=masks[:, mask], scale=1.0, scalar=-3.0e38,
                    op0=ALU.add, op1=ALU.max, accum_out=sm[:, 0, h:h + 1]),
                    [sc, ld_masks, last.get(("pt_pe", g - 2)), last.get(("exp", g - 2))])
            last["ps_s"] = mx
            last["max", g] = mx

        def soft(g):
            p, sm = pr[g % 2], small[g % 2]
            nm = c.pool(lambda e: e.tensor_scalar(sm[:, 1], sm[:, 0], -1.0 / DH ** 0.5, None, ALU.mult), [last["max", g], last.get(("exp", g - 2))])
            for h in range(HEADS):
                ex = c.act(lambda e, h=h: e.activation(p[:, h], p[:, h], ACTF.Exp, bias=sm[:, 1, h:h + 1],
                                                       scale=1.0 / DH ** 0.5, accum_out=sm[:, 2, h:h + 1]),
                           [nm, last.get(("prob", g - 2))])
            last["exp", g] = ex

        def normalise(g):
            p, sm = pr[g % 2], small[g % 2]
            rc = c.dve(lambda e: e.reciprocal(sm[:, 3], sm[:, 2]), [last["exp", g], last.get(("prob", g - 2))])
            for h in range(HEADS):
                pn = c.dve(lambda e, h=h: e.tensor_scalar(p[:, h], p[:, h], sm[:, 3, h:h + 1], None, ALU.mult), [rc])
            last["prob", g] = pn

        def transpose_p(g):
            p = pr[g % 2]

            def emit(e):
                for kb in range(2):
                    for h in range(HEADS):
                        x = e.transpose(ps_pt[:, kb, h], p[:, h, kb * P:(kb + 1) * P], ident[:])
                return x
            t = c.pe(emit, [last["prob", g], last.get("ps_pt")])
            last["pt_pe", g] = t
            hi = c.act(act_copy(pth[g % 2][:], ps_pt[:]), [t, last.get(("av", g - 2))])
            lo = c.dve(sub(ptl[g % 2][:], ps_pt[:], pth[g % 2][:]), [hi, last.get(("av", g - 2))])
            last["ps_pt"] = last["pt", g] = lo

        def attend(g):
            par, i, _ = place(g)
            G = g // GRP
            cols = slice((g % GRP) * P, (g % GRP + 1) * P)

            def emit(e):
                for c2 in range(KC):
                    vc = slice(c2 * P, (c2 + 1) * P)
                    x = matmul_split(ps_av[:, c2], [(vh[par][:, i + kb, vc], vl[par][:, i + kb, vc]) for kb in range(2)],
                                     [(pth[g % 2][:, kb, 2 * c2:2 * c2 + 2], ptl[g % 2][:, kb, 2 * c2:2 * c2 + 2])
                                      for kb in range(2)])(e)
                return x
            Gb = min(G, NGRP - 1)
            need = [last["pt", g], last.get("ps_av")] + [s for k in v_ready if k[0] in (G, G - 1, NGRP) for s in v_ready[k]]
            av = c.pe(emit, need)
            last["av", g] = av
            for half in range(2):
                r, src = slice(half * DH, (half + 1) * DH), slice(half * P, (half + 1) * P)
                hi = c.act(act_copy(ah[r, :, cols], ps_av[r, :, src]), [av, last.get(("wo", G - 1))])
            for half in range(2):
                r, src = slice(half * DH, (half + 1) * DH), slice(half * P, (half + 1) * P)
                lo = c.dve(sub(al[r, :, cols], ps_av[r, :, src], ah[r, :, cols]), [hi, last.get(("wo", G - 1))])
            last["ps_av"] = last["attn", g] = lo

        def out_project(G):
            n, m_done = blocks(G) * P, []
            wh, wl = w["wo"]
            for m in range(KC):
                mc = slice(m * P, (m + 1) * P)
                mm = c.pe(matmul_split(ps_j[:, 0:n], [(wh[:, k, mc], wl[:, k, mc]) for k in range(KC)],
                                       [(ah[:, k, 0:n], al[:, k, 0:n]) for k in range(KC)]),
                          [last["attn", 4 * G + blocks(G) - 1], last.get("ps_j"), ws[3]])
                ev = c.act(act_copy(oT[:, m, 0:n], ps_j[:, 0:n]), [mm, last.get(("oT_st", G - 1))])
                last["ps_j"] = ev
                m_done.append(ev)
            last["wo", G] = mm
            for h in range((blocks(G) + 1) // 2):
                k = min(2, blocks(G))
                last["oT_st", G] = c.dma(c.sync, "oT_st", io["oT_d"][2 * G + h][:, :, 0:k * P],
                                         oT[:, :, 2 * h * P:(2 * h + k) * P], m_done)

        def prep(G, j):
            if j == 0:
                load_x(G + 1)
                transpose_x(G, 0)
            elif j == 1:
                if G + 1 < NGRP:
                    norm(G + 1)
                if G < NGRP:
                    transpose_x(G, 1)
            elif j == 2:
                project_v(G, 0)
                project_qk(G, 0)
                project_qk(G, 2)
            else:
                if G < NGRP:
                    project_v(G, 1)
                project_qk(G, 1)
                project_qk(G, 3)

        norm(NGRP)
        load_x(0)
        for j in range(4):
            if j == 1:
                norm(0)
                continue
            prep(NGRP, j)
        for G in range(2):
            for j in range(4):
                prep(G, j)
        for a in range(NBLK + 4):
            if a <= NBLK:
                scores(a)
            if a // GRP + 2 < NGRP:
                prep(a // GRP + 2, a % GRP)
            if a <= NBLK:
                soft(a)
            if 1 <= a <= NBLK + 1:
                transpose_p(a - 1)
            if a <= NBLK:
                normalise(a)
            if a >= 3 and ((a - 3) % GRP == GRP - 1 or a - 3 == NBLK):
                out_project((a - 3) // GRP)
            if 2 <= a <= NBLK + 2:
                attend(a - 2)
        stores = [last["xn_st", G] for G in (NGRP - 1, NGRP - 2)]
        stores += [last["xT_st", G] for G in (NGRP - 1, NGRP - 2)] + [last["oT_st", NGRP]]
        c.sync(lambda e: e.nop(), stores)
        c.run()


def gradient_phase(c, io, g1, g2, b1n, b2n):
    nc = c.nc
    with ExitStack() as ctx:
        def sb(name, shape, dt=F32):
            return ctx.enter_context(nc.sbuf_tensor(name, shape, dt))

        def ps(name, shape, dt=F32):
            return ctx.enter_context(nc.psum_tensor(name, shape, dt))

        hf = [sb(f"h_full{i}", [P, HID]) for i in range(2)]
        qf = sb("silu_q", [P, HID])
        sp = [sb(f"silu_slope{i}", [P, HID]) for i in range(4)]
        w1h, w1l = sb("w1_h", [P, KC, HID], F32R), sb("w1_l", [P, KC, HID], F32R)
        w2Th, w2Tl = sb("w2T_h", [P, HC, D], F32R), sb("w2T_l", [P, HC, D], F32R)
        w2h, w2l = sb("w2_h", [P, KC, HID], F32R), sb("w2_l", [P, KC, HID], F32R)
        w_ready = {}
        w1_v = io["w1T"].rearrange("(c p) n -> p c n", p=P)
        w2T_v = io["w2T"].rearrange("(c p) n -> p c n", p=P)
        w2_v = io["w2"].rearrange("(c p) n -> p c n", p=P)
        stages = [(w1h[:, k], w1l[:, k], w1_v[:, k], "w1") for k in range(KC)]
        stages += [(w2Th[:, 4 * k:4 * k + 4], w2Tl[:, 4 * k:4 * k + 4], w2T_v[:, 4 * k:4 * k + 4], "w2T") for k in range(2)]
        stages += [(w2h[:, k], w2l[:, k], w2_v[:, k], "w2") for k in range(KC)]
        last = {}
        for n, (hi, lo, src, key) in enumerate(stages):
            full = sp[n % 4][:] if key != "w2T" else sp[n % 4][:].rearrange("p (a b) -> p a b", b=D)
            ld = c.dma(c.sync, f"g_w{n}", full, src, [last.get(("stage", n - 4))])
            h = c.act(act_copy(hi, full), [ld])
            last["stage", n] = w_ready[key] = c.dve(sub(lo, full, hi), [h])

        ident = sb("g_ident", [P, P])
        ld_ident = c.dma(c.sync, "g_ident", ident[:], io["ident"])
        row_scale = sb("mem_row_scale", [P, P])
        ld_scale = c.dma(c.sync, "g_scale", row_scale[:], io["mem_scale"])
        b2c = sb("b2_col", [P, KC])
        ld_b2 = c.dma(c.sync, "g_b2", b2c[:], io["b2c"])
        b1f, b1s, ones2f = qf[0:2, :], sb("b1_rows", [2, HID], F32R), sb("ones2_f", [2, P])
        b1h, b1l = hf[0][0:2, :], hf[1][0:2, :]
        ones2 = sb("ones2", [2, P], F32R)
        b1t = sb("b1_high", [2, HID], F32R)
        ld_b1 = [c.dma(c.sync, "g_b1", qf[r:r + 1, :], io["b1"].rearrange("(a n) -> a n", a=1)) for r in range(2)]
        hi = c.dve(copy(b1t[:], b1f), [ld_b1[1]])
        hs = c.dve(lambda e: e.tensor_scalar(b1h, b1t[:], ident[0:2, 0:1], None, ALU.mult), [hi, ld_ident])
        lo = c.dve(sub(b1l, b1f, b1t[:]), [hi])
        b1_ready = c.dve(lambda e: e.scalar_tensor_tensor(b1s[:], b1l, ident[0:2, 1:2], b1h, ALU.mult, ALU.add), [hs, lo])
        set1 = c.dve(lambda e: e.memset(ones2f[:], 1.0))
        ones_ready = c.dve(copy(ones2[:], ones2f[:]), [set1])

        dz_sum = sb("dz_sum", [P, HID])
        db2 = sb("db2_parts", [P, KC, NPAIR + 1])
        zero = [c.pool(lambda e, t=t: e.memset(t, 0.0)) for t in (g1[:], g2[:], dz_sum[:])]

        xn_f = [sb(f"xn_f{i}", [P, 2, D]) for i in range(2)]
        xT_f = [sb(f"xT_f{i}", [P, KC, 2 * P]) for i in range(2)]
        oT_f = [sb(f"oT_f{i}", [P, KC, 2 * P]) for i in range(2)]
        xnh = [sb(f"xn_h{i}", [P, 2, D], F32R) for i in range(2)]
        xnl = [sb(f"xn_l{i}", [P, 2, D], F32R) for i in range(2)]
        xTh = [sb(f"g_xTh{i}", [P, KC, 2 * P], F32R) for i in range(1)]
        xTl = [sb(f"g_xTl{i}", [P, KC, 2 * P], F32R) for i in range(1)]
        hh = [sb(f"h_h{i}", [P, HID], F32R) for i in range(4)]
        hl = [sb(f"h_l{i}", [P, HID], F32R) for i in range(4)]
        hTh, hTl = sb("hT_h", [P, HC, 2 * P], F32R), sb("hT_l", [P, HC, 2 * P], F32R)
        dzh = [sb(f"dz_h{i}", [P, HID], F32R) for i in range(2)]
        dzl = [sb(f"dz_l{i}", [P, HID], F32R) for i in range(2)]
        dpf = sb("dpredT", [P, KC, 2 * P])
        dTh, dTl = sb("dpredT_h", [P, KC, 2 * P], F32R), sb("dpredT_l", [P, KC, 2 * P], F32R)
        dth, dtl = sb("dpred_h", [P, 2, D], F32R), sb("dpred_l", [P, 2, D], F32R)

        ps_z = ps("ps_z", [P, HID])
        ps_d = ps("ps_dh", [P, HID])
        ps_t = ps("ps_hT", [P, HC, P])
        ps_g = [ps(f"ps_g{i}", [P, 512]) for i in range(2)]
        turn = [0]

        def n_of(p):
            return 2 if p < NPAIR else 1

        def load(p):
            n, s = n_of(p), p % 2
            last["ld", p] = [
                c.dma(c.sync, f"g_xn{s}", xn_f[s][:, 0:n], io["xn_d"][p][:, 0:n], [last.get(("xnl", p - 2))]),
                c.dma(c.sync, f"g_xT{s}", xT_f[s][:, :, 0:n * P], io["xT_d"][p][:, :, 0:n * P], [last.get(("xTl", p - 2))]),
                c.dma(c.sync, f"g_oT{s}", oT_f[s][:, :, 0:n * P], io["oT_d"][p][:, :, 0:n * P], [last.get(("dp", p - 2))])]

        def split_inputs(p):
            n, s = n_of(p), p % 2
            ld = last["ld", p]
            h = c.act(act_copy(xTh[0][:, :, 0:n * P], xT_f[s][:, :, 0:n * P]), [ld[1], last.get(("z", p - 1))])
            last["xTl", p] = c.dve(sub(xTl[0][:, :, 0:n * P], xT_f[s][:, :, 0:n * P], xTh[0][:, :, 0:n * P]), [h, last.get(("z", p - 1))])
            h = c.act(act_copy(xnh[s][:, 0:n], xn_f[s][:, 0:n]), [ld[0], last.get(("gw1", p - 2))])
            last["xnl", p] = c.dve(sub(xnl[s][:, 0:n], xn_f[s][:, 0:n], xnh[s][:, 0:n]), [h, last.get(("gw1", p - 2))])

        def forward(p, b):
            g = 2 * p + b
            cols = slice(b * P, (b + 1) * P)

            def emit(e):
                for half in range(2):
                    hc = slice(half * 512, (half + 1) * 512)
                    e.matmul(ps_z[:, hc], ones2[:], b1s[:, hc], start=True, stop=False)
                    i = matmul_split(ps_z[:, hc], [(xTh[0][:, k, cols], xTl[0][:, k, cols]) for k in range(KC)],
                                     [(w1h[:, k, hc], w1l[:, k, hc]) for k in range(KC)], first=False)(e)
                return i
            z = c.pe(emit, [last["xTl", p], w_ready["w1"], b1_ready, ones_ready, last.get("ps_z")])
            last["z", p] = z
            t = sp[g % 4]
            s = c.act(lambda e: e.activation(t[:], ps_z[:], ACTF.Sigmoid), [z, last.get(("dzs", g - 4)), w_ready["w2"]])
            hfull = hf[g % 2]
            free = [last.get(("hT_pe", g - 2)), last.get(("hl", g - 2)), last.get(("q", g - 2)), b1_ready]
            h = c.dve(lambda e: e.tensor_tensor(hfull[:], ps_z[:], t[:], ALU.mult), [s] + free)
            last["ps_z"] = last["h", g] = h
            q = c.dve(lambda e: e.scalar_tensor_tensor(qf[:], t[:], 1.0, hfull[:], ALU.subtract, ALU.mult), [h, last.get(("sp", g - 1))])
            last["q", g] = q
            last["sp", g] = c.pool(sub(t[:], t[:], qf[:]), [q])
            hi = c.act(act_copy(hh[g % 4][:], hfull[:]), [h, last.get(("gw2", p - 2))])
            last["hl", g] = c.pool(sub(hl[g % 4][:], hfull[:], hh[g % 4][:]), [hi, last.get(("gw2", p - 2))])

        def transpose_h(p, b):
            g = 2 * p + b

            def emit(e):
                for k in range(HC):
                    i = e.transpose(ps_t[:, k], hf[g % 2][:, k * P:(k + 1) * P], ident[:])
                return i
            t = c.pe(emit, [last["h", g], ld_ident, last.get("ps_t")])
            last["hT_pe", g] = t
            cols = slice(b * P, (b + 1) * P)
            hi = c.act(act_copy(hTh[:, :, cols], ps_t[:]), [t, last.get(("pred", p - 1))])
            lo = c.dve(sub(hTl[:, :, cols], ps_t[:], hTh[:, :, cols]), [hi, last.get(("pred", p - 1))])
            last["ps_t"] = last["hT", g] = lo

        def bank():
            turn[0] += 1
            return ps_g[turn[0] % 2], ("bank", turn[0] % 2)

        def predict(p):
            n, s = n_of(p), p % 2
            N = n * P
            acc, key = bank()

            def emit(e):
                for m in range(KC):
                    mc = slice(m * P, (m + 1) * P)
                    i = matmul_split(acc[:, m * 2 * P:m * 2 * P + N], [(w2Th[:, k, mc], w2Tl[:, k, mc]) for k in range(HC)],
                                     [(hTh[:, k, 0:N], hTl[:, k, 0:N]) for k in range(HC)])(e)
                return i
            mm = c.pe(emit, [last["hT", 2 * p + n - 1], w_ready["w2T"], last.get(key)])
            last["pred", p] = mm
            free = [last.get(("dT_pe", p - 1)), last.get(("dTl", p - 1))]
            for m in range(KC):
                d = c.dve(lambda e, m=m: e.scalar_tensor_tensor(
                    dpf[:, m, 0:N], acc[:, m * 2 * P:m * 2 * P + N], b2c[:, m:m + 1], oT_f[s][:, m, 0:N],
                    ALU.add, ALU.subtract, accum_out=db2[:, m, p:p + 1]), [mm, ld_b2, last["ld", p][2]] + free)
            last[key] = last["dp", p] = d
            if p == NPAIR:
                for m in range(KC):
                    d = c.dve(lambda e, m=m: e.tensor_tensor(dpf[:, m, 0:N], dpf[:, m, 0:N], row_scale[:], ALU.mult), [d, ld_scale])
                for m in range(KC):
                    d2 = c.dve(lambda e, m=m: e.tensor_reduce(db2[:, m, p:p + 1], dpf[:, m, 0:N], AX.X, ALU.add), [d])
                last["db2"] = d2
            hi = c.act(act_copy(dTh[:, :, 0:N], dpf[:, :, 0:N]), [d, last.get(("dh", p - 1))])
            last["dTl", p] = c.dve(sub(dTl[:, :, 0:N], dpf[:, :, 0:N], dTh[:, :, 0:N]), [hi, last.get(("dh", p - 1))])
            last["dpf", p] = d

        def transpose_d(p):
            n = n_of(p)
            acc, key = bank()

            def emit(e):
                for b in range(n):
                    for m in range(KC):
                        i = e.transpose(acc[:, (2 * b + m) * P:(2 * b + m + 1) * P], dpf[:, m, b * P:(b + 1) * P], ident[:])
                return i
            t = c.pe(emit, [last["dpf", p], last.get(key)])
            last["dT_pe", p] = t
            src = acc[:, 0:n * D].rearrange("p (b d) -> p b d", b=n)
            hi = c.act(act_copy(dth[:, 0:n], src), [t, last.get(("gw2", p - 1))])
            lo = c.dve(sub(dtl[:, 0:n], src, dth[:, 0:n]), [hi, last.get(("gw2", p - 1))])
            last[key] = last["dtok", p] = lo

        def backward(p, b):
            g = 2 * p + b
            cols = slice(b * P, (b + 1) * P)

            def emit(e):
                for half in range(2):
                    hc = slice(half * 512, (half + 1) * 512)
                    i = matmul_split(ps_d[:, hc], [(dTh[:, k, cols], dTl[:, k, cols]) for k in range(KC)],
                                     [(w2h[:, k, hc], w2l[:, k, hc]) for k in range(KC)])(e)
                return i
            mm = c.pe(emit, [last["dTl", p], w_ready["w2"], last.get("ps_d")])
            last["dh", p] = mm
            t = sp[g % 4]
            dz = c.dve(lambda e: e.tensor_tensor(t[:], ps_d[:], t[:], ALU.mult), [mm, last["sp", g]])
            last["ps_d"] = dz
            hi = c.act(act_copy(dzh[b][:], t[:]), [dz, last.get(("gw1", p - 1))])
            last["dz", g] = c.pool(sub(dzl[b][:], t[:], dzh[b][:]), [hi, last.get(("gw1", p - 1))])
            last["dzs", g] = c.pool(add(dz_sum[:], dz_sum[:], t[:]), [dz, last.get(("dzs", g - 1)), zero[2]])

        def accumulate_w2(p):
            n = n_of(p)
            for t in range(HC // 2):
                acc, key = bank()

                def emit(e, t=t, acc=acc):
                    for u in range(2):
                        hc = slice((2 * t + u) * P, (2 * t + u + 1) * P)
                        i = matmul_split(acc[:, u * D:(u + 1) * D], [(hh[(2 * p + b) % 4][:, hc], hl[(2 * p + b) % 4][:, hc]) for b in range(n)],
                                         [(dth[:, b], dtl[:, b]) for b in range(n)])(e)
                    return i
                mm = c.pe(emit, [last["dtok", p], last["hl", 2 * p + n - 1], last.get(key)])
                dst = g2[:, 2 * t:2 * t + 2].rearrange("p a b -> p (a b)")
                last[key] = last["g2", t] = c.dve(add(dst, acc[:], dst), [mm, zero[1], last.get(("g2", t))])
            last["gw2", p] = mm

        def accumulate_w1(p):
            n, s = n_of(p), p % 2
            for t in range(2 * KC):
                k, hc = t // 2, slice((t % 2) * 512, (t % 2 + 1) * 512)
                acc, key = bank()
                mm = c.pe(matmul_split(acc[:], [(xnh[s][:, b, k * P:(k + 1) * P], xnl[s][:, b, k * P:(k + 1) * P]) for b in range(n)],
                                       [(dzh[b][:, hc], dzl[b][:, hc]) for b in range(n)]),
                          [last["dz", 2 * p + n - 1], last["xnl", p], last.get(key)])
                last[key] = last["g1", t] = c.dve(add(g1[:, k, hc], acc[:], g1[:, k, hc]), [mm, zero[0], last.get(("g1", t))])
            last["gw1", p] = mm

        NP_ = NPAIR + 1
        load(0)
        load(1)
        for p in range(NP_ + 1):
            now, before = p < NP_, p >= 1
            if now:
                split_inputs(p)
                forward(p, 0)
            if before:
                backward(p - 1, 0)
            if now and n_of(p) == 2:
                forward(p, 1)
            if now:
                transpose_h(p, 0)
            if before and n_of(p - 1) == 2:
                backward(p - 1, 1)
            if before:
                accumulate_w2(p - 1)
            if now and n_of(p) == 2:
                transpose_h(p, 1)
            if now:
                predict(p)
            if before:
                accumulate_w1(p - 1)
            if now:
                transpose_d(p)
            if p + 2 < NP_:
                load(p + 2)

        rates = sb("g_rates_sb", [P, 4])
        ld_r = c.dma(c.sync, "g_rates", rates[:, 0:2], io["rates"])
        keep = c.dve(lambda e: e.tensor_scalar(rates[:, 2:3], rates[:, 0:1], -1.0, 1.0, ALU.mult, ALU.add), [ld_r])
        step = c.dve(lambda e: e.tensor_scalar(rates[:, 3:4], rates[:, 1:2], -1.0, None, ALU.mult), [ld_r])
        ones = c.dve(lambda e: e.memset(rates[:, 0:1], 1.0), [keep])
        bank1, key = bank()

        def emit(e):
            for k in range(HC):
                i = e.matmul(bank1[:, k:k + 1], dz_sum[:, k * P:(k + 1) * P], rates[:, 0:1], start=True, stop=True)
            return i
        mm = c.pe(emit, [last["dzs", 2 * NPAIR], last.get(key), ones])
        b1c = sb("b1_col", [P, HC])
        ld = c.dma(c.sync, "g_b1c", b1c[:], io["b1c"])
        a = c.dve(lambda e: e.tensor_scalar(b1c[:], b1c[:], rates[:, 2:3], None, ALU.mult), [ld, keep])
        c.dve(lambda e: e.scalar_tensor_tensor(b1n[:], bank1[:, 0:HC], rates[:, 3:4], b1c[:], ALU.mult, ALU.add), [mm, step, a])
        red = c.dve(lambda e: e.tensor_reduce(b2n[:], db2[:], AX.X, ALU.add), [last["db2"]])
        a = c.dve(lambda e: e.tensor_scalar(b2c[:], b2c[:], rates[:, 2:3], None, ALU.mult), [last["dp", NPAIR]])
        c.dve(lambda e: e.scalar_tensor_tensor(b2n[:], b2n[:], rates[:, 3:4], b2c[:], ALU.mult, ALU.add), [a, red])
        for n, (gt, view, t) in enumerate([(g1[:, k], w1_v[:, k], sp[k]) for k in range(2)]
                                          + [(g2[:, 4 * k:4 * k + 4], w2T_v[:, 4 * k:4 * k + 4], sp[2 + k]) for k in range(2)]):
            w = t[:] if n < 2 else t[:].rearrange("p (a b) -> p a b", b=D)
            ld = c.dma(c.sync, f"g_old{n}", w, view, [last["dzs", 2 * NPAIR], last["dzs", 2 * NPAIR - 1], last["dz", 2 * NPAIR], last["dz", 2 * NPAIR - 1]])
            a = c.dve(lambda e, w=w: e.tensor_scalar(w, w, rates[:, 2:3], None, ALU.mult), [ld, keep])
            done = [last["g1", t] for t in range(4)] + [last["g2", t] for t in range(4)]
            c.dve(lambda e, w=w, gt=gt: e.scalar_tensor_tensor(gt, gt, rates[:, 3:4], w, ALU.mult, ALU.add), [a, step] + done)
        c.run()


NCH = NGRP
T = GRP * P
SLOTS = TOPK * NSLOT
OUTSIDE = 65536.0


def merge_phase(c, io, g1, g2, b1n, b2n, route, weight):
    nc = c.nc
    with ExitStack() as ctx:
        def sb(name, shape, dt=F32):
            return ctx.enter_context(nc.sbuf_tensor(name, shape, dt))

        def ps(name, shape, dt=F32):
            return ctx.enter_context(nc.psum_tensor(name, shape, dt))

        last = {}
        w1h, w1l = sb("m_w1_h", [P, KC, HID], F32R), sb("m_w1_l", [P, KC, HID], F32R)
        w2h, w2l = sb("m_w2_h", [P, HC, D], F32R), sb("m_w2_l", [P, HC, D], F32R)
        for k in range(KC):
            hi = c.act(act_copy(w1h[:, k], g1[:, k]))
            w1_ready = c.dve(sub(w1l[:, k], g1[:, k], w1h[:, k]), [hi])
        for k in range(2):
            r = slice(4 * k, 4 * k + 4)
            hi = c.act(act_copy(w2h[:, r], g2[:, r]))
            w2_ready = c.dve(sub(w2l[:, r], g2[:, r], w2h[:, r]), [hi])
        lin, lin_ready = {}, {}
        lin_f = [sb(f"lin_f{i}", [P, KC, D]) for i in range(2)]
        for n, k in enumerate(("lin1", "lin2")):
            lin[k] = sb(k + "_h", [P, KC, D], F32R), sb(k + "_l", [P, KC, D], F32R)
            ld = c.dma(c.sync, k, lin_f[n][:], io[k + "T"].rearrange("(c p) n -> p c n", p=P))
            hi = c.act(act_copy(lin[k][0][:], lin_f[n][:]), [ld])
            lin_ready[k] = c.dve(sub(lin[k][1][:], lin_f[n][:], lin[k][0][:]), [hi])
        gate = sb("gate_w", [P, KC, E])
        ld_gate = c.dma(c.sync, "gate_w", gate[:], io["gateT"].rearrange("(c p) n -> p c n", p=P))
        gate_b = sb("gate_bias", [P, E])
        ld_gb = c.dma(c.sync, "gate_b", gate_b[:], io["gate_b"])
        ident, before, ones = sb("m_ident", [P, P]), sb("m_before", [P, P]), sb("m_ones", [P, P])
        ld_ident = c.dma(c.sync, "m_ident", ident[:], io["ident"])
        ld_before = c.dma(c.sync, "m_before", before[:], io["before"])
        set_ones = c.pool(lambda e: e.memset(ones[:], 1.0))
        experts = sb("expert_ids", [P, E])
        ld_exp = c.dma(c.sync, "m_experts", experts[:], io["experts"])
        neg_half = sb("m_neg_half", [P, GRP])
        set_half = c.pool(lambda e: e.memset(neg_half[:], -0.5))
        counts = sb("expert_counts", [P, TOPK, E])
        set_counts = c.pool(lambda e: e.memset(counts[:], 0.0))

        zeros = sb("zeros", [P, 1024])
        set_zero = c.pool(lambda e: e.memset(zeros[:], 0.0))
        rows = SLOTS // P * D // 1024
        xbuf_rows = io["xbuf_d"].rearrange("(p a) d -> p (a d)", p=P)

        xT_f = [sb(f"m_xT{i}", [P, KC, T]) for i in range(2)]
        oT = [sb(f"m_oT{i}", [P, KC, T]) for i in range(2)]
        x_t = [sb(f"m_x{i}", [P, GRP, D]) for i in range(2)]
        xTh, xTl = sb("m_xTh", [P, KC, T], F32R), sb("m_xTl", [P, KC, T], F32R)
        oTh, oTl = sb("m_oTh", [P, KC, T], F32R), sb("m_oTl", [P, KC, T], F32R)
        st = [sb(f"m_sig{i}", [P, T]) for i in range(2)]
        hf = [sb(f"m_hf{i}", [P, T]) for i in range(2)]
        hh, hl = sb("m_hh", [P, HC, T], F32R), sb("m_hl", [P, HC, T], F32R)
        om, omh, oml = sb("memT", [P, KC, T]), sb("memT_h", [P, KC, T], F32R), sb("memT_l", [P, KC, T], F32R)
        ga, gb = sb("gate1", [P, KC, T]), sb("gate2", [P, KC, T])
        x1 = [sb(f"x1_{i}", [P, GRP, D]) for i in range(2)]
        x2 = [sb(f"xn2_{i}", [P, GRP, D]) for i in range(3)]
        x2T = sb("xn2T", [P, KC, T])
        stats, mv, rstd = sb("m_stats", [P, GRP, 6]), sb("m_mv", [P, GRP, 2]), sb("m_rstd", [P, 2, GRP])
        lg = sb("logits", [P, GRP, E])
        pr = sb("router_probs", [P, GRP, E])
        mx, sm = sb("router_max", [P, GRP]), sb("router_sum", [P, 2, GRP])
        top = sb("router_top", [P, GRP, 8])
        idx = sb("router_idx", [P, GRP, 8], mybir.dt.uint32)
        idf = sb("router_idf", [P, TOPK, GRP])
        hot = sb("router_hot", [P, TOPK, GRP, E])
        pos_e, pos = sb("router_pos_e", [P, TOPK, GRP, E]), sb("router_pos", [P, TOPK, GRP])
        keep = sb("router_keep", [P, TOPK, GRP])
        slot, slot2 = sb("router_slot", [P, TOPK, GRP]), sb("router_slot2", [P, TOPK, GRP])
        sidx = [sb(f"scatter_rows{i}", [P, TOPK, GRP], I32) for i in range(2)]

        ps_z = [ps(f"m_ps_z{i}", [P, T]) for i in range(2)]
        ps_o = [ps(f"m_ps_o{i}", [P, T]) for i in range(2)]
        ps_r = ps("m_ps_r", [P, GRP, D])
        ps_l = ps("m_ps_l", [P, 512])
        ps_c = ps("m_ps_c", [P, 512])
        x_v = io["x"].rearrange("(g j p) d -> g p j d", j=GRP, p=P)
        x1_v = io["x1_d"].rearrange("(g j p) d -> g p j d", j=GRP, p=P)
        turn = [0]

        def load_xT(C):
            for h in range(2):
                t = slice(2 * h * P, (2 * h + 2) * P)
                last["ld_xT", C] = c.dma(c.sync, f"m_xT{C % 2}", xT_f[C % 2][:, :, t], io["xT_d"][2 * C + h], [last.get(("xTl", C - 2))])

        def load_rest(C):
            s = C % 2
            for h in range(2):
                t = slice(2 * h * P, (2 * h + 2) * P)
                last["ld_oT", C] = c.dma(c.sync, f"m_oT{s}", oT[s][:, :, t], io["oT_d"][2 * C + h], [last.get(("merge", C - 2))])
            last["ld_x", C] = c.dma(c.sync, f"m_x{s}", x_t[s][:], x_v[C], [last.get(("x1", C - 2))])

        def split_inputs(C):
            s = C % 2
            h = c.act(act_copy(xTh[:], xT_f[s][:]), [last["ld_xT", C], last.get(("z", C - 1))])
            last["xTl", C] = c.dve(sub(xTl[:], xT_f[s][:], xTh[:]), [h, last.get(("z", C - 1))])
            h = c.act(act_copy(oTh[:], oT[s][:]), [last["ld_oT", C], last.get(("g1", C - 1))])
            last["oTl", C] = c.dve(sub(oTl[:], oT[s][:], oTh[:]), [h, last.get(("g1", C - 1))])

        def hidden(C, t):
            acc, key, mc, r = ps_z[t % 2], ("ps_z", t % 2), slice(t * P, (t + 1) * P), t % 2
            z = c.pe(matmul_split(acc[:], [(w1h[:, k, mc], w1l[:, k, mc]) for k in range(KC)],
                                  [(xTh[:, k], xTl[:, k]) for k in range(KC)]), [last["xTl", C], w1_ready, last.get(key)])
            last["z", C] = z
            s = c.act(lambda e: e.activation(st[r][:], acc[:], ACTF.Sigmoid, bias=b1n[:, t:t + 1]), [z, last.get(("hf", r))])
            h = c.dve(lambda e: e.scalar_tensor_tensor(hf[r][:], acc[:], b1n[:, t:t + 1], st[r][:], ALU.add, ALU.mult),
                      [s, last.get(("hl", r))])
            last[key] = last["hf", r] = h
            hi = c.act(act_copy(hh[:, t], hf[r][:]), [h, last.get(("om", C - 1))])
            last["hl", r] = c.pool(sub(hl[:, t], hf[r][:], hh[:, t]), [hi, last.get(("om", C - 1))])

        def bank():
            turn[0] += 1
            return ps_o[turn[0] % 2], ("ps_o", turn[0] % 2)

        def linear_gate(C, name, dst, high, low, ready, free):
            wh, wl = lin[name]
            for m in range(KC):
                acc, key = bank()
                mc = slice(m * P, (m + 1) * P)
                mm = c.pe(matmul_split(acc[:], [(wh[:, k, mc], wl[:, k, mc]) for k in range(KC)],
                                       [(high[:, k], low[:, k]) for k in range(KC)]), [ready, lin_ready[name], last.get(key)])
                last[key] = a = c.act(lambda e, m=m, acc=acc: e.activation(dst[:, m], acc[:], ACTF.Sigmoid), [mm] + free)
            return mm, a

        def memory_out(C, m):
            acc, key = bank()
            mc = slice(m * P, (m + 1) * P)
            mm = c.pe(matmul_split(acc[:], [(w2h[:, k, mc], w2l[:, k, mc]) for k in range(HC)],
                                   [(hh[:, k], hl[:, k]) for k in range(HC)]),
                      [last["hl", 0], last["hl", 1], w2_ready, last.get(key)])
            last["om", C] = mm
            f = c.act(lambda e: e.activation(om[:, m], acc[:], ACTF.Identity, bias=b2n[:, m:m + 1]),
                      [mm, last.get(("merge_om", C - 1)), last.get(("oml", C - 1, m))])
            last[key] = f
            hi = c.dve(copy(omh[:, m], om[:, m]), [f, last.get(("g2", C - 1))])
            last["oml", C, m] = c.dve(sub(oml[:, m], om[:, m], omh[:, m]), [hi, last.get(("g2", C - 1))])

        def gate1(C):
            mm, last["ga", C] = linear_gate(C, "lin1", ga, oTh, oTl, last["oTl", C], [last.get(("merge", C - 1)), last.get(("mergeT", C - 1))])
            last["g1", C] = mm

        def gate2(C):
            mm, g = linear_gate(C, "lin2", gb, omh, oml, last["oml", C, 1], [last.get(("merge", C - 1))])
            last["g2", C] = mm
            s = C % 2
            a = c.dve(lambda e: e.tensor_tensor(ga[:], ga[:], oT[s][:], ALU.mult), [last["ga", C]])
            b = c.pool(lambda e: e.tensor_tensor(gb[:], gb[:], om[:], ALU.mult), [g, last["oml", C, 0]])
            last["merge_om", C] = b
            last["merge", C] = c.dve(add(ga[:], ga[:], gb[:]), [a, b])

        def residual(C):
            def emit(e):
                for j in range(GRP):
                    for m in range(KC):
                        i = e.transpose(ps_r[:, j, m * P:(m + 1) * P], ga[:, m, j * P:(j + 1) * P], ident[:])
                return i
            t = c.pe(emit, [last["merge", C], ld_ident, last.get("ps_r")])
            last["mergeT", C] = t
            y, z = x1[C % 2], x2[C % 3]
            a = c.dve(add(y[:], ps_r[:], x_t[C % 2][:]), [t, last["ld_x", C], last.get(("x1_st", C - 2)), last.get(("ln2", C - 2))])
            last["ps_r"] = last["x1", C] = a
            last["x1_st", C] = c.dma(c.sync, f"x1_st{C % 2}", x1_v[C], y[:], [a])
            for j in range(GRP):
                b = c.dve(lambda e, j=j: e.bn_stats(stats[:, j], y[:, j]), [a, last.get("mv")])
            for j in range(GRP):
                g = c.dve(lambda e, j=j: e.bn_aggr(mv[:, j], stats[:, j]), [b, last.get(("ln2", C - 1))])
            last["mv"] = g
            v = c.dve(lambda e: e.tensor_scalar(rstd[:, 0], mv[:, :, 1], EPS, None, ALU.add), [g, last.get("rstd")])
            r = c.pool(lambda e: e.tensor_tensor(rstd[:, 1], rstd[:, 0], neg_half[:], ALU.pow), [v, set_half, last.get(("ln2", C - 1))])
            last["rstd"] = r
            for j in range(GRP):
                n = c.dve(lambda e, j=j: e.tensor_scalar(z[:, j], y[:, j], mv[:, j, 0:1], rstd[:, 1, j:j + 1], ALU.subtract, ALU.mult),
                          [r] + last.get(("scatter", C - 3), []))
            last["ln2", C] = n

        def transpose_x2(C):
            z = x2[C % 3]

            def emit(e):
                for m in range(KC):
                    for j in range(GRP):
                        i = e.transpose(ps_r[:, 2 * m + j // 2, (j % 2) * P:(j % 2 + 1) * P], z[:, j, m * P:(m + 1) * P], ident[:])
                return i
            t = c.pe(emit, [last["ln2", C], last.get("ps_r")])
            last["x2T", C] = last["ps_r"] = c.act(act_copy(x2T[:].rearrange("p m t -> p (m t)"), ps_r[:].rearrange("p a b -> p (a b)")),
                                                  [t, last.get(("logits", C - 1))])

        def router(C):
            def emit(e):
                for j in range(GRP):
                    for k in range(KC):
                        i = e.matmul(ps_l[:, j * E:(j + 1) * E], x2T[:, k, j * P:(j + 1) * P], gate[:, k], start=k == 0, stop=k == KC - 1)
                return i
            mm = c.pe(emit, [last["x2T", C], ld_gate, last.get("ps_l")])
            last["logits", C] = mm
            wide = [P, GRP, E]
            src = ps_l[:, 0:GRP * E].rearrange("p (j x) -> p j x", x=E)
            a = c.dve(add(lg[:], src, gate_b[:].unsqueeze(1).broadcast_to(wide)), [mm, ld_gb, last.get("sh")])
            last["ps_l"] = a
            m = c.dve(lambda e: e.tensor_reduce(mx[:], lg[:], AX.X, ALU.max), [a, last.get("sh")])
            s = c.dve(sub(lg[:], lg[:], mx[:].unsqueeze(2).broadcast_to(wide)), [m, last.get("ex")])
            last["sh"] = s
            x = c.act(lambda e: e.activation(pr[:], lg[:], ACTF.Exp), [s, last.get("find")])
            last["ex"] = x
            r = c.dve(lambda e: e.tensor_reduce(sm[:, 0], pr[:], AX.X, ALU.add), [x, last.get("probs")])
            r = c.dve(lambda e: e.reciprocal(sm[:, 1], sm[:, 0]), [r])
            q = c.dve(lambda e: e.tensor_tensor(pr[:], pr[:], sm[:, 1].unsqueeze(2).broadcast_to(wide), ALU.mult), [r])
            last["probs"] = q
            for j in range(GRP):
                t = c.dve(lambda e, j=j: e.max(top[:, j], pr[:, j]), [q, last.get("weights")])
            for j in range(GRP):
                f = c.dve(lambda e, j=j: e.max_index(idx[:, j], top[:, j], pr[:, j]), [t, last.get("idf")])
            last["find"] = f
            d = c.dve(copy(idf[:], idx[:, :, 0:TOPK].rearrange("p j k -> p k j")), [f, last.get("slots")])
            last["idf"] = d
            for k in range(TOPK):
                o = c.dve(lambda e, k=k: e.tensor_tensor(hot[:, k], experts[:].unsqueeze(1).broadcast_to(wide),
                                                         idf[:, k].unsqueeze(2).broadcast_to(wide), ALU.is_equal),
                          [d, ld_exp, last.get("pos_e"), last.get("count_pe")])
            last["hot", C] = o

        def dispatch(C):
            n = TOPK * E

            def emit(e):
                for j in range(GRP + 1):
                    out = ps_c[:, j * n:(j + 1) * n].rearrange("p (k x) -> p k x", x=E)
                    for i in range(min(j, GRP - 1) + 1):
                        lhs = before if i == j else ones
                        x = e.matmul(out, lhs[:], hot[:, :, i], start=i == 0, stop=i == min(j, GRP - 1))
                return x
            mm = c.pe(emit, [last["hot", C], ld_before, set_ones, last.get("ps_c")])
            last["count_pe"] = mm
            wide = [P, GRP, E]
            for k in range(TOPK):
                src = ps_c[:, 0:GRP * n].rearrange("p (j k x) -> p j k x", k=TOPK, x=E)[:, :, k]
                a = c.dve(add(pos_e[:, k], src, counts[:, k].unsqueeze(1).broadcast_to(wide)), [mm, set_counts, last.get("counts"), last.get("pos")])
            cn = c.dve(add(counts[:], counts[:], ps_c[:, GRP * n:(GRP + 1) * n].rearrange("p (k x) -> p k x", x=E)), [a, mm])
            last["ps_c"] = last["counts"] = cn
            b = c.dve(lambda e: e.tensor_tensor(pos_e[:], pos_e[:], hot[:], ALU.mult), [a])
            last["pos_e"] = b
            p = c.dve(lambda e: e.tensor_reduce(pos[:], pos_e[:], AX.X, ALU.add), [b, last.get("slots")])
            last["pos"] = p
            k1 = c.dve(lambda e: e.tensor_scalar(keep[:], pos[:], float(CAP), None, ALU.is_lt), [p, last.get("slots")])
            cols = slice(C * GRP, (C + 1) * GRP)
            s = c.dve(lambda e: e.scalar_tensor_tensor(slot[:], idf[:], float(CAP), pos[:], ALU.mult, ALU.add), [p, last.get("slots")])
            s = c.dve(lambda e: e.tensor_scalar(slot[:, 1], slot[:, 1], float(NSLOT), None, ALU.add), [s])
            u = c.dve(lambda e: e.tensor_scalar(slot2[:], keep[:], -OUTSIDE, OUTSIDE, ALU.mult, ALU.add), [k1, last.get("slots")])
            sc = c.dve(add(sidx[C % 2][:], slot[:], slot2[:]), [s, u] + last.get(("scatter", C - 2), []))
            ends = [float(NSLOT * (k + 1) - 1) for k in range(TOPK)]
            for k in range(TOPK):
                v = c.dve(lambda e, k=k: e.tensor_scalar(slot[:, k], slot[:, k], -ends[k], None, ALU.add), [sc])
            v = c.dve(lambda e: e.tensor_tensor(slot[:], slot[:], keep[:], ALU.mult), [v])
            v2 = c.dve(lambda e: e.tensor_scalar(route[:, :, cols], slot[:], float(NSLOT - 1), None, ALU.add), [v])
            w = c.dve(lambda e: e.tensor_tensor(weight[:, :, cols], top[:, :, 0:TOPK].rearrange("p j k -> p k j"), keep[:], ALU.mult), [k1])
            last["weights"] = last["slots"] = w
            last["route"] = v2
            steps = []
            for k in range(TOPK):
                for j in range(GRP):
                    sem = c.sem(f"dma_scatter{C % 3}", dma=True)
                    sem.count += 16
                    after = [sc, last["ln2", C]] + zero_done
                    st_ = Step(c.pool, lambda e, k=k, j=j: e.indirect_dma_start(
                        io["xbuf_d"], bass.IndirectOffsetOnAxis(ap=sidx[C % 2][:, k, j:j + 1], axis=0), x2[C % 3][:, j], None,
                        bounds_check=SLOTS - 1, oob_is_err=False), after, sem, sem.count)
                    for a_ in st_.after:
                        a_.awaited = True
                    c.pool.steps.append(st_)
                    steps.append(st_)
            last["scatter", C] = steps[-1:]

        load_xT(0)
        load_rest(0)
        zero_done = []
        for n in range(rows):
            zero_done.append(c.dma(c.act, "zero", xbuf_rows[:, n * 1024:(n + 1) * 1024], zeros[:], [set_zero]))
        zero_done = zero_done[-1:]
        load_xT(1)
        for C in range(NCH + 2):
            now, tail = C < NCH, 1 <= C <= NCH
            if now:
                split_inputs(C)
                hidden(C, 0)
            if tail:
                gate2(C - 1)
            if C >= 2:
                dispatch(C - 2)
            if now:
                for t in range(1, 5):
                    hidden(C, t)
            if tail:
                residual(C - 1)
            if C + 1 < NCH:
                load_rest(C + 1)
            if now:
                for t in range(5, HC):
                    hidden(C, t)
                gate1(C)
                memory_out(C, 0)
            if tail:
                transpose_x2(C - 1)
            if now:
                memory_out(C, 1)
            if tail:
                router(C - 1)
            if C + 2 < NCH:
                load_xT(C + 2)
        ends = [last["x1_st", C] for C in (NCH - 1, NCH - 2)]
        for C in range(NCH - 3, NCH):
            ends += last["scatter", C][-1:]
        c.sync(lambda e: e.nop(), ends)
        c.run()


SB = CAP // P
HALF = CAP // 2


def expert_phase(c, io, route, weight):
    nc = c.nc
    with ExitStack() as ctx:
        def sb(name, shape, dt=F32):
            return ctx.enter_context(nc.sbuf_tensor(name, shape, dt))

        def ps(name, shape, dt=F32):
            return ctx.enter_context(nc.psum_tensor(name, shape, dt))

        last = {}
        ident = sb("e_ident", [P, P])
        ld_ident = c.dma(c.sync, "e_ident", ident[:], io["ident"])
        b1, b2 = sb("e_b1", [P, E, HC]), sb("e_b2", [P, E, KC])
        ld_b1 = c.dma(c.sync, "e_b1", b1[:], io["eb1"])
        ld_b2 = c.dma(c.sync, "e_b2", b2[:], io["eb2"])
        acc = sb("acc", [P, NBLK, D])
        s1, s2 = sb("e_w1_f", [P, KC, HID]), sb("e_w2_f", [P, HC, D])
        w1h, w1l = sb("e_w1_h", [P, KC, HID], F32R), sb("e_w1_l", [P, KC, HID], F32R)
        w2h, w2l = sb("e_w2_h", [P, HC, D], F32R), sb("e_w2_l", [P, HC, D], F32R)
        xs = [sb(f"slots{i}", [P, SB, D]) for i in range(2)]
        xh, xl = sb("slotsT_h", [P, KC, CAP], F32R), sb("slotsT_l", [P, KC, CAP], F32R)
        hf = [sb(f"e_hf{i}", [P, CAP]) for i in range(2)]
        hh, hl = sb("e_hh", [P, HC, CAP], F32R), sb("e_hl", [P, HC, CAP], F32R)
        yT = sb("e_yT", [P, KC, CAP])
        ys = sb("e_ys", [P, SB, D])
        yg = [sb(f"gathered{i}", [P, D]) for i in range(4)]
        ps_z = [ps(f"e_ps_z{i}", [P, 2, 512]) for i in range(2)]
        ps_x = ps("e_ps_x", [P, 4 * D])
        ps_t = ps("e_ps_t", [P, 4, D])
        x_v = io["xbuf_d"].rearrange("(i b p) d -> i p b d", b=SB, p=P)
        y_v = [io[f"ybuf{k}_d"].rearrange("(i b p) d -> i p b d", b=SB, p=P) for k in range(TOPK)]
        N = TOPK * E

        def load_slots(i):
            last["xs", i] = c.dma(c.sync, f"slots{i % 2}", xs[i % 2][:], x_v[i], [last.get(("xT_pe", i - 2))])

        def load_w(i):
            e = i % E
            last["ld_w1", i] = c.dma(c.sync, "e_w1", s1[:], io["W1"][e].rearrange("(c p) n -> p c n", p=P), [last.get(("w1", i - 1))])
            last["ld_w2", i] = c.dma(c.sync, "e_w2", s2[:], io["W2"][e].rearrange("(c p) n -> p c n", p=P), [last.get(("w2", i - 1))])

        def split_w1(i):
            for k in range(KC):
                hi = c.act(act_copy(w1h[:, k], s1[:, k]), [last["ld_w1", i], last.get(("h", i - 1))])
                last["w1", i] = c.pool(sub(w1l[:, k], s1[:, k], w1h[:, k]), [hi, last.get(("h", i - 1))])

        def split_w2(i):
            for k in range(2):
                r = slice(4 * k, 4 * k + 4)
                hi = c.dve(copy(w2h[:, r], s2[:, r]), [last["ld_w2", i], last.get(("y", i - 1))])
                last["w2", i] = c.dve(sub(w2l[:, r], s2[:, r], w2h[:, r]), [hi, last.get(("y", i - 1))])

        def transpose_slots(i, blocks):
            n = len(blocks)

            def emit(e):
                for m in range(KC):
                    for a, b in enumerate(blocks):
                        x = e.transpose(ps_x[:, (m * n + a) * P:(m * n + a + 1) * P], xs[i % 2][:, b, m * P:(m + 1) * P], ident[:])
                return x
            t = c.pe(emit, [last["xs", i], ld_ident, last.get("ps_x")])
            last["xT_pe", i] = t
            cols = slice(blocks[0] * P, (blocks[-1] + 1) * P)
            src = ps_x[:, 0:KC * n * P].rearrange("p (m t) -> p m t", m=KC)
            hi = c.act(act_copy(xh[:, :, cols], src), [t, last.get(("h", i - 1))])
            last["ps_x"] = last["xT", i] = c.dve(sub(xl[:, :, cols], src, xh[:, :, cols]), [hi, last.get(("h", i - 1))])

        turn = [0]

        def bank():
            turn[0] += 1
            return ps_z[turn[0] % 2], ("ps_z", turn[0] % 2)

        def product(out, lhs, rhs, after):
            def emit(e):
                for s in range(2):
                    cols = slice(s * HALF, (s + 1) * HALF)
                    x = matmul_split(out[:, s, 0:HALF], lhs, [(h[:, cols], l[:, cols]) for h, l in rhs])(e)
                return x
            return c.pe(emit, after)

        def up(i, t):
            e_, mc, (out, key), r = i % E, slice(t * P, (t + 1) * P), bank(), t % 2
            mm = product(out, [(w1h[:, k, mc], w1l[:, k, mc]) for k in range(KC)],
                         [(xh[:, k], xl[:, k]) for k in range(KC)], [last["xT", i], last["w1", i], last.get(key)])
            last["h", i] = mm
            src, bias = out[:, :, 0:HALF], b1[:, e_, t:t + 1]
            two = lambda ap: ap.rearrange("p (s n) -> p s n", s=2)
            hi = c.act(lambda e: e.activation(two(hh[:, t]), src, ACTF.Relu, bias=bias), [mm, ld_b1, last.get(("y", i - 1))])
            f = c.dve(lambda e: e.tensor_scalar(two(hf[r][:]), src, bias, 0.0, ALU.add, ALU.max), [hi, last.get(("hl", r))])
            last[key] = f
            last["hl", r] = c.pool(sub(hl[:, t], hf[r][:], hh[:, t]), [f, last.get(("y", i - 1))])

        def down(i, m):
            mc, (out, key) = slice(m * P, (m + 1) * P), bank()
            mm = product(out, [(w2h[:, k, mc], w2l[:, k, mc]) for k in range(HC)],
                         [(hh[:, k], hl[:, k]) for k in range(HC)], [last["hl", 0], last["hl", 1], last["w2", i], last.get(key)])
            last["y", i] = mm
            last[key] = last["yT", i] = c.act(
                lambda e: e.activation(yT[:, m].rearrange("p (s n) -> p s n", s=2), out[:, :, 0:HALF], ACTF.Identity, bias=b2[:, i % E, m:m + 1]),
                [mm, ld_b2, last.get(("yT_pe", i - 1))])

        def transpose_y(i, blocks):
            def emit(e):
                for a, b in enumerate(blocks):
                    for m in range(KC):
                        x = e.transpose(ps_t[:, a, m * P:(m + 1) * P], yT[:, m, b * P:(b + 1) * P], ident[:])
                return x
            t = c.pe(emit, [last["yT", i], last.get("ps_t")])
            last["yT_pe", i] = t
            n = len(blocks)
            d = c.dve(copy(ys[:, blocks[0]:blocks[0] + n], ps_t[:, 0:n]), [t, last.get(("ys_st", i - 1))])
            last["ps_t"] = d
            return d

        def store_y(i, d):
            last["ys_st", i] = c.dma(c.sync, "ys_st", y_v[i // E][i % E], ys[:], [d])

        def combine(k, g):
            n = k * NBLK + g
            sem = c.sem(f"dma_gather{n % 4}", dma=True)
            sem.count += 16
            st = Step(c.pool, lambda e: e.indirect_dma_start(
                yg[n % 4][:], None, io[f"ybuf{k}_d"], bass.IndirectOffsetOnAxis(ap=route[:, k, g:g + 1], axis=0),
                bounds_check=NSLOT - 1, oob_is_err=False),
                [last["ys_st", k * E + E - 1], last.get(("yg", n % 4))], sem, sem.count)
            for a in st.after:
                a.awaited = True
            c.pool.steps.append(st)
            last["yg", n % 4] = last["acc", g] = c.dve(lambda e: e.scalar_tensor_tensor(
                acc[:, g], yg[n % 4][:], weight[:, k, g:g + 1], acc[:, g], ALU.mult, ALU.add), [st, ld_acc, last.get(("acc", g))])

        load_w(0)
        load_slots(0)
        load_slots(1)
        acc_v = io["x1_d"].rearrange("(g p) d -> p g d", p=P)
        for q in range(4):
            ld_acc = c.dma(c.act, "acc", acc[:, 16 * q:16 * q + 16], acc_v[:, 16 * q:16 * q + 16])
        split_w1(0)
        split_w2(0)
        transpose_slots(0, [0, 1, 2, 3])
        transpose_slots(0, [4])
        load_w(1)
        gathers = [(0, g) for g in range(NBLK)]
        per = -(-NBLK // (E - 1))
        for i in range(N):
            for t in range(HC):
                up(i, t)
                if t == 2 and i:
                    d = transpose_y(i - 1, [0, 1, 2, 3])
                if t == 5 and i:
                    d = transpose_y(i - 1, [4])
                    store_y(i - 1, d)
            if i + 1 < N:
                split_w1(i + 1)
            if i > E:
                for k, g in gathers[:per]:
                    combine(k, g)
                del gathers[:per]
            down(i, 0)
            if i + 1 < N:
                transpose_slots(i + 1, [0, 1, 2, 3])
            down(i, 1)
            if i + 1 < N:
                transpose_slots(i + 1, [4])
                split_w2(i + 1)
            if i + 2 < N:
                load_w(i + 2)
                load_slots(i + 2)
        transpose_y(N - 1, [0, 1, 2, 3])
        store_y(N - 1, transpose_y(N - 1, [4]))
        out_v = io["out"].rearrange("(g p) d -> p g d", p=P)
        done = []
        for g in range(NBLK):
            combine(1, g)
            if g % GRP == GRP - 1:
                done.append(c.dma(c.sync, "out", out_v[:, g - GRP + 1:g + 1], acc[:, g - GRP + 1:g + 1], [last["acc", g]]))
        c.sync(lambda e: e.nop(), done[-1:] + [last["ys_st", N - 1]])
        c.run()


def build(nc, io):
    io["xn_d"] = nc.dram_tensor("xn_d", [NPAIR + 1, P, 2, D], F32).ap()
    io["xT_d"] = nc.dram_tensor("xT_d", [NPAIR + 1, P, KC, 2 * P], F32).ap()
    io["oT_d"] = nc.dram_tensor("oT_d", [NPAIR + 1, P, KC, 2 * P], F32).ap()
    io["x1_d"] = nc.dram_tensor("x1_d", [NT, D], F32).ap()
    io["xbuf_d"] = nc.dram_tensor("xbuf_d", [TOPK * NSLOT, D], F32).ap()
    for k in range(TOPK):
        io[f"ybuf{k}_d"] = nc.dram_tensor(f"ybuf{k}_d", [NSLOT, D], F32).ap()
    with ExitStack() as ctx:
        def sb(name, shape, dt=F32):
            return ctx.enter_context(nc.sbuf_tensor(name, shape, dt))

        c = Core(nc, ctx)
        attention_phase(c, io)
        route, weight = sb("route", [P, TOPK, NBLK], I32), sb("route_weight", [P, TOPK, NBLK])
        with ExitStack() as weights:
            g1 = weights.enter_context(nc.sbuf_tensor("new_w1T", [P, KC, HID], F32))
            g2 = weights.enter_context(nc.sbuf_tensor("new_w2T", [P, HC, D], F32))
            b1n = weights.enter_context(nc.sbuf_tensor("new_b1", [P, HC], F32))
            b2n = weights.enter_context(nc.sbuf_tensor("new_b2", [P, KC], F32))
            gradient_phase(c, io, g1, g2, b1n, b2n)
            merge_phase(c, io, g1, g2, b1n, b2n, route, weight)
        expert_phase(c, io, route, weight)


def window_masks():
    q, k = np.arange(P)[:, None], np.arange(P)[None]
    masks = np.full((3, P, 2 * P), -1e30, np.float32)
    masks[0, :, :P][k > q] = 0
    masks[0, :, P:][k <= q] = 0
    masks[1] = masks[0]
    masks[1, :, :P - NMEM] = -1e30
    masks[2, :, :P][(k >= P - NMEM) & (k <= q)] = 0
    return masks


def layouts(a):
    t = np.ascontiguousarray
    io = {"x": a["L0_attn_x"].reshape(NT, D), "memp": np.zeros((P, D), np.float32)}
    io["memp"][P - NMEM:] = a["L0_attn_mem"]
    for k in ("wq", "wk", "wv", "wo", "w1", "w2", "lin1", "lin2"):
        io[k + "T"] = t(a["L0_attn_" + k].T)
    io["w2"], io["b1"] = a["L0_attn_w2"], a["L0_attn_b1"]
    io["b1c"] = t(a["L0_attn_b1"].reshape(HC, P).T)
    io["b2c"] = t(a["L0_attn_b2"].reshape(KC, P).T)
    io["rates"] = np.empty((P, 2), np.float32)
    io["rates"][:, 0], io["rates"][:, 1] = a["L0_attn_alpha"], a["L0_attn_theta"]
    io["gateT"] = t(a["L0_ffn_gate_w"].T)
    io["gate_b"] = t(np.broadcast_to(a["L0_ffn_gate_b"], (P, E)))
    io["W1"], io["W2"] = a["L0_ffn_W1"], a["L0_ffn_W2"]
    io["eb1"] = t(a["L0_ffn_b1"].reshape(E, HC, P).transpose(2, 0, 1))
    io["eb2"] = t(a["L0_ffn_b2"].reshape(E, KC, P).transpose(2, 0, 1))
    io["ident"] = np.eye(P, dtype=np.float32)
    io["masks"] = window_masks()
    io["before"] = np.triu(np.ones((P, P), np.float32), 1)
    io["experts"] = t(np.broadcast_to(np.arange(E, dtype=np.float32), (P, E)))
    io["mem_scale"] = np.zeros((P, P), np.float32)
    io["mem_scale"][:, P - NMEM:] = B
    return io


def kernel(**inputs):
    import concourse.bacc as bacc
    from concourse.bass_utils import run_bass_kernel_spmd

    arrays = layouts({k: np.asarray(v) for k, v in inputs.items()})
    nc = bacc.Bacc("TRN2", target_bir_lowering=False, num_devices=1)
    io = {k: nc.dram_tensor("in_" + k, v.shape, F32, kind="ExternalInput").ap() for k, v in arrays.items()}
    io["out"] = nc.dram_tensor("out", [NT, D], F32, kind="ExternalOutput").ap()
    build(nc, io)
    r = run_bass_kernel_spmd(nc, [{"in_" + k: v for k, v in arrays.items()}], core_ids=[0])
    return r.results[0]["out"].reshape(B, S, D)
```

```python
import numpy as np
import concourse.bass as bass
from concourse import mybir
from concourse.alu_op_type import AluOpType as ALU
from contextlib import ExitStack

F32 = mybir.dt.float32
F32R = mybir.dt.float32r
BF16 = mybir.dt.bfloat16
I32 = mybir.dt.int32
ACTF = mybir.ActivationFunctionType
AX = mybir.AxisListType

P = 128
B, S, D = 8, 1024, 256
HID = 1024
HEADS, DH = 4, 64
NMEM = 64
NT = B * S
NBLK = NT // P
GRP = 4
NGRP = NBLK // GRP
NPAIR = NBLK // 2
KC = D // P
HC = HID // P
E, TOPK, CAP = 8, 2, 640
NSLOT = E * CAP
EPS = 1e-5
NPR = 3


class Step:

    def __init__(self, queue, emit, after, sem=None, value=None):
        self.queue, self.emit, self.after = queue, emit, [s for s in after if s is not None]
        self.sem, self.value, self.awaited = sem, value, sem is not None


class Queue:

    def __init__(self, engine, done):
        self.engine, self.done, self.steps = engine, done, []

    def __call__(self, emit, after=()):
        step = Step(self, emit, after)
        for s in step.after:
            s.awaited = True
        self.steps.append(step)
        return step

    def number(self):
        for s in self.steps:
            if s.awaited and s.sem is None:
                self.done.count += 1
                s.sem, s.value = self.done, self.done.count

    def drain(self, handle):
        for s in self.steps:
            for w in s.after:
                if self.passed.get(w.sem.name, 0) < w.value:
                    handle.wait_ge(w.sem.sem, w.value)
                    self.passed[w.sem.name] = w.value
            last = s.emit(self.engine)
            if s.sem is not None:
                last.then_inc(s.sem.sem, 16 if s.sem.dma else 1)
        self.steps = []

    passed = None


class Sem:
    def __init__(self, sem, name, dma=False):
        self.sem, self.name, self.dma, self.count = sem, name, dma, 0


class Core:

    def __init__(self, nc, ctx):
        self.nc, self.ctx = nc, ctx
        self.sems = {}
        self.pe = Queue(nc.tensor, self.sem("pe_done"))
        self.act = Queue(nc.scalar, self.sem("act_done"))
        self.dve = Queue(nc.vector, self.sem("dve_done"))
        self.pool = Queue(nc.gpsimd, self.sem("pool_done"))
        self.sync = Queue(nc.sync, self.sem("sync_done"))
        for q in self.queues():
            q.passed = {}

    def queues(self):
        return [self.pe, self.act, self.dve, self.pool, self.sync]

    def sem(self, name, dma=False):
        if name not in self.sems:
            self.sems[name] = Sem(self.ctx.enter_context(self.nc.semaphore(name)), name, dma)
        return self.sems[name]

    def dma(self, queue, buffer, out, in_, after=()):
        sem = self.sem("dma_" + buffer, dma=True)
        sem.count += 16
        step = Step(queue, lambda e: e.dma_start(out, in_), after, sem, sem.count)
        for s in step.after:
            s.awaited = True
        queue.steps.append(step)
        return step

    def run(self):
        for q in self.queues():
            q.number()
        with self.nc.Block() as block:
            block.tensor(self.pe.drain)
            block.scalar(self.act.drain)
            block.vector(self.dve.drain)
            block.gpsimd(self.pool.drain)
            block.sync(self.sync.drain)


def matmul_split(out, lhs, rhs, first=True, last=True):
    terms = []
    for (ah, al), (bh, bl) in zip(lhs, rhs):
        terms += [(al, bh), (ah, bl), (ah, bh)]

    def emit(e):
        for n, (a, b) in enumerate(terms):
            i = e.matmul(out, a, b, start=first and n == 0, stop=last and n == len(terms) - 1)
        return i
    return emit


def copy(out, in_):
    return lambda e: e.tensor_copy(out, in_)


def act_copy(out, in_):
    return lambda e: e.activation(out, in_, ACTF.Copy)


def sub(out, a, b):
    return lambda e: e.tensor_tensor(out, a, b, ALU.subtract)


def add(out, a, b):
    return lambda e: e.tensor_tensor(out, a, b, ALU.add)


def attention_phase(c, io):
    nc = c.nc
    with ExitStack() as ctx:
        def sb(name, shape, dt=F32):
            return ctx.enter_context(nc.sbuf_tensor(name, shape, dt))

        def ps(name, shape, dt=F32):
            return ctx.enter_context(nc.psum_tensor(name, shape, dt))

        pr = [sb(f"prob{i}", [P, HEADS, 2 * P]) for i in range(NPR)]
        w = {}
        ws = []
        for n, k in enumerate(("wq", "wk", "wv", "wo")):
            hi, lo = sb(k + "_h", [P, KC, D], F32R), sb(k + "_l", [P, KC, D], F32R)
            full = pr[n // 2][:, 2 * (n % 2):2 * (n % 2) + 2]
            ld = c.dma(c.sync, k, full, io[k + "T"].rearrange("(c p) n -> p c n", p=P))
            h = c.dve(copy(hi[:], full), [ld])
            ws.append(c.dve(sub(lo[:], full, hi[:]), [h]))
            w[k] = (hi, lo)
        ident, masks = sb("a_ident", [P, P]), sb("a_masks", [P, 3, 2 * P])
        ld_ident = c.dma(c.sync, "a_ident", ident[:], io["ident"])
        ld_masks = c.dma(c.sync, "a_masks", masks[:], io["masks"].rearrange("m p k -> p m k"))
        neg_half = sb("neg_half", [P, GRP])
        set_half = c.pool(lambda e: e.memset(neg_half[:], -0.5))

        x_g = [sb(f"x_g{i}", [P, GRP, D]) for i in range(2)]
        xn = [sb(f"xn{i}", [P, GRP, D]) for i in range(2)]
        stats = [sb(f"ln_stats{i}", [P, GRP, 6]) for i in range(2)]
        mv = [sb(f"ln_mv{i}", [P, GRP, 2]) for i in range(2)]
        rstd = [sb(f"ln_rstd{i}", [P, 2, GRP]) for i in range(2)]
        xT = [sb(f"xT{i}", [P, KC, GRP * P]) for i in range(2)]
        xTh = [sb(f"xTh{i}", [P, KC, GRP * P], F32R) for i in range(2)]
        xTl = [sb(f"xTl{i}", [P, KC, GRP * P], F32R) for i in range(2)]
        qh = [sb(f"qh{i}", [P, KC, GRP * P if i < 3 else P], F32R) for i in range(4)]
        ql = [sb(f"ql{i}", [P, KC, GRP * P if i < 3 else P], F32R) for i in range(4)]
        kh = [sb(f"kh{i}", [P, KC, 9 * P], F32R) for i in range(2)]
        kl = [sb(f"kl{i}", [P, KC, 9 * P], F32R) for i in range(2)]
        vh = [sb(f"vh{i}", [P, 9, D], F32R) for i in range(2)]
        vl = [sb(f"vl{i}", [P, 9, D], F32R) for i in range(2)]
        small = [sb(f"softmax_small{i}", [P, 4, HEADS]) for i in range(NPR)]
        pth = [sb(f"probT_h{i}", [P, 2, HEADS, P], F32R) for i in range(2)]
        ptl = [sb(f"probT_l{i}", [P, 2, HEADS, P], F32R) for i in range(2)]
        ah = [sb(f"attnT_h{i}", [P, KC, GRP * P], F32R) for i in range(2)]
        al = [sb(f"attnT_l{i}", [P, KC, GRP * P], F32R) for i in range(2)]
        oT = sb("outT", [P, KC, GRP * P])

        ps_s = ps("ps_scores", [P, 2, 2, 2 * P])
        ps_pt = ps("ps_probT", [P, 2, HEADS, P])
        ps_av = ps("ps_av", [P, KC, 2 * P])
        ps_p = [ps(f"ps_proj{i}", [P, GRP * P]) for i in range(3)]

        x_v = io["x"].rearrange("(g j p) d -> g p j d", j=GRP, p=P)
        last = {}
        xn_ready, xT_stored, qk_ready, v_ready = {}, {}, {}, {}
        xT_pair = {}

        turn = [0]

        def bank(n=None):
            turn[0] += 1
            return ps_p[turn[0] % 3], ("ps_p", turn[0] % 3)

        def order(G):
            return -1 if G == NGRP else G

        def blocks(G):
            return GRP if G < NGRP else 1

        def load_x(G):
            if G < NGRP:
                last["x", G] = c.dma(c.sync, f"x{G % 2}", x_g[G % 2][:], x_v[G], [last.get(("ln", G - 2))])

        def store_pairs(name, G, tile_of, dram, steps):
            for h in range((blocks(G) + 1) // 2):
                pair, n = 2 * G + h, min(2, blocks(G))
                out, in_ = tile_of(h, n, dram[pair])
                last[name, order(G)] = c.dma(c.sync, f"{name}{order(G) % 2}", out, in_, steps[h])

        def free_xn(o):
            return [last.get(("xn_st", o - 2)), last.get(("tx_pe", o - 2))]

        def store_xn(G, t):
            store_pairs("xn_st", G, lambda h, n, d: (d[:, 0:n, :], t[:, 2 * h:2 * h + n, :]), io["xn_d"], [xn_ready[G]] * 2)

        def take_memory():
            t = xn[order(NGRP) % 2]
            xn_ready[NGRP] = [c.dma(c.sync, "mem", t[:, 0, :], io["memp"])]
            store_xn(NGRP, t)

        def norm_stats(G, part):
            s, ld, src = G % 2, last["x", G], x_g[G % 2]
            js = range(2 * part, 2 * part + 2)
            for j in js:
                st = c.dve(lambda e, j=j: e.bn_stats(stats[s][:, j], src[:, j]), [ld, last.get(("ln_ag", G - 2))])
            for j in js:
                ag = c.dve(lambda e, j=j: e.bn_aggr(mv[s][:, j], stats[s][:, j]), [st, last.get(("ln", G - 2))])
            if part:
                last["ln_ag", G] = ag
                ve = c.dve(lambda e: e.tensor_scalar(rstd[s][:, 0], mv[s][:, :, 1], EPS, None, ALU.add), [ag, last.get(("ln_r", G - 2))])
                last["ln_r", G] = c.pool(lambda e: e.tensor_tensor(rstd[s][:, 1], rstd[s][:, 0], neg_half[:], ALU.pow),
                                         [ve, set_half, last.get(("ln", G - 2))])

        def norm_apply(G, part):
            s, t, src = G % 2, xn[G % 2], x_g[G % 2]
            for j in range(2 * part, 2 * part + 2):
                a = c.dve(lambda e, j=j: e.tensor_scalar(t[:, j], src[:, j], mv[s][:, j, 0:1], rstd[s][:, 1, j:j + 1],
                                                          ALU.subtract, ALU.mult), [last["ln_r", G]] + free_xn(G))
            if part:
                last["ln", G] = a
                xn_ready[G] = [a]
                store_xn(G, t)

        def transpose_x(G, h):
            o = order(G)
            s, n = o % 2, min(2, blocks(G))
            cols = slice(2 * h * P, (2 * h + n) * P)
            b, key = bank()
            ps_x = b[:].rearrange("p (k t) -> p k t", k=KC)

            def emit(e):
                for k in range(KC):
                    for j in range(n):
                        i = e.transpose(ps_x[:, k, j * P:(j + 1) * P], xn[s][:, 2 * h + j, k * P:(k + 1) * P], ident[:])
                return i
            t = c.pe(emit, xn_ready[G] + [ld_ident, last.get(key)])
            last["tx_pe", o] = t
            f = c.act(act_copy(xT[s][:, :, cols], ps_x[:, :, 0:n * P]), [t, last.get(("xT_st", o - 2)), last.get(("xTl", o - 2))])
            last[key] = f
            hi = c.dve(copy(xTh[s][:, :, cols], xT[s][:, :, cols]), [f, last.get(("xT_use", o - 2))])
            lo = c.pool(sub(xTl[s][:, :, cols], xT[s][:, :, cols], xTh[s][:, :, cols]), [hi, last.get(("xT_use", o - 2))])
            last["xTl", o] = lo
            xT_pair[G, h] = lo
            d = io["xT_d"][2 * G + h]
            last["xT_st", o] = c.dma(c.sync, f"xT_st{s}", d[:, :, 0:n * P], xT[s][:, :, cols], [f])

        def q_slot(G, low):
            return (ql if low else qh)[3 if G == NGRP else G % 3]

        def project_qk(G, t):
            s, n, m = order(G) % 2, blocks(G) * P, t % 2
            wh, wl = w["wq" if t < 2 else "wk"]
            lhs = [(wh[:, k, m * P:(m + 1) * P], wl[:, k, m * P:(m + 1) * P]) for k in range(KC)]
            rhs = [(xTh[s][:, k, 0:n], xTl[s][:, k, 0:n]) for k in range(KC)]
            ps_j, key = bank()
            mm = c.pe(matmul_split(ps_j[:, 0:n], lhs, rhs), [xT_pair[G, 0], xT_pair.get((G, 1)), last.get(key), ws[0], ws[1]])
            last["xT_use", order(G)] = mm
            if t < 2:
                free = [last.get(("score", g)) for g in range(GRP * (G - 3), GRP * (G - 3) + GRP)] if 3 <= G < NGRP else []
                dst = [(q_slot(G, 0)[:, m, 0:n], q_slot(G, 1)[:, m, 0:n])]
            elif G < NGRP:
                b = G // 2
                free = [last.get(("score", 8 * (b - 2) + 7))] if b >= 2 else []
                cols = slice(P + (G % 2) * GRP * P, P + (G % 2 + 1) * GRP * P)
                dst = [(kh[b % 2][:, m, cols], kl[b % 2][:, m, cols])]
            else:
                free, dst = [], [(kh[b][:, m, 0:P], kl[b][:, m, 0:P]) for b in range(2)]
            for hi_t, _ in dst:
                hi = c.act(act_copy(hi_t, ps_j[:, 0:n]), [mm] + free)
            for hi_t, lo_t in dst:
                lo = c.dve(sub(lo_t, ps_j[:, 0:n], hi_t), [hi] + free)
                qk_ready[G, t] = qk_ready.get((G, t), []) + [lo]
                last[key] = lo

        def project_v(G, h):
            s, n = order(G) % 2, min(2, blocks(G))
            wh, wl = w["wv"]
            b, key = bank()
            ps_v = b[:].rearrange("p (j d) -> p j d", j=2)

            def emit(e):
                for j in range(n):
                    cols = slice((2 * h + j) * P, (2 * h + j + 1) * P)
                    i = matmul_split(ps_v[:, j], [(xTh[s][:, k, cols], xTl[s][:, k, cols]) for k in range(KC)],
                                     [(wh[:, k], wl[:, k]) for k in range(KC)])(e)
                return i
            mm = c.pe(emit, [xT_pair[G, h], last.get(key), ws[2]])
            last["xT_use", order(G)] = mm
            if G < NGRP:
                b = G // 2
                free = [last.get(("av", 8 * (b - 2) + 7))] if b >= 2 else []
                at = 1 + (G % 2) * GRP + 2 * h
                dst = [(vh[b % 2][:, at:at + 2], vl[b % 2][:, at:at + 2])]
            else:
                free, dst = [], [(vh[b][:, 0:1], vl[b][:, 0:1]) for b in range(2)]
            for hi_t, _ in dst:
                hi = c.act(act_copy(hi_t, ps_v[:, 0:n]), [mm] + free)
            for hi_t, lo_t in dst:
                lo = c.dve(sub(lo_t, ps_v[:, 0:n], hi_t), [hi] + free)
                v_ready[G, h] = v_ready.get((G, h), []) + [lo]
                last[key] = lo

        def place(g):
            if g == NBLK:
                return (B - 1) % 2, 0, 2
            return (g // 8) % 2, g % 8, 1 if g % 8 == 0 else 0

        def scores(g):
            G, (par, i, mask) = g // GRP, place(g)
            qc, kcols = slice((g % GRP) * P, (g % GRP + 1) * P), slice(i * P, (i + 2) * P)

            def emit(e):
                for c2 in range(2):
                    for n in range(3):
                        for half in range(2):
                            r = slice(half * DH, (half + 1) * DH)
                            a = q_slot(G, n == 0)[r, c2, qc]
                            b = (kl if n == 1 else kh)[par][r, c2, kcols]
                            x = e.matmul(ps_s[:, half, c2], a, b, start=n == 0, stop=n == 2)
                return x
            need = [s for t in range(4) for s in qk_ready[G, t]]
            need += [s for t in (2, 3) for s in qk_ready[NGRP, t]]
            if g % GRP == 0 and g % 8 and g < NBLK:
                need += [s for t in (2, 3) for s in qk_ready[G - 1, t]]
            sc = c.pe(emit, need + [last.get("ps_s")])
            last["score", g] = sc
            p, sm = pr[g % NPR], small[g % NPR]
            for h in range(HEADS):
                mx = c.dve(lambda e, h=h: e.tensor_tensor_reduce(
                    out=p[:, h], in0=ps_s[:, h % 2, h // 2], in1=masks[:, mask], scale=1.0, scalar=-3.0e38,
                    op0=ALU.add, op1=ALU.max, accum_out=sm[:, 0, h:h + 1]),
                    [sc, ld_masks, ws[3], last.get(("pt_pe", g - NPR)), last.get(("exp", g - NPR))])
            last["ps_s"] = mx
            last["max", g] = mx

        def soft(g):
            p, sm = pr[g % NPR], small[g % NPR]
            nm = c.dve(lambda e: e.tensor_scalar(sm[:, 1], sm[:, 0], -1.0 / DH ** 0.5, None, ALU.mult), [last["max", g], last.get(("exp", g - NPR))])
            for h in range(HEADS):
                ex = c.act(lambda e, h=h: e.activation(p[:, h], p[:, h], ACTF.Exp, bias=sm[:, 1, h:h + 1],
                                                       scale=1.0 / DH ** 0.5, accum_out=sm[:, 2, h:h + 1]),
                           [nm, last.get(("prob", g - NPR))])
            last["exp", g] = ex

        def normalise(g):
            p, sm = pr[g % NPR], small[g % NPR]
            rc = c.dve(lambda e: e.reciprocal(sm[:, 3], sm[:, 2]), [last["exp", g], last.get(("prob", g - NPR))])
            last["prob", g] = c.pool(lambda e: e.tensor_tensor(p[:], p[:], sm[:, 3].unsqueeze(2).broadcast_to([P, HEADS, 2 * P]), ALU.mult), [rc])

        def transpose_p(g):
            p = pr[g % NPR]

            def emit(e):
                for kb in range(2):
                    for h in range(HEADS):
                        x = e.transpose(ps_pt[:, kb, h], p[:, h, kb * P:(kb + 1) * P], ident[:])
                return x
            t = c.pe(emit, [last["prob", g], last.get("ps_pt")])
            last["pt_pe", g] = t
            hi = c.act(act_copy(pth[g % 2][:], ps_pt[:]), [t, last.get(("av", g - 2))])
            lo = c.dve(sub(ptl[g % 2][:], ps_pt[:], pth[g % 2][:]), [hi, last.get(("av", g - 2))])
            last["ps_pt"] = last["pt", g] = lo

        def attend(g):
            par, i, _ = place(g)
            G = g // GRP
            cols = slice((g % GRP) * P, (g % GRP + 1) * P)

            def emit(e):
                for c2 in range(KC):
                    vc = slice(c2 * P, (c2 + 1) * P)
                    x = matmul_split(ps_av[:, c2], [(vh[par][:, i + kb, vc], vl[par][:, i + kb, vc]) for kb in range(2)],
                                     [(pth[g % 2][:, kb, 2 * c2:2 * c2 + 2], ptl[g % 2][:, kb, 2 * c2:2 * c2 + 2])
                                      for kb in range(2)])(e)
                return x
            need = [last["pt", g], last.get("ps_av")] + [s for k in v_ready if k[0] in (G, G - 1, NGRP) for s in v_ready[k]]
            av = c.pe(emit, need)
            last["av", g] = av
            for half in range(2):
                r, src = slice(half * DH, (half + 1) * DH), slice(half * P, (half + 1) * P)
                hi = c.act(act_copy(ah[G % 2][r, :, cols], ps_av[r, :, src]), [av, last.get(("wo", G - 2))])
            for half in range(2):
                r, src = slice(half * DH, (half + 1) * DH), slice(half * P, (half + 1) * P)
                lo = c.dve(sub(al[G % 2][r, :, cols], ps_av[r, :, src], ah[G % 2][r, :, cols]), [hi, last.get(("wo", G - 2))])
            last["ps_av"] = last["attn", g] = lo

        def out_project(G, m):
            n = blocks(G) * P
            wh, wl = w["wo"]
            mc = slice(m * P, (m + 1) * P)
            ps_j, key = bank()
            mm = c.pe(matmul_split(ps_j[:, 0:n], [(wh[:, k, mc], wl[:, k, mc]) for k in range(KC)],
                                   [(ah[G % 2][:, k, 0:n], al[G % 2][:, k, 0:n]) for k in range(KC)]),
                      [last["attn", 4 * G + blocks(G) - 1], last.get(key), ws[3]])
            last[key] = ev = c.act(act_copy(oT[:, m, 0:n], ps_j[:, 0:n]), [mm, last.get(("oT_st", G - 1))])
            if m == KC - 1:
                last["wo", G] = mm
                for h in range((blocks(G) + 1) // 2):
                    k = min(2, blocks(G))
                    last["oT_st", G] = c.dma(c.sync, "oT_st", io["oT_d"][2 * G + h][:, :, 0:k * P],
                                             oT[:, :, 2 * h * P:(2 * h + k) * P], [ev])

        def prep(G, n):
            if n < 2:
                if G < NGRP or n == 0:
                    transpose_x(G, n)
            elif n in (5, 7):
                if G < NGRP or n == 5:
                    project_v(G, (n - 5) // 2)
            else:
                project_qk(G, {2: 0, 3: 2, 4: 1, 6: 3}[n])

        take_memory()
        for G in range(2):
            load_x(G)
        for G in (NGRP, 0, 1):
            for n in range(8):
                prep(G, n)
                if n % 2 and G < NGRP:
                    (norm_stats if n < 4 else norm_apply)(G + 1, n // 2 % 2)
                if n < 4 and G == NGRP:
                    (norm_stats if n < 2 else norm_apply)(0, n % 2)
            load_x({NGRP: 2, 0: 3, 1: 4}[G])
        for a in range(NBLK + 6):
            G, j = a // GRP + 2, a % GRP
            if a <= NBLK:
                scores(a)
            if G < NGRP:
                prep(G, 2 * j)
            if 2 <= a <= NBLK + 2:
                transpose_p(a - 2)
            if a <= NBLK:
                soft(a)
            if 3 <= a <= NBLK + 3:
                attend(a - 3)
            if G < NGRP:
                prep(G, 2 * j + 1)
            if G + 1 < NGRP:
                (norm_stats if j < 2 else norm_apply)(G + 1, j % 2)
            if G + 3 < NGRP and j == 3:
                load_x(G + 3)
            if a <= NBLK:
                normalise(a)
            if a > 3 and j in (3, 0) and (a - j) // GRP - (1 if j else 2) >= 0 and a <= NBLK + 4:
                out_project((a - j) // GRP - (1 if j else 2), 0 if j else 1)
        for m in range(KC):
            out_project(NGRP, m)
        stores = [last["xn_st", G] for G in (NGRP - 1, NGRP - 2)]
        stores += [last["xT_st", G] for G in (NGRP - 1, NGRP - 2)] + [last["oT_st", NGRP]]
        c.sync(lambda e: e.nop(), stores)
        c.run()


def gradient_phase(c, io, g1, g2, b1n, b2n):
    nc = c.nc
    with ExitStack() as ctx:
        def sb(name, shape, dt=F32):
            return ctx.enter_context(nc.sbuf_tensor(name, shape, dt))

        def ps(name, shape, dt=F32):
            return ctx.enter_context(nc.psum_tensor(name, shape, dt))

        hf = [sb(f"h_full{i}", [P, HID]) for i in range(2)]
        qf = sb("silu_q", [P, HID])
        sp = [sb(f"silu_slope{i}", [P, HID]) for i in range(4)]
        w1h, w1l = sb("w1_h", [P, KC, HID], F32R), sb("w1_l", [P, KC, HID], F32R)
        w2Th, w2Tl = sb("w2T_h", [P, HC, D], F32R), sb("w2T_l", [P, HC, D], F32R)
        w2h, w2l = sb("w2_h", [P, KC, HID], F32R), sb("w2_l", [P, KC, HID], F32R)
        w_ready = {}
        w1_v = io["w1T"].rearrange("(c p) n -> p c n", p=P)
        w2T_v = io["w2T"].rearrange("(c p) n -> p c n", p=P)
        w2_v = io["w2"].rearrange("(c p) n -> p c n", p=P)
        stages = [(w1h[:, k], w1l[:, k], w1_v[:, k], "w1") for k in range(KC)]
        stages += [(w2Th[:, 4 * k:4 * k + 4], w2Tl[:, 4 * k:4 * k + 4], w2T_v[:, 4 * k:4 * k + 4], "w2T") for k in range(2)]
        stages += [(w2h[:, k], w2l[:, k], w2_v[:, k], "w2") for k in range(KC)]
        last = {}
        for n, (hi, lo, src, key) in enumerate(stages):
            full = sp[n % 4][:] if key != "w2T" else sp[n % 4][:].rearrange("p (a b) -> p a b", b=D)
            ld = c.dma(c.sync, f"g_w{n}", full, src, [last.get(("stage", n - 4))])
            h = c.act(act_copy(hi, full), [ld])
            last["stage", n] = w_ready[key] = c.dve(sub(lo, full, hi), [h])

        ident = sb("g_ident", [P, P])
        ld_ident = c.dma(c.sync, "g_ident", ident[:], io["ident"])
        row_scale = sb("mem_row_scale", [P, P])
        ld_scale = c.dma(c.sync, "g_scale", row_scale[:], io["mem_scale"])
        b2c = sb("b2_col", [P, KC])
        ld_b2 = c.dma(c.sync, "g_b2", b2c[:], io["b2c"])
        b1f, b1s, ones2f = qf[0:2, :], sb("b1_rows", [2, HID], F32R), sb("ones2_f", [2, P])
        b1h, b1l = hf[0][0:2, :], hf[1][0:2, :]
        ones2 = sb("ones2", [2, P], F32R)
        b1t = sb("b1_high", [2, HID], F32R)
        ld_b1 = [c.dma(c.sync, "g_b1", qf[r:r + 1, :], io["b1"].rearrange("(a n) -> a n", a=1)) for r in range(2)]
        hi = c.dve(copy(b1t[:], b1f), [ld_b1[1]])
        hs = c.dve(lambda e: e.tensor_scalar(b1h, b1t[:], ident[0:2, 0:1], None, ALU.mult), [hi, ld_ident])
        lo = c.dve(sub(b1l, b1f, b1t[:]), [hi])
        b1_ready = c.dve(lambda e: e.scalar_tensor_tensor(b1s[:], b1l, ident[0:2, 1:2], b1h, ALU.mult, ALU.add), [hs, lo])
        set1 = c.dve(lambda e: e.memset(ones2f[:], 1.0))
        ones_ready = c.dve(copy(ones2[:], ones2f[:]), [set1])

        dz_sum = sb("dz_sum", [P, HID])
        db2 = sb("db2_parts", [P, KC, NPAIR + 1])
        zero = [c.pool(lambda e, t=t: e.memset(t, 0.0)) for t in (g1[:], g2[:], dz_sum[:])]

        xn_f = [sb(f"xn_f{i}", [P, 2, D]) for i in range(2)]
        xT_f = [sb(f"xT_f{i}", [P, KC, 2 * P]) for i in range(2)]
        oT_f = [sb(f"oT_f{i}", [P, KC, 2 * P]) for i in range(2)]
        xnh = [sb(f"xn_h{i}", [P, 2, D], F32R) for i in range(2)]
        xnl = [sb(f"xn_l{i}", [P, 2, D], F32R) for i in range(2)]
        xTh = sb("g_xTh", [P, KC, 2 * P], F32R)
        xTl = sb("g_xTl", [P, KC, 2 * P], F32R)
        hh = [sb(f"h_h{i}", [P, HID], F32R) for i in range(4)]
        hl = [sb(f"h_l{i}", [P, HID], F32R) for i in range(4)]
        hTh, hTl = sb("hT_h", [P, HC, 2 * P], F32R), sb("hT_l", [P, HC, 2 * P], F32R)
        dzh = [sb(f"dz_h{i}", [P, HID], F32R) for i in range(2)]
        dzl = [sb(f"dz_l{i}", [P, HID], F32R) for i in range(2)]
        dpf = sb("dpredT", [P, KC, 2 * P])
        dTh, dTl = sb("dpredT_h", [P, KC, 2 * P], F32R), sb("dpredT_l", [P, KC, 2 * P], F32R)
        dth, dtl = sb("dpred_h", [P, 2, D], F32R), sb("dpred_l", [P, 2, D], F32R)

        banks = [ps(f"g_bank{i}", [P, 512]) for i in range(8)]
        turn = [0]

        def bank():
            turn[0] += 1
            return banks[turn[0] % 8], ("bank", turn[0] % 8)

        def n_of(p):
            return 2 if p < NPAIR else 1

        def load(p):
            n, s = n_of(p), p % 2
            last["ld", p] = [
                c.dma(c.sync, f"g_xn{s}", xn_f[s][:, 0:n], io["xn_d"][p][:, 0:n], [last.get(("xnl", p - 2))]),
                c.dma(c.sync, f"g_xT{s}", xT_f[s][:, :, 0:n * P], io["xT_d"][p][:, :, 0:n * P], [last.get(("xTl", p - 2))]),
                c.dma(c.sync, f"g_oT{s}", oT_f[s][:, :, 0:n * P], io["oT_d"][p][:, :, 0:n * P], [last.get(("dp", p - 2))])]

        def split_xT(p):
            n, s = n_of(p), p % 2
            ld = last["ld", p]
            h = c.act(act_copy(xTh[:, :, 0:n * P], xT_f[s][:, :, 0:n * P]), [ld[1], last.get(("z", p - 1))])
            last["xTl", p] = c.dve(sub(xTl[:, :, 0:n * P], xT_f[s][:, :, 0:n * P], xTh[:, :, 0:n * P]), [h, last.get(("z", p - 1))])

        def split_xn(p):
            n, s = n_of(p), p % 2
            ld = last["ld", p]
            h = c.act(act_copy(xnh[s][:, 0:n], xn_f[s][:, 0:n]), [ld[0], last.get(("gw1", p - 2))])
            last["xnl", p] = c.dve(sub(xnl[s][:, 0:n], xn_f[s][:, 0:n], xnh[s][:, 0:n]), [h, last.get(("gw1", p - 2))])

        def forward(p, b):
            g = 2 * p + b
            cols = slice(b * P, (b + 1) * P)
            t, hfull = sp[g % 4], hf[g % 2]
            free = [last.get(("hT_pe", g - 2)), last.get(("hl", g - 2)), last.get(("q", g - 2)), b1_ready]
            for half in range(2):
                hc = slice(half * 512, (half + 1) * 512)
                acc, key = bank()

                def emit(e, acc=acc, hc=hc):
                    e.matmul(acc[:], ones2[:], b1s[:, hc], start=True, stop=False)
                    return matmul_split(acc[:], [(xTh[:, k, cols], xTl[:, k, cols]) for k in range(KC)],
                                        [(w1h[:, k, hc], w1l[:, k, hc]) for k in range(KC)], first=False)(e)
                z = c.pe(emit, [last["xTl", p], w_ready["w1"], b1_ready, ones_ready, last.get(key)])
                s = c.act(lambda e, hc=hc, acc=acc: e.activation(t[:, hc], acc[:], ACTF.Sigmoid), [z, last.get(("dzs", g - 4)), w_ready["w2"]])
                last[key] = h = c.dve(lambda e, hc=hc, acc=acc: e.tensor_tensor(hfull[:, hc], acc[:], t[:, hc], ALU.mult), [s] + free)
            last["z", p] = z
            last["h", g] = h
            q = c.dve(lambda e: e.scalar_tensor_tensor(qf[:], t[:], 1.0, hfull[:], ALU.subtract, ALU.mult), [h, last.get(("sp", g - 1))])
            last["q", g] = q
            hi = c.act(act_copy(hh[g % 4][:], hfull[:]), [h, last.get(("gw2", p - 2))])
            last["sp", g] = c.pool(sub(t[:], t[:], qf[:]), [q])
            last["hl", g] = c.pool(sub(hl[g % 4][:], hfull[:], hh[g % 4][:]), [hi, last.get(("gw2", p - 2))])

        def transpose_h(p, b):
            g = 2 * p + b
            cols = slice(b * P, (b + 1) * P)
            for half in range(2):
                ks = slice(4 * half, 4 * half + 4)
                acc, key = bank()

                def emit(e, half=half, acc=acc):
                    for k in range(4):
                        i = e.transpose(acc[:, k * P:(k + 1) * P], hf[g % 2][:, (4 * half + k) * P:(4 * half + k + 1) * P], ident[:])
                    return i
                t = c.pe(emit, [last["h", g], ld_ident, last.get(key)])
                src = acc[:].rearrange("p (k t) -> p k t", k=4)
                hi = c.act(act_copy(hTh[:, ks, cols], src), [t, last.get(("pred", p - 1))])
                lo = c.dve(sub(hTl[:, ks, cols], src, hTh[:, ks, cols]), [hi, last.get(("pred", p - 1))])
                last[key] = lo
            last["hT_pe", g] = t
            last["hT", g] = lo

        def predict(p):
            n, s = n_of(p), p % 2
            N = n * P
            acc, key = bank()

            def emit(e):
                for m in range(KC):
                    mc = slice(m * P, (m + 1) * P)
                    i = matmul_split(acc[:, m * 2 * P:m * 2 * P + N], [(w2Th[:, k, mc], w2Tl[:, k, mc]) for k in range(HC)],
                                     [(hTh[:, k, 0:N], hTl[:, k, 0:N]) for k in range(HC)])(e)
                return i
            mm = c.pe(emit, [last["hT", 2 * p + n - 1], w_ready["w2T"], last.get(key)])
            last["pred", p] = mm
            free = [last.get(("dT_pe", p - 1)), last.get(("dTl", p - 1))]
            for m in range(KC):
                d = c.dve(lambda e, m=m: e.scalar_tensor_tensor(
                    dpf[:, m, 0:N], acc[:, m * 2 * P:m * 2 * P + N], b2c[:, m:m + 1], oT_f[s][:, m, 0:N],
                    ALU.add, ALU.subtract, accum_out=db2[:, m, p:p + 1]), [mm, ld_b2, last["ld", p][2]] + free)
            last[key] = last["dp", p] = d
            if p == NPAIR:
                for m in range(KC):
                    d = c.dve(lambda e, m=m: e.tensor_tensor(dpf[:, m, 0:N], dpf[:, m, 0:N], row_scale[:], ALU.mult), [d, ld_scale])
                for m in range(KC):
                    d2 = c.dve(lambda e, m=m: e.tensor_reduce(db2[:, m, p:p + 1], dpf[:, m, 0:N], AX.X, ALU.add), [d])
                last["db2"] = d2
            hi = c.act(act_copy(dTh[:, :, 0:N], dpf[:, :, 0:N]), [d, last.get(("dh", p - 1))])
            last["dTl", p] = c.dve(sub(dTl[:, :, 0:N], dpf[:, :, 0:N], dTh[:, :, 0:N]), [hi, last.get(("dh", p - 1))])
            last["dpf", p] = d

        def transpose_d(p):
            n = n_of(p)
            acc, key = bank()

            def emit(e):
                for b in range(n):
                    for m in range(KC):
                        i = e.transpose(acc[:, (2 * b + m) * P:(2 * b + m + 1) * P], dpf[:, m, b * P:(b + 1) * P], ident[:])
                return i
            t = c.pe(emit, [last["dpf", p], last.get(key)])
            last["dT_pe", p] = t
            src = acc[:, 0:n * D].rearrange("p (b d) -> p b d", b=n)
            hi = c.act(act_copy(dth[:, 0:n], src), [t, last.get(("gw2", p - 1))])
            lo = c.dve(sub(dtl[:, 0:n], src, dth[:, 0:n]), [hi, last.get(("gw2", p - 1))])
            last[key] = last["dtok", p] = lo

        def backward(p, b):
            g = 2 * p + b
            cols = slice(b * P, (b + 1) * P)
            t = sp[g % 4]
            for half in range(2):
                hc = slice(half * 512, (half + 1) * 512)
                acc, key = bank()
                mm = c.pe(matmul_split(acc[:], [(dTh[:, k, cols], dTl[:, k, cols]) for k in range(KC)],
                                       [(w2h[:, k, hc], w2l[:, k, hc]) for k in range(KC)]),
                          [last["dTl", p], w_ready["w2"], last.get(key)])
                last[key] = dz = c.dve(lambda e, hc=hc, acc=acc: e.tensor_tensor(t[:, hc], acc[:], t[:, hc], ALU.mult), [mm, last["sp", g]])
            last["dh", p] = mm
            hi = c.act(act_copy(dzh[b][:], t[:]), [dz, last.get(("gw1", p - 1))])
            last["dz", g] = c.pool(sub(dzl[b][:], t[:], dzh[b][:]), [hi, last.get(("gw1", p - 1))])
            last["dzs", g] = c.pool(add(dz_sum[:], dz_sum[:], t[:]), [dz, last.get(("dzs", g - 1)), zero[2]])

        def accumulate_w2(p, tiles):
            n = n_of(p)
            for t in tiles:
                acc, key = bank()

                def emit(e, t=t, acc=acc):
                    for u in range(2):
                        hc = slice((2 * t + u) * P, (2 * t + u + 1) * P)
                        i = matmul_split(acc[:, u * D:(u + 1) * D], [(hh[(2 * p + b) % 4][:, hc], hl[(2 * p + b) % 4][:, hc]) for b in range(n)],
                                         [(dth[:, b], dtl[:, b]) for b in range(n)])(e)
                    return i
                mm = c.pe(emit, [last["dtok", p], last["hl", 2 * p + n - 1], last.get(key)])
                dst = g2[:, 2 * t:2 * t + 2].rearrange("p a b -> p (a b)")
                last[key] = last["g2", t] = c.dve(add(dst, acc[:], dst), [mm, zero[1], last.get(("g2", t))])
            last["gw2", p] = mm

        def accumulate_w1(p, tiles):
            n, s = n_of(p), p % 2
            for t in tiles:
                k, hc = t // 2, slice((t % 2) * 512, (t % 2 + 1) * 512)
                acc, key = bank()
                mm = c.pe(matmul_split(acc[:], [(xnh[s][:, b, k * P:(k + 1) * P], xnl[s][:, b, k * P:(k + 1) * P]) for b in range(n)],
                                       [(dzh[b][:, hc], dzl[b][:, hc]) for b in range(n)]),
                          [last["dz", 2 * p + n - 1], last["xnl", p], last.get(key)])
                last[key] = last["g1", t] = c.dve(add(g1[:, k, hc], acc[:], g1[:, k, hc]), [mm, zero[0], last.get(("g1", t))])
            last["gw1", p] = mm

        pairs = NPAIR + 1
        load(0)
        load(1)
        split_xT(0)
        split_xn(0)
        for p in range(pairs + 1):
            now, both = p < pairs, p < NPAIR
            before = p >= 1
            if now:
                forward(p, 0)
            if before:
                backward(p - 1, 0)
            if both:
                forward(p, 1)
            if before and n_of(p - 1) == 2:
                backward(p - 1, 1)
            if before:
                accumulate_w2(p - 1, [0])
            if now:
                transpose_h(p, 0)
            if before:
                accumulate_w2(p - 1, [1])
            if both:
                transpose_h(p, 1)
            if p + 1 < pairs:
                split_xT(p + 1)
            if before:
                accumulate_w2(p - 1, [2, 3])
            if now:
                predict(p)
            if before:
                accumulate_w1(p - 1, [0, 1])
            if now:
                transpose_d(p)
            if before:
                accumulate_w1(p - 1, [2, 3])
            if p + 1 < pairs:
                split_xn(p + 1)
            if p + 2 < pairs:
                load(p + 2)

        rates = sb("g_rates_sb", [P, 4])
        ld_r = c.dma(c.sync, "g_rates", rates[:, 0:2], io["rates"])
        keep = c.dve(lambda e: e.tensor_scalar(rates[:, 2:3], rates[:, 0:1], -1.0, 1.0, ALU.mult, ALU.add), [ld_r])
        step = c.dve(lambda e: e.tensor_scalar(rates[:, 3:4], rates[:, 1:2], -1.0, None, ALU.mult), [ld_r])
        ones = c.dve(lambda e: e.memset(rates[:, 0:1], 1.0), [keep])
        bank1, key = bank()

        def emit(e):
            for k in range(HC):
                i = e.matmul(bank1[:, k:k + 1], dz_sum[:, k * P:(k + 1) * P], rates[:, 0:1], start=True, stop=True)
            return i
        mm = c.pe(emit, [last["dzs", 2 * NPAIR], last.get(key), ones])
        b1c = sb("b1_col", [P, HC])
        ld = c.dma(c.sync, "g_b1c", b1c[:], io["b1c"])
        a = c.dve(lambda e: e.tensor_scalar(b1c[:], b1c[:], rates[:, 2:3], None, ALU.mult), [ld, keep])
        c.dve(lambda e: e.scalar_tensor_tensor(b1n[:], bank1[:, 0:HC], rates[:, 3:4], b1c[:], ALU.mult, ALU.add), [mm, step, a])
        red = c.dve(lambda e: e.tensor_reduce(b2n[:], db2[:], AX.X, ALU.add), [last["db2"]])
        a = c.dve(lambda e: e.tensor_scalar(b2c[:], b2c[:], rates[:, 2:3], None, ALU.mult), [last["dp", NPAIR]])
        c.dve(lambda e: e.scalar_tensor_tensor(b2n[:], b2n[:], rates[:, 3:4], b2c[:], ALU.mult, ALU.add), [a, red])
        for n, (gt, view, t) in enumerate([(g1[:, k], w1_v[:, k], sp[k]) for k in range(2)]
                                          + [(g2[:, 4 * k:4 * k + 4], w2T_v[:, 4 * k:4 * k + 4], sp[2 + k]) for k in range(2)]):
            w = t[:] if n < 2 else t[:].rearrange("p (a b) -> p a b", b=D)
            ld = c.dma(c.sync, f"g_old{n}", w, view, [last["dzs", 2 * NPAIR], last["dzs", 2 * NPAIR - 1], last["dz", 2 * NPAIR], last["dz", 2 * NPAIR - 1]])
            a = c.dve(lambda e, w=w: e.tensor_scalar(w, w, rates[:, 2:3], None, ALU.mult), [ld, keep])
            done = [last["g1", t] for t in range(4)] + [last["g2", t] for t in range(4)]
            c.dve(lambda e, w=w, gt=gt: e.scalar_tensor_tensor(gt, gt, rates[:, 3:4], w, ALU.mult, ALU.add), [a, step] + done)
        c.run()


NCH = NGRP
NZ = 3
T = GRP * P
SLOTS = TOPK * NSLOT
OUTSIDE = 65536.0


def merge_phase(c, io, g1, g2, b1n, b2n, route, weight):
    nc = c.nc
    with ExitStack() as ctx:
        def sb(name, shape, dt=F32):
            return ctx.enter_context(nc.sbuf_tensor(name, shape, dt))

        def ps(name, shape, dt=F32):
            return ctx.enter_context(nc.psum_tensor(name, shape, dt))

        last = {}
        w1h, w1l = sb("m_w1_h", [P, KC, HID], F32R), sb("m_w1_l", [P, KC, HID], F32R)
        w2h, w2l = sb("m_w2_h", [P, HC, D], F32R), sb("m_w2_l", [P, HC, D], F32R)
        for k in range(KC):
            hi = c.act(act_copy(w1h[:, k], g1[:, k]))
            w1_ready = c.dve(sub(w1l[:, k], g1[:, k], w1h[:, k]), [hi])
        for k in range(2):
            r = slice(4 * k, 4 * k + 4)
            hi = c.act(act_copy(w2h[:, r], g2[:, r]))
            w2_ready = c.dve(sub(w2l[:, r], g2[:, r], w2h[:, r]), [hi])
        lin, lin_ready = {}, {}
        lin_f = [sb(f"lin_f{i}", [P, KC, D]) for i in range(2)]
        for n, k in enumerate(("lin1", "lin2")):
            lin[k] = sb(k + "_h", [P, KC, D], F32R), sb(k + "_l", [P, KC, D], F32R)
            ld = c.dma(c.sync, k, lin_f[n][:], io[k + "T"].rearrange("(c p) n -> p c n", p=P))
            hi = c.act(act_copy(lin[k][0][:], lin_f[n][:]), [ld])
            lin_ready[k] = c.dve(sub(lin[k][1][:], lin_f[n][:], lin[k][0][:]), [hi])
        gate = sb("gate_w", [P, KC, E])
        ld_gate = c.dma(c.sync, "gate_w", gate[:], io["gateT"].rearrange("(c p) n -> p c n", p=P))
        gate_b = sb("gate_bias", [P, E])
        ld_gb = c.dma(c.sync, "gate_b", gate_b[:], io["gate_b"])
        ident, before_f = sb("m_ident", [P, P]), sb("m_before_f", [P, P])
        before, ones = sb("m_before", [P, P], BF16), sb("m_ones", [P, P], BF16)
        ld_ident = c.dma(c.sync, "m_ident", ident[:], io["ident"])
        ld_before = c.dma(c.sync, "m_before", before_f[:], io["before"])
        before_ready = c.dve(copy(before[:], before_f[:]), [ld_before])
        set_ones = c.pool(lambda e: e.memset(ones[:], 1.0))
        experts = sb("expert_ids", [P, E])
        ld_exp = c.dma(c.sync, "m_experts", experts[:], io["experts"])
        neg_half = sb("m_neg_half", [P, GRP])
        set_half = c.pool(lambda e: e.memset(neg_half[:], -0.5))
        counts = sb("expert_counts", [P, TOPK, E])
        set_counts = c.pool(lambda e: e.memset(counts[:], 0.0))

        zeros = sb("zeros", [P, 1024])
        set_zero = c.pool(lambda e: e.memset(zeros[:], 0.0))
        rows = SLOTS // P * D // 1024
        xbuf_rows = io["xbuf_d"].rearrange("(p a) d -> p (a d)", p=P)

        xT_f = [sb(f"m_xT{i}", [P, KC, T]) for i in range(2)]
        oT = [sb(f"m_oT{i}", [P, KC, T]) for i in range(2)]
        x_t = [sb(f"m_x{i}", [P, GRP, D]) for i in range(2)]
        xTh, xTl = sb("m_xTh", [P, KC, T], F32R), sb("m_xTl", [P, KC, T], F32R)
        oTh, oTl = sb("m_oTh", [P, KC, T], F32R), sb("m_oTl", [P, KC, T], F32R)
        st = [sb(f"m_sig{i}", [P, T]) for i in range(NZ)]
        hf = [sb(f"m_hf{i}", [P, T]) for i in range(NZ)]
        hh, hl = sb("m_hh", [P, HC, T], F32R), sb("m_hl", [P, HC, T], F32R)
        om, omh, oml = sb("memT", [P, KC, T]), sb("memT_h", [P, KC, T], F32R), sb("memT_l", [P, KC, T], F32R)
        ga, gb = sb("gate1", [P, KC, T]), sb("gate2", [P, KC, T])
        x1 = [sb(f"x1_{i}", [P, GRP, D]) for i in range(2)]
        x2 = [sb(f"xn2_{i}", [P, GRP, D]) for i in range(3)]
        x2T = sb("xn2T", [P, KC, T])
        stats, mv, rstd = sb("m_stats", [P, GRP, 6]), sb("m_mv", [P, GRP, 2]), sb("m_rstd", [P, 2, GRP])
        lg = sb("logits", [P, GRP, E])
        pr = sb("router_probs", [P, GRP, E])
        mx, sm = sb("router_max", [P, GRP]), sb("router_sum", [P, 2, GRP])
        top = sb("router_top", [P, GRP, 8])
        idx = sb("router_idx", [P, GRP, 8], mybir.dt.uint32)
        idf = sb("router_idf", [P, TOPK, GRP])
        hot = sb("router_hot", [P, TOPK, GRP, E], BF16)
        pos_e, pos = sb("router_pos_e", [P, TOPK, GRP, E]), sb("router_pos", [P, TOPK, GRP])
        keep = sb("router_keep", [P, TOPK, GRP])
        slot, slot2 = sb("router_slot", [P, TOPK, GRP]), sb("router_slot2", [P, TOPK, GRP])
        sidx = [sb(f"scatter_rows{i}", [P, TOPK, GRP], I32) for i in range(2)]

        ps_z = [ps(f"m_ps_z{i}", [P, T]) for i in range(NZ)]
        ps_o = [ps(f"m_ps_o{i}", [P, T]) for i in range(2)]
        ps_r = ps("m_ps_r", [P, GRP, D])
        ps_s = ps("m_ps_s", [P, 512])
        ps_l, ps_c = ps_s[:, 0:GRP * E], ps_s[:, GRP * E:]
        x_v = io["x"].rearrange("(g j p) d -> g p j d", j=GRP, p=P)
        x1_v = io["x1_d"].rearrange("(g j p) d -> g p j d", j=GRP, p=P)
        turn = [0]

        def load_xT(C):
            for h in range(2):
                t = slice(2 * h * P, (2 * h + 2) * P)
                last["ld_xT", C] = c.dma(c.sync, f"m_xT{C % 2}", xT_f[C % 2][:, :, t], io["xT_d"][2 * C + h], [last.get(("xTl", C - 2))])

        def load_oT(C):
            s = C % 2
            for h in range(2):
                t = slice(2 * h * P, (2 * h + 2) * P)
                last["ld_oT", C] = c.dma(c.sync, f"m_oT{s}", oT[s][:, :, t], io["oT_d"][2 * C + h], [last.get(("merge", C - 2))])

        def load_x(C):
            s = C % 2
            last["ld_x", C] = c.dma(c.sync, f"m_x{s}", x_t[s][:], x_v[C], [last.get(("x1", C - 2))])

        def split_xT(C):
            s = C % 2
            h = c.act(act_copy(xTh[:], xT_f[s][:]), [last["ld_xT", C], last.get(("z", C - 1))])
            last["xTl", C] = c.dve(sub(xTl[:], xT_f[s][:], xTh[:]), [h, last.get(("z", C - 1))])

        def split_oT(C):
            s = C % 2
            h = c.act(act_copy(oTh[:], oT[s][:]), [last["ld_oT", C], last.get(("g1", C - 1))])
            last["oTl", C] = c.dve(sub(oTl[:], oT[s][:], oTh[:]), [h, last.get(("g1", C - 1))])

        def hidden(C, t):
            r, mc = (HC * C + t) % NZ, slice(t * P, (t + 1) * P)
            acc, key = ps_z[r], ("ps_z", r)
            z = c.pe(matmul_split(acc[:], [(w1h[:, k, mc], w1l[:, k, mc]) for k in range(KC)],
                                  [(xTh[:, k], xTl[:, k]) for k in range(KC)]), [last["xTl", C], w1_ready, last.get(key)])
            last["z", C] = z
            s = c.act(lambda e: e.activation(st[r][:], acc[:], ACTF.Sigmoid, bias=b1n[:, t:t + 1]), [z, last.get(("hf", r))])
            h = c.dve(lambda e: e.scalar_tensor_tensor(hf[r][:], acc[:], b1n[:, t:t + 1], st[r][:], ALU.add, ALU.mult),
                      [s, last.get(("hl", r))])
            last[key] = last["hf", r] = last["h", C, t] = h

        def split_hidden(C, t):
            r = (HC * C + t) % NZ
            h = last["h", C, t]
            hi = c.act(act_copy(hh[:, t], hf[r][:]), [h, last.get(("om", C - 1))])
            last["hl", r] = last["hl", C, t] = (c.dve if t % 4 == 3 else c.pool)(sub(hl[:, t], hf[r][:], hh[:, t]), [hi, last.get(("om", C - 1))])

        def bank():
            turn[0] += 1
            return ps_o[turn[0] % 2], ("ps_o", turn[0] % 2)

        def linear_gate(C, name, dst, high, low, ready, free):
            wh, wl = lin[name]
            for m in range(KC):
                acc, key = bank()
                mc = slice(m * P, (m + 1) * P)
                mm = c.pe(matmul_split(acc[:], [(wh[:, k, mc], wl[:, k, mc]) for k in range(KC)],
                                       [(high[:, k], low[:, k]) for k in range(KC)]), [ready, lin_ready[name], last.get(key)])
                last[key] = a = c.act(lambda e, m=m, acc=acc: e.activation(dst[:, m], acc[:], ACTF.Sigmoid), [mm] + free)
            return mm, a

        def memory_out(C, m, half):
            if half == 0:
                last["acc", m] = bank()
            acc, key = last["acc", m]
            mc, ks = slice(m * P, (m + 1) * P), range(4 * half, 4 * half + 4)
            mm = c.pe(matmul_split(acc[:], [(w2h[:, k, mc], w2l[:, k, mc]) for k in ks],
                                   [(hh[:, k], hl[:, k]) for k in ks], first=half == 0, last=half == 1),
                      [last["hl", C, k] for k in ks] + [w2_ready, last.get(key)])
            last["om", C] = mm
            if half:
                f = c.act(lambda e: e.activation(om[:, m], acc[:], ACTF.Identity, bias=b2n[:, m:m + 1]),
                          [mm, last.get(("merge_om", C - 1)), last.get(("oml", C - 1, m))])
                hi = c.act(lambda e: e.activation(omh[:, m], acc[:], ACTF.Identity, bias=b2n[:, m:m + 1]), [mm, last.get(("g2", C - 1))])
                last[key] = hi
                last["oml", C, m] = c.dve(sub(oml[:, m], om[:, m], omh[:, m]), [f, hi, last.get(("g2", C - 1))])

        def gate1(C):
            mm, last["ga", C] = linear_gate(C, "lin1", ga, oTh, oTl, last["oTl", C], [last.get(("merge", C - 1)), last.get(("mergeT", C - 1))])
            last["g1", C] = mm

        def gate2(C):
            mm, g = linear_gate(C, "lin2", gb, omh, oml, last["oml", C, 1], [last.get(("merge", C - 1))])
            last["g2", C] = mm
            s = C % 2
            a = c.dve(lambda e: e.tensor_tensor(ga[:], ga[:], oT[s][:], ALU.mult), [last["ga", C]])
            last["merge_om", C] = b = c.dve(lambda e: e.tensor_tensor(gb[:], gb[:], om[:], ALU.mult), [g, last["oml", C, 0]])
            last["merge", C] = c.dve(add(ga[:], ga[:], gb[:]), [a, b])

        def residual(C):
            def emit(e):
                for j in range(GRP):
                    for m in range(KC):
                        i = e.transpose(ps_r[:, j, m * P:(m + 1) * P], ga[:, m, j * P:(j + 1) * P], ident[:])
                return i
            t = c.pe(emit, [last["merge", C], ld_ident, last.get("ps_r")])
            last["mergeT", C] = t
            y = x1[C % 2]
            a = c.dve(add(y[:], ps_r[:], x_t[C % 2][:]), [t, last["ld_x", C], last.get(("x1_st", C - 2)), last.get(("ln2", C - 2))])
            last["ps_r"] = last["x1", C] = a
            last["x1_st", C] = c.dma(c.sync, f"x1_st{C % 2}", x1_v[C], y[:], [a])

        def norm_stats(C):
            y, a = x1[C % 2], last["x1", C]
            for j in range(GRP):
                b = c.dve(lambda e, j=j: e.bn_stats(stats[:, j], y[:, j]), [a, last.get("mv")])
            for j in range(GRP):
                g = c.dve(lambda e, j=j: e.bn_aggr(mv[:, j], stats[:, j]), [b, last.get(("ln2", C - 1))])
            last["mv"] = g
            v = c.dve(lambda e: e.tensor_scalar(rstd[:, 0], mv[:, :, 1], EPS, None, ALU.add), [g, last.get("rstd")])
            r = c.pool(lambda e: e.tensor_tensor(rstd[:, 1], rstd[:, 0], neg_half[:], ALU.pow), [v, set_half, last.get(("ln2", C - 1))])
            last["rstd"] = r

        def norm_apply(C):
            y, z, r = x1[C % 2], x2[C % 3], last["rstd"]
            for j in range(GRP):
                n = c.dve(lambda e, j=j: e.tensor_scalar(z[:, j], y[:, j], mv[:, j, 0:1], rstd[:, 1, j:j + 1], ALU.subtract, ALU.mult),
                          [r] + last.get(("scatter", C - 3), []))
            last["ln2", C] = n

        def transpose_x2(C):
            z = x2[C % 3]

            def emit(e):
                for m in range(KC):
                    for j in range(GRP):
                        i = e.transpose(ps_r[:, 2 * m + j // 2, (j % 2) * P:(j % 2 + 1) * P], z[:, j, m * P:(m + 1) * P], ident[:])
                return i
            t = c.pe(emit, [last["ln2", C], last.get("ps_r")])
            last["x2T", C] = last["ps_r"] = c.act(act_copy(x2T[:].rearrange("p m t -> p (m t)"), ps_r[:].rearrange("p a b -> p (a b)")),
                                                  [t, last.get(("logits", C - 1))])

        def router(C):
            def emit(e):
                for j in range(GRP):
                    for k in range(KC):
                        i = e.matmul(ps_l[:, j * E:(j + 1) * E], x2T[:, k, j * P:(j + 1) * P], gate[:, k], start=k == 0, stop=k == KC - 1)
                return i
            mm = c.pe(emit, [last["x2T", C], ld_gate, last.get("ps_s")])
            last["logits", C] = mm
            wide = [P, GRP, E]
            src = ps_l.rearrange("p (j x) -> p j x", x=E)
            a = c.dve(add(lg[:], src, gate_b[:].unsqueeze(1).broadcast_to(wide)), [mm, ld_gb, last.get("sh")])
            last["ps_s"] = a
            m = c.dve(lambda e: e.tensor_reduce(mx[:], lg[:], AX.X, ALU.max), [a, last.get("sh")])
            s = c.dve(sub(lg[:], lg[:], mx[:].unsqueeze(2).broadcast_to(wide)), [m, last.get("ex")])
            last["sh"] = s
            x = c.act(lambda e: e.activation(pr[:], lg[:], ACTF.Exp), [s, last.get("find")])
            last["ex"] = x

        def choose(C):
            wide, x = [P, GRP, E], last["ex"]
            r = c.dve(lambda e: e.tensor_reduce(sm[:, 0], pr[:], AX.X, ALU.add), [x, last.get("probs")])
            r = c.dve(lambda e: e.reciprocal(sm[:, 1], sm[:, 0]), [r])
            q = c.dve(lambda e: e.tensor_tensor(pr[:], pr[:], sm[:, 1].unsqueeze(2).broadcast_to(wide), ALU.mult), [r])
            last["probs"] = q
            for j in range(GRP):
                t = c.dve(lambda e, j=j: e.max(top[:, j], pr[:, j]), [q, last.get("weights")])
            for j in range(GRP):
                f = c.dve(lambda e, j=j: e.max_index(idx[:, j], top[:, j], pr[:, j]), [t, last.get("idf")])
            last["find"] = f
            d = c.dve(copy(idf[:], idx[:, :, 0:TOPK].rearrange("p j k -> p k j")), [f, last.get("slots")])
            last["idf"] = d
            for k in range(TOPK):
                o = c.dve(lambda e, k=k: e.tensor_tensor(hot[:, k], experts[:].unsqueeze(1).broadcast_to(wide),
                                                         idf[:, k].unsqueeze(2).broadcast_to(wide), ALU.is_equal),
                          [d, ld_exp, last.get("pos_e"), last.get("count_pe")])
            last["hot", C] = o

        def dispatch(C):
            n = TOPK * E

            def emit(e):
                for j in range(GRP + 1):
                    out = ps_c[:, j * n:(j + 1) * n].rearrange("p (k x) -> p k x", x=E)
                    for i in range(min(j, GRP - 1) + 1):
                        lhs = before if i == j else ones
                        x = e.matmul(out, lhs[:], hot[:, :, i], start=i == 0, stop=i == min(j, GRP - 1))
                return x
            mm = c.pe(emit, [last["hot", C], before_ready, set_ones, last.get("ps_s")])
            last["count_pe"] = mm
            wide = [P, GRP, E]
            for k in range(TOPK):
                src = ps_c[:, 0:GRP * n].rearrange("p (j k x) -> p j k x", k=TOPK, x=E)[:, :, k]
                a = c.dve(add(pos_e[:, k], src, counts[:, k].unsqueeze(1).broadcast_to(wide)), [mm, set_counts, last.get("counts"), last.get("pos")])
            cn = c.dve(add(counts[:], counts[:], ps_c[:, GRP * n:(GRP + 1) * n].rearrange("p (k x) -> p k x", x=E)), [a, mm])
            last["ps_s"] = last["counts"] = cn
            b = c.dve(lambda e: e.tensor_tensor(pos_e[:], pos_e[:], hot[:], ALU.mult), [a])
            last["pos_e"] = b
            p = c.dve(lambda e: e.tensor_reduce(pos[:], pos_e[:], AX.X, ALU.add), [b, last.get("slots")])
            last["pos"] = p
            k1 = c.dve(lambda e: e.tensor_scalar(keep[:], pos[:], float(CAP), None, ALU.is_lt), [p, last.get("slots")])
            cols = slice(C * GRP, (C + 1) * GRP)
            s = c.dve(lambda e: e.scalar_tensor_tensor(slot[:], idf[:], float(CAP), pos[:], ALU.mult, ALU.add), [p, last.get("slots")])
            s = c.dve(lambda e: e.tensor_scalar(slot[:, 1], slot[:, 1], float(NSLOT), None, ALU.add), [s])
            u = c.dve(lambda e: e.tensor_scalar(slot2[:], keep[:], -OUTSIDE, OUTSIDE, ALU.mult, ALU.add), [k1, last.get("slots")])
            sc = c.dve(add(sidx[C % 2][:], slot[:], slot2[:]), [s, u] + last.get(("scatter", C - 2), []))
            ends = [float(NSLOT * (k + 1) - 1) for k in range(TOPK)]
            for k in range(TOPK):
                v = c.dve(lambda e, k=k: e.tensor_scalar(slot[:, k], slot[:, k], -ends[k], None, ALU.add), [sc])
            v = c.dve(lambda e: e.tensor_tensor(slot[:], slot[:], keep[:], ALU.mult), [v])
            v2 = c.dve(lambda e: e.tensor_scalar(route[:, :, cols], slot[:], float(NSLOT - 1), None, ALU.add), [v])
            w = c.dve(lambda e: e.tensor_tensor(weight[:, :, cols], top[:, :, 0:TOPK].rearrange("p j k -> p k j"), keep[:], ALU.mult), [k1])
            last["weights"] = last["slots"] = w
            last["route"] = v2
            last["sidx", C] = sc

        def scatter(C):
            steps = []
            for k in range(TOPK):
                for j in range(GRP):
                    sem = c.sem(f"dma_scatter{C % 3}", dma=True)
                    sem.count += 16
                    after = [last["sidx", C], last["ln2", C]] + zero_done
                    st_ = Step(c.pool, lambda e, k=k, j=j: e.indirect_dma_start(
                        io["xbuf_d"], bass.IndirectOffsetOnAxis(ap=sidx[C % 2][:, k, j:j + 1], axis=0), x2[C % 3][:, j], None,
                        bounds_check=SLOTS - 1, oob_is_err=False), after, sem, sem.count)
                    for a_ in st_.after:
                        a_.awaited = True
                    c.pool.steps.append(st_)
                    steps.append(st_)
            last["scatter", C] = steps[-1:]

        load_xT(0)
        load_oT(0)
        load_x(0)
        zero_done = []
        for n in range(rows):
            zero_done.append(c.dma(c.act, "zero", xbuf_rows[:, n * 1024:(n + 1) * 1024], zeros[:], [set_zero]))
        zero_done = zero_done[-1:]
        load_xT(1)
        split_xT(0)
        split_oT(0)
        for C in range(NCH + 2):
            now, tail, sent = C < NCH, 1 <= C <= NCH, C >= 2
            if now:
                hidden(C, 0)
                hidden(C, 1)
                split_hidden(C, 0)
            if tail:
                gate2(C - 1)
            if C + 1 < NCH:
                load_oT(C + 1)
            if now:
                hidden(C, 2)
                split_hidden(C, 1)
            if sent:
                choose(C - 2)
            for t in (3, 4, 5):
                if now:
                    hidden(C, t)
                    split_hidden(C, t - 1)
            if sent:
                dispatch(C - 2)
            if tail:
                residual(C - 1)
            if C + 1 < NCH:
                load_x(C + 1)
            if now:
                hidden(C, 6)
                split_hidden(C, 5)
            if tail:
                norm_stats(C - 1)
            if now:
                hidden(C, 7)
                split_hidden(C, 6)
                gate1(C)
                split_hidden(C, 7)
            if tail:
                norm_apply(C - 1)
            if sent:
                scatter(C - 2)
            if C + 1 < NCH:
                split_xT(C + 1)
            if now:
                memory_out(C, 0, 0)
                memory_out(C, 0, 1)
            if C + 1 < NCH:
                split_oT(C + 1)
            if tail:
                transpose_x2(C - 1)
            if now:
                memory_out(C, 1, 0)
            if tail:
                router(C - 1)
            if now:
                memory_out(C, 1, 1)
            if C + 2 < NCH:
                load_xT(C + 2)
        ends = [last["x1_st", C] for C in (NCH - 1, NCH - 2)]
        for C in range(NCH - 3, NCH):
            ends += last["scatter", C][-1:]
        c.sync(lambda e: e.nop(), ends)
        c.run()


SB = CAP // P
HALF = CAP // 2


def expert_phase(c, io, route, weight):
    nc = c.nc
    with ExitStack() as ctx:
        def sb(name, shape, dt=F32):
            return ctx.enter_context(nc.sbuf_tensor(name, shape, dt))

        def ps(name, shape, dt=F32):
            return ctx.enter_context(nc.psum_tensor(name, shape, dt))

        last = {}
        ident = sb("e_ident", [P, P])
        ld_ident = c.dma(c.sync, "e_ident", ident[:], io["ident"])
        b1, b2 = sb("e_b1", [P, E, HC]), sb("e_b2", [P, E, KC])
        ld_b1 = c.dma(c.sync, "e_b1", b1[:], io["eb1"])
        ld_b2 = c.dma(c.sync, "e_b2", b2[:], io["eb2"])
        acc = sb("acc", [P, NBLK, D])
        s1, s2 = sb("e_w1_f", [P, KC, HID]), sb("e_w2_f", [P, HC, D])
        w1h, w1l = sb("e_w1_h", [P, KC, HID], F32R), sb("e_w1_l", [P, KC, HID], F32R)
        w2h, w2l = sb("e_w2_h", [P, HC, D], F32R), sb("e_w2_l", [P, HC, D], F32R)
        xs = [sb(f"slots{i}", [P, SB, D]) for i in range(2)]
        xh, xl = sb("slotsT_h", [P, KC, CAP], F32R), sb("slotsT_l", [P, KC, CAP], F32R)
        hf = [sb(f"e_hf{i}", [P, CAP]) for i in range(2)]
        hh, hl = sb("e_hh", [P, HC, CAP], F32R), sb("e_hl", [P, HC, CAP], F32R)
        yT = sb("e_yT", [P, KC, CAP])
        ys = sb("e_ys", [P, SB, D])
        yg = [sb(f"gathered{i}", [P, D]) for i in range(4)]
        ps_z = [ps(f"e_ps_z{i}", [P, 2, 512]) for i in range(2)]
        ps_x = ps("e_ps_x", [P, 4 * D])
        ps_t = ps("e_ps_t", [P, 4, D])
        x_v = io["xbuf_d"].rearrange("(i b p) d -> i p b d", b=SB, p=P)
        y_v = [io[f"ybuf{k}_d"].rearrange("(i b p) d -> i p b d", b=SB, p=P) for k in range(TOPK)]
        N = TOPK * E

        def load_slots(i):
            last["xs", i] = c.dma(c.sync, f"slots{i % 2}", xs[i % 2][:], x_v[i], [last.get(("xT_pe", i - 2))])

        def load_w(i):
            e = i % E
            last["ld_w1", i] = c.dma(c.sync, "e_w1", s1[:], io["W1"][e].rearrange("(c p) n -> p c n", p=P), [last.get(("w1", i - 1))])
            last["ld_w2", i] = c.dma(c.sync, "e_w2", s2[:], io["W2"][e].rearrange("(c p) n -> p c n", p=P), [last.get(("w2", i - 1))])

        def split_w1(i):
            for k in range(KC):
                hi = c.act(act_copy(w1h[:, k], s1[:, k]), [last["ld_w1", i], last.get(("h", i - 1))])
                last["w1", i] = c.pool(sub(w1l[:, k], s1[:, k], w1h[:, k]), [hi, last.get(("h", i - 1))])

        def split_w2(i):
            for k in range(2):
                r = slice(4 * k, 4 * k + 4)
                hi = c.dve(copy(w2h[:, r], s2[:, r]), [last["ld_w2", i], last.get(("y", i - 1))])
                last["w2", i] = c.dve(sub(w2l[:, r], s2[:, r], w2h[:, r]), [hi, last.get(("y", i - 1))])

        def transpose_slots(i, blocks):
            n = len(blocks)

            def emit(e):
                for m in range(KC):
                    for a, b in enumerate(blocks):
                        x = e.transpose(ps_x[:, (m * n + a) * P:(m * n + a + 1) * P], xs[i % 2][:, b, m * P:(m + 1) * P], ident[:])
                return x
            t = c.pe(emit, [last["xs", i], ld_ident, last.get("ps_x")])
            last["xT_pe", i] = t
            cols = slice(blocks[0] * P, (blocks[-1] + 1) * P)
            src = ps_x[:, 0:KC * n * P].rearrange("p (m t) -> p m t", m=KC)
            hi = c.act(act_copy(xh[:, :, cols], src), [t, last.get(("h", i - 1))])
            last["ps_x"] = last["xT", i] = c.dve(sub(xl[:, :, cols], src, xh[:, :, cols]), [hi, last.get(("h", i - 1))])

        turn = [0]

        def bank():
            turn[0] += 1
            return ps_z[turn[0] % 2], ("ps_z", turn[0] % 2)

        def product(out, lhs, rhs, after):
            def emit(e):
                for s in range(2):
                    cols = slice(s * HALF, (s + 1) * HALF)
                    x = matmul_split(out[:, s, 0:HALF], lhs, [(h[:, cols], l[:, cols]) for h, l in rhs])(e)
                return x
            return c.pe(emit, after)

        def up(i, t):
            e_, mc, (out, key), r = i % E, slice(t * P, (t + 1) * P), bank(), t % 2
            mm = product(out, [(w1h[:, k, mc], w1l[:, k, mc]) for k in range(KC)],
                         [(xh[:, k], xl[:, k]) for k in range(KC)], [last["xT", i], last["w1", i], last.get(key)])
            last["h", i] = mm
            src, bias = out[:, :, 0:HALF], b1[:, e_, t:t + 1]
            two = lambda ap: ap.rearrange("p (s n) -> p s n", s=2)
            hi = c.act(lambda e: e.activation(two(hh[:, t]), src, ACTF.Relu, bias=bias), [mm, ld_b1, last.get(("y", i - 1))])
            f = c.dve(lambda e: e.tensor_scalar(two(hf[r][:]), src, bias, 0.0, ALU.add, ALU.max), [hi, last.get(("hl", r))])
            last[key] = f
            last["hl", r] = c.pool(sub(hl[:, t], hf[r][:], hh[:, t]), [f, last.get(("y", i - 1))])

        def down(i, m):
            mc, (out, key) = slice(m * P, (m + 1) * P), bank()
            mm = product(out, [(w2h[:, k, mc], w2l[:, k, mc]) for k in range(HC)],
                         [(hh[:, k], hl[:, k]) for k in range(HC)], [last["hl", 0], last["hl", 1], last["w2", i], last.get(key)])
            last["y", i] = mm
            last[key] = last["yT", i] = c.act(
                lambda e: e.activation(yT[:, m].rearrange("p (s n) -> p s n", s=2), out[:, :, 0:HALF], ACTF.Identity, bias=b2[:, i % E, m:m + 1]),
                [mm, ld_b2, last.get(("yT_pe", i - 1))])

        def transpose_y(i, blocks):
            def emit(e):
                for a, b in enumerate(blocks):
                    for m in range(KC):
                        x = e.transpose(ps_t[:, a, m * P:(m + 1) * P], yT[:, m, b * P:(b + 1) * P], ident[:])
                return x
            t = c.pe(emit, [last["yT", i], last.get("ps_t")])
            last["yT_pe", i] = t
            n = len(blocks)
            d = c.dve(copy(ys[:, blocks[0]:blocks[0] + n], ps_t[:, 0:n]), [t, last.get(("ys_st", i - 1))])
            last["ps_t"] = d
            return d

        def store_y(i, d):
            last["ys_st", i] = c.dma(c.sync, "ys_st", y_v[i // E][i % E], ys[:], [d])

        def combine(k, g):
            n = k * NBLK + g
            sem = c.sem(f"dma_gather{n % 4}", dma=True)
            sem.count += 16
            st = Step(c.pool, lambda e: e.indirect_dma_start(
                yg[n % 4][:], None, io[f"ybuf{k}_d"], bass.IndirectOffsetOnAxis(ap=route[:, k, g:g + 1], axis=0),
                bounds_check=NSLOT - 1, oob_is_err=False),
                [last["ys_st", k * E + E - 1], last.get(("yg", n % 4))], sem, sem.count)
            for a in st.after:
                a.awaited = True
            c.pool.steps.append(st)
            last["yg", n % 4] = last["acc", g] = c.dve(lambda e: e.scalar_tensor_tensor(
                acc[:, g], yg[n % 4][:], weight[:, k, g:g + 1], acc[:, g], ALU.mult, ALU.add), [st, ld_acc, last.get(("acc", g))])

        load_w(0)
        load_slots(0)
        load_slots(1)
        acc_v = io["x1_d"].rearrange("(g p) d -> p g d", p=P)
        for q in range(4):
            ld_acc = c.dma(c.act, "acc", acc[:, 16 * q:16 * q + 16], acc_v[:, 16 * q:16 * q + 16])
        split_w1(0)
        split_w2(0)
        transpose_slots(0, [0, 1, 2, 3])
        transpose_slots(0, [4])
        load_w(1)
        gathers = [(0, g) for g in range(NBLK)]
        per = -(-NBLK // (E - 1))
        for i in range(N):
            for t in range(HC):
                up(i, t)
                if t == 2 and i:
                    d = transpose_y(i - 1, [0, 1, 2, 3])
                if t == 5 and i:
                    d = transpose_y(i - 1, [4])
                    store_y(i - 1, d)
            if i + 1 < N:
                split_w1(i + 1)
            if i > E:
                for k, g in gathers[:per]:
                    combine(k, g)
                del gathers[:per]
            down(i, 0)
            if i + 1 < N:
                transpose_slots(i + 1, [0, 1, 2, 3])
            down(i, 1)
            if i + 1 < N:
                transpose_slots(i + 1, [4])
                split_w2(i + 1)
            if i + 2 < N:
                load_w(i + 2)
                load_slots(i + 2)
        transpose_y(N - 1, [0, 1, 2, 3])
        store_y(N - 1, transpose_y(N - 1, [4]))
        out_v = io["out"].rearrange("(g p) d -> p g d", p=P)
        done = []
        for g in range(NBLK):
            combine(1, g)
            if g % GRP == GRP - 1:
                done.append(c.dma(c.sync, "out", out_v[:, g - GRP + 1:g + 1], acc[:, g - GRP + 1:g + 1], [last["acc", g]]))
        c.sync(lambda e: e.nop(), done[-1:] + [last["ys_st", N - 1]])
        c.run()


def build(nc, io):
    io["xn_d"] = nc.dram_tensor("xn_d", [NPAIR + 1, P, 2, D], F32).ap()
    io["xT_d"] = nc.dram_tensor("xT_d", [NPAIR + 1, P, KC, 2 * P], F32).ap()
    io["oT_d"] = nc.dram_tensor("oT_d", [NPAIR + 1, P, KC, 2 * P], F32).ap()
    io["x1_d"] = nc.dram_tensor("x1_d", [NT, D], F32).ap()
    io["xbuf_d"] = nc.dram_tensor("xbuf_d", [TOPK * NSLOT, D], F32).ap()
    for k in range(TOPK):
        io[f"ybuf{k}_d"] = nc.dram_tensor(f"ybuf{k}_d", [NSLOT, D], F32).ap()
    with ExitStack() as ctx:
        def sb(name, shape, dt=F32):
            return ctx.enter_context(nc.sbuf_tensor(name, shape, dt))

        c = Core(nc, ctx)
        attention_phase(c, io)
        route, weight = sb("route", [P, TOPK, NBLK], I32), sb("route_weight", [P, TOPK, NBLK])
        with ExitStack() as weights:
            g1 = weights.enter_context(nc.sbuf_tensor("new_w1T", [P, KC, HID], F32))
            g2 = weights.enter_context(nc.sbuf_tensor("new_w2T", [P, HC, D], F32))
            b1n = weights.enter_context(nc.sbuf_tensor("new_b1", [P, HC], F32))
            b2n = weights.enter_context(nc.sbuf_tensor("new_b2", [P, KC], F32))
            gradient_phase(c, io, g1, g2, b1n, b2n)
            merge_phase(c, io, g1, g2, b1n, b2n, route, weight)
        expert_phase(c, io, route, weight)


def window_masks():
    q, k = np.arange(P)[:, None], np.arange(P)[None]
    masks = np.full((3, P, 2 * P), -1e30, np.float32)
    masks[0, :, :P][k > q] = 0
    masks[0, :, P:][k <= q] = 0
    masks[1] = masks[0]
    masks[1, :, :P - NMEM] = -1e30
    masks[2, :, :P][(k >= P - NMEM) & (k <= q)] = 0
    return masks


def layouts(a):
    t = np.ascontiguousarray
    io = {"x": a["L0_attn_x"].reshape(NT, D), "memp": np.zeros((P, D), np.float32)}
    io["memp"][P - NMEM:] = a["L0_attn_mem"]
    for k in ("wq", "wk", "wv", "wo", "w1", "w2", "lin1", "lin2"):
        io[k + "T"] = t(a["L0_attn_" + k].T)
    io["w2"], io["b1"] = a["L0_attn_w2"], a["L0_attn_b1"]
    io["b1c"] = t(a["L0_attn_b1"].reshape(HC, P).T)
    io["b2c"] = t(a["L0_attn_b2"].reshape(KC, P).T)
    io["rates"] = np.empty((P, 2), np.float32)
    io["rates"][:, 0], io["rates"][:, 1] = a["L0_attn_alpha"], a["L0_attn_theta"]
    io["gateT"] = t(a["L0_ffn_gate_w"].T)
    io["gate_b"] = t(np.broadcast_to(a["L0_ffn_gate_b"], (P, E)))
    io["W1"], io["W2"] = a["L0_ffn_W1"], a["L0_ffn_W2"]
    io["eb1"] = t(a["L0_ffn_b1"].reshape(E, HC, P).transpose(2, 0, 1))
    io["eb2"] = t(a["L0_ffn_b2"].reshape(E, KC, P).transpose(2, 0, 1))
    io["ident"] = np.eye(P, dtype=np.float32)
    io["masks"] = window_masks()
    io["before"] = np.triu(np.ones((P, P), np.float32), 1)
    io["experts"] = t(np.broadcast_to(np.arange(E, dtype=np.float32), (P, E)))
    io["mem_scale"] = np.zeros((P, P), np.float32)
    io["mem_scale"][:, P - NMEM:] = B
    return io


def kernel(**inputs):
    import concourse.bacc as bacc
    from concourse.bass_utils import run_bass_kernel_spmd

    arrays = layouts({k: np.asarray(v) for k, v in inputs.items()})
    nc = bacc.Bacc("TRN2", target_bir_lowering=False, num_devices=1)
    io = {k: nc.dram_tensor("in_" + k, v.shape, F32, kind="ExternalInput").ap() for k, v in arrays.items()}
    io["out"] = nc.dram_tensor("out", [NT, D], F32, kind="ExternalOutput").ap()
    build(nc, io)
    r = run_bass_kernel_spmd(nc, [{"in_" + k: v for k, v in arrays.items()}], core_ids=[0])
    return r.results[0]["out"].reshape(B, S, D)
```

```python
import numpy as np
import concourse.bass as bass
from concourse import mybir
from concourse.alu_op_type import AluOpType as ALU
from contextlib import ExitStack

F32 = mybir.dt.float32
F32R = mybir.dt.float32r
BF16 = mybir.dt.bfloat16
I32 = mybir.dt.int32
ACTF = mybir.ActivationFunctionType
AX = mybir.AxisListType

P = 128
B, S, D = 8, 1024, 256
HID = 1024
HEADS, DH = 4, 64
NMEM = 64
NT = B * S
NBLK = NT // P
GRP = 4
NGRP = NBLK // GRP
NPAIR = NBLK // 2
KC = D // P
HC = HID // P
E, TOPK = 8, 2
ROUTED = 4 * 512
CAP = -(-5 * ROUTED * TOPK // (4 * E))
NSLOT = E * CAP
SLOTS = TOPK * NSLOT
ROW = D + 4
CLEAR = 5
EPS = 1e-5
NPR = 3
T = GRP * P
NCH = NT // T
NZ = 3
OUTSIDE = 65536.0
SB = CAP // P
NHF = 3
HALF = CAP // 2


class Step:

    def __init__(self, queue, emit, after, sem=None, value=None):
        self.queue, self.emit, self.after = queue, emit, [s for s in after if s is not None]
        self.sem, self.value, self.awaited = sem, value, sem is not None


class Queue:

    def __init__(self, engine, done):
        self.engine, self.done, self.steps = engine, done, []
        self.passed = {}

    def __call__(self, emit, after=()):
        step = Step(self, emit, after)
        for s in step.after:
            s.awaited = True
        self.steps.append(step)
        return step

    def number(self):
        for s in self.steps:
            if s.awaited and s.sem is None:
                self.done.count += 1
                s.sem, s.value = self.done, self.done.count

    def drain(self, handle):
        for s in self.steps:
            for w in s.after:
                if self.passed.get(w.sem.name, 0) < w.value:
                    handle.wait_ge(w.sem.sem, w.value)
                    self.passed[w.sem.name] = w.value
            last = s.emit(self.engine)
            if s.sem is not None:
                last.then_inc(s.sem.sem, 16 if s.sem.dma else 1)
        self.steps = []


class Sem:

    def __init__(self, sem, name, dma=False):
        self.sem, self.name, self.dma, self.count = sem, name, dma, 0


class Core:

    def __init__(self, nc, ctx):
        self.nc, self.ctx = nc, ctx
        self.sems = {}
        self.pe = Queue(nc.tensor, self.sem("pe_done"))
        self.act = Queue(nc.scalar, self.sem("act_done"))
        self.dve = Queue(nc.vector, self.sem("dve_done"))
        self.pool = Queue(nc.gpsimd, self.sem("pool_done"))
        self.sync = Queue(nc.sync, self.sem("sync_done"))

    def queues(self):
        return [self.pe, self.act, self.dve, self.pool, self.sync]

    def sem(self, name, dma=False):
        if name not in self.sems:
            self.sems[name] = Sem(self.ctx.enter_context(self.nc.semaphore(name)), name, dma)
        return self.sems[name]

    def transfer(self, queue, buffer, emit, after=()):
        sem = self.sem("dma_" + buffer, dma=True)
        sem.count += 16
        step = Step(queue, emit, after, sem, sem.count)
        for s in step.after:
            s.awaited = True
        queue.steps.append(step)
        return step

    def dma(self, queue, buffer, out, in_, after=()):
        return self.transfer(queue, buffer, lambda e: e.dma_start(out, in_), after)

    def gather(self, buffer, out, rows, at, bound, after=()):
        return self.transfer(self.pool, buffer, lambda e: e.indirect_dma_start(
            out, None, rows, bass.IndirectOffsetOnAxis(ap=at, axis=0), bounds_check=bound - 1, oob_is_err=False), after)

    def scatter(self, buffer, rows, at, in_, bound, after=()):
        return self.transfer(self.pool, buffer, lambda e: e.indirect_dma_start(
            rows, bass.IndirectOffsetOnAxis(ap=at, axis=0), in_, None, bounds_check=bound - 1, oob_is_err=False), after)

    def run(self):
        for q in self.queues():
            q.number()
        with self.nc.Block() as block:
            block.tensor(self.pe.drain)
            block.scalar(self.act.drain)
            block.vector(self.dve.drain)
            block.gpsimd(self.pool.drain)
            block.sync(self.sync.drain)


def matmul_split(out, lhs, rhs, first=True, last=True):
    terms = []
    for (ah, al), (bh, bl) in zip(lhs, rhs):
        terms += [(al, bh), (ah, bl), (ah, bh)]

    def emit(e):
        for n, (a, b) in enumerate(terms):
            i = e.matmul(out, a, b, start=first and n == 0, stop=last and n == len(terms) - 1)
        return i
    return emit


def copy(out, in_):
    return lambda e: e.tensor_copy(out, in_)


def act_copy(out, in_):
    return lambda e: e.activation(out, in_, ACTF.Copy)


def sub(out, a, b):
    return lambda e: e.tensor_tensor(out, a, b, ALU.subtract)


def add(out, a, b):
    return lambda e: e.tensor_tensor(out, a, b, ALU.add)


class Shared:

    def __init__(self, sb):
        self.x = [sb(f"shared_x{i}", [P, GRP * D]) for i in range(2)]
        self.xT = [sb(f"shared_xT{i}", [P, KC * GRP * P]) for i in range(2)]
        self.w1 = sb("w1_h", [P, KC, HID], F32R), sb("w1_l", [P, KC, HID], F32R)

    def pair_xT(self, i):
        n = KC * 2 * P
        return self.xT[0][:, i * n:(i + 1) * n].rearrange("p (k t) -> p k t", k=KC)


def attention_phase(c, io, shared):
    nc = c.nc
    with ExitStack() as ctx:
        def sb(name, shape, dt=F32):
            return ctx.enter_context(nc.sbuf_tensor(name, shape, dt))

        def ps(name, shape, dt=F32):
            return ctx.enter_context(nc.psum_tensor(name, shape, dt))

        pr = [sb(f"prob{i}", [P, HEADS, 2 * P]) for i in range(NPR)]
        w = {k: (sb(k + "_h", [P, KC, D], F32R), sb(k + "_l", [P, KC, D], F32R)) for k in ("wq", "wk", "wv", "wo")}
        ws = []
        ident, masks = sb("a_ident", [P, P]), sb("a_masks", [P, 3, 2 * P])
        ld_ident = c.dma(c.sync, "a_ident", ident[:], io["ident"])
        neg_half = sb("neg_half", [P, GRP])
        set_half = c.pool(lambda e: e.memset(neg_half[:], -0.5))

        x_g = [t[:].rearrange("p (j d) -> p j d", j=GRP) for t in shared.x]
        xn = [sb(f"xn{i}", [P, GRP, D]) for i in range(2)]
        stats = [sb(f"ln_stats{i}", [P, GRP, 6]) for i in range(2)]
        mv = [sb(f"ln_mv{i}", [P, GRP, 2]) for i in range(2)]
        rstd = [sb(f"ln_rstd{i}", [P, 2, GRP]) for i in range(2)]
        w1h, w1l = shared.w1
        xT, xTh, xTl = ([t.rearrange("p (k t) -> p k t", k=KC) for t in ts] for ts in
                        ([t[:] for t in shared.xT], [w1h[:, i] for i in range(2)], [w1l[:, i] for i in range(2)]))
        qh = [sb(f"qh{i}", [P, KC, GRP * P if i < 3 else P], F32R) for i in range(4)]
        ql = [sb(f"ql{i}", [P, KC, GRP * P if i < 3 else P], F32R) for i in range(4)]
        kh = [sb(f"kh{i}", [P, KC, 9 * P], F32R) for i in range(2)]
        kl = [sb(f"kl{i}", [P, KC, 9 * P], F32R) for i in range(2)]
        vh = [sb(f"vh{i}", [P, 9, D], F32R) for i in range(2)]
        vl = [sb(f"vl{i}", [P, 9, D], F32R) for i in range(2)]
        small = [sb(f"softmax_small{i}", [P, 4, HEADS]) for i in range(NPR)]
        pth = [sb(f"probT_h{i}", [P, 2, HEADS, P], F32R) for i in range(2)]
        ptl = [sb(f"probT_l{i}", [P, 2, HEADS, P], F32R) for i in range(2)]
        ah = [sb(f"attnT_h{i}", [P, KC, GRP * P], F32R) for i in range(2)]
        al = [sb(f"attnT_l{i}", [P, KC, GRP * P], F32R) for i in range(2)]
        oT = sb("outT", [P, KC, GRP * P])

        ps_s = ps("ps_scores", [P, 2, 2, 2 * P])
        ps_pt = ps("ps_probT", [P, 2, HEADS, P])
        ps_av = ps("ps_av", [P, KC, 2 * P])
        ps_p = [ps(f"ps_proj{i}", [P, GRP * P]) for i in range(3)]

        x_v = io["x"].rearrange("(g j p) d -> g p j d", j=GRP, p=P)
        last = {}
        xn_ready, qk_ready, v_ready, xT_pair = {}, {}, {}, {}
        turn = [0]

        def bank():
            turn[0] += 1
            return ps_p[turn[0] % 3], ("ps_p", turn[0] % 3)

        def order(G):
            return -1 if G == NGRP else G

        def blocks(G):
            return GRP if G < NGRP else 1

        def load_x(G):
            if G < NGRP:
                last["x", G] = c.dma(c.sync, f"x{G % 2}", x_g[G % 2][:], x_v[G], [last.get(("ln", G - 2))])

        def store_pairs(name, G, tile_of, dram, steps):
            for h in range((blocks(G) + 1) // 2):
                pair, n = 2 * G + h, min(2, blocks(G))
                out, in_ = tile_of(h, n, dram[pair])
                last[name, order(G)] = c.dma(c.sync, f"{name}{order(G) % 2}", out, in_, steps[h])

        def free_xn(o):
            return [last.get(("xn_st", o - 2)), last.get(("tx_pe", o - 2))]

        def store_xn(G, t):
            store_pairs("xn_st", G, lambda h, n, d: (d[:, 0:n, :], t[:, 2 * h:2 * h + n, :]), io["xn_d"], [xn_ready[G]] * 2)

        def take_memory():
            t = xn[order(NGRP) % 2]
            xn_ready[NGRP] = [c.dma(c.sync, "mem", t[:, 0, :], io["memp"])]
            store_xn(NGRP, t)

        def norm_stats(G, part):
            s, ld, src = G % 2, last["x", G], x_g[G % 2]
            js = range(2 * part, 2 * part + 2)
            for j in js:
                st = c.dve(lambda e, j=j: e.bn_stats(stats[s][:, j], src[:, j]), [ld, last.get(("ln_ag", G - 2))])
            for j in js:
                ag = c.dve(lambda e, j=j: e.bn_aggr(mv[s][:, j], stats[s][:, j]), [st, last.get(("ln", G - 2))])
            if part:
                last["ln_ag", G] = ag
                ve = c.dve(lambda e: e.tensor_scalar(rstd[s][:, 0], mv[s][:, :, 1], EPS, None, ALU.add), [ag, last.get(("ln_r", G - 2))])
                last["ln_r", G] = c.pool(lambda e: e.tensor_tensor(rstd[s][:, 1], rstd[s][:, 0], neg_half[:], ALU.pow),
                                         [ve, set_half, last.get(("ln", G - 2))])

        def norm_apply(G, part):
            s, t, src = G % 2, xn[G % 2], x_g[G % 2]
            for j in range(2 * part, 2 * part + 2):
                a = c.dve(lambda e, j=j: e.tensor_scalar(t[:, j], src[:, j], mv[s][:, j, 0:1], rstd[s][:, 1, j:j + 1],
                                                          ALU.subtract, ALU.mult), [last["ln_r", G]] + free_xn(G))
            if part:
                last["ln", G] = a
                xn_ready[G] = [a]
                store_xn(G, t)

        def transpose_x(G, h):
            o = order(G)
            s, n = o % 2, min(2, blocks(G))
            cols = slice(2 * h * P, (2 * h + n) * P)
            b, key = bank()
            ps_x = b[:].rearrange("p (k t) -> p k t", k=KC)

            def emit(e):
                for k in range(KC):
                    for j in range(n):
                        i = e.transpose(ps_x[:, k, j * P:(j + 1) * P], xn[s][:, 2 * h + j, k * P:(k + 1) * P], ident[:])
                return i
            t = c.pe(emit, xn_ready[G] + [ld_ident, last.get(key)])
            last["tx_pe", o] = t
            f = c.act(act_copy(xT[s][:, :, cols], ps_x[:, :, 0:n * P]), [t, last.get(("xT_st", o - 2)), last.get(("xTl", o - 2))])
            last[key] = f
            hi = c.dve(copy(xTh[s][:, :, cols], xT[s][:, :, cols]), [f, last.get(("xT_use", o - 2))])
            lo = c.pool(sub(xTl[s][:, :, cols], xT[s][:, :, cols], xTh[s][:, :, cols]), [hi, last.get(("xT_use", o - 2))])
            last["xTl", o] = lo
            xT_pair[G, h] = lo
            d = io["xT_d"][2 * G + h]
            last["xT_st", o] = c.dma(c.sync, f"xT_st{s}", d[:, :, 0:n * P], xT[s][:, :, cols], [f])

        def q_slot(G, low):
            return (ql if low else qh)[3 if G == NGRP else G % 3]

        def project_qk(G, t):
            s, n, m = order(G) % 2, blocks(G) * P, t % 2
            wh, wl = w["wq" if t < 2 else "wk"]
            lhs = [(wh[:, k, m * P:(m + 1) * P], wl[:, k, m * P:(m + 1) * P]) for k in range(KC)]
            rhs = [(xTh[s][:, k, 0:n], xTl[s][:, k, 0:n]) for k in range(KC)]
            ps_j, key = bank()
            mm = c.pe(matmul_split(ps_j[:, 0:n], lhs, rhs), [xT_pair[G, 0], xT_pair.get((G, 1)), last.get(key), ws[0], ws[1]])
            last["xT_use", order(G)] = mm
            if t < 2:
                free = [last.get(("score", g)) for g in range(GRP * (G - 3), GRP * (G - 3) + GRP)] if 3 <= G < NGRP else []
                dst = [(q_slot(G, 0)[:, m, 0:n], q_slot(G, 1)[:, m, 0:n])]
            elif G < NGRP:
                b = G // 2
                free = [last.get(("score", 8 * (b - 2) + 7))] if b >= 2 else []
                cols = slice(P + (G % 2) * GRP * P, P + (G % 2 + 1) * GRP * P)
                dst = [(kh[b % 2][:, m, cols], kl[b % 2][:, m, cols])]
            else:
                free, dst = [], [(kh[b][:, m, 0:P], kl[b][:, m, 0:P]) for b in range(2)]
            for hi_t, _ in dst:
                hi = c.act(act_copy(hi_t, ps_j[:, 0:n]), [mm] + free)
            for hi_t, lo_t in dst:
                lo = c.dve(sub(lo_t, ps_j[:, 0:n], hi_t), [hi] + free)
                qk_ready[G, t] = qk_ready.get((G, t), []) + [lo]
                last[key] = lo

        def project_v(G, h):
            s, n = order(G) % 2, min(2, blocks(G))
            wh, wl = w["wv"]
            b, key = bank()
            ps_v = b[:].rearrange("p (j d) -> p j d", j=2)

            def emit(e):
                for j in range(n):
                    cols = slice((2 * h + j) * P, (2 * h + j + 1) * P)
                    i = matmul_split(ps_v[:, j], [(xTh[s][:, k, cols], xTl[s][:, k, cols]) for k in range(KC)],
                                     [(wh[:, k], wl[:, k]) for k in range(KC)])(e)
                return i
            mm = c.pe(emit, [xT_pair[G, h], last.get(key), ws[2]])
            last["xT_use", order(G)] = mm
            if G < NGRP:
                b = G // 2
                free = [last.get(("av", 8 * (b - 2) + 7))] if b >= 2 else []
                at = 1 + (G % 2) * GRP + 2 * h
                dst = [(vh[b % 2][:, at:at + 2], vl[b % 2][:, at:at + 2])]
            else:
                free, dst = [], [(vh[b][:, 0:1], vl[b][:, 0:1]) for b in range(2)]
            for hi_t, _ in dst:
                hi = c.act(act_copy(hi_t, ps_v[:, 0:n]), [mm] + free)
            for hi_t, lo_t in dst:
                lo = c.dve(sub(lo_t, ps_v[:, 0:n], hi_t), [hi] + free)
                v_ready[G, h] = v_ready.get((G, h), []) + [lo]
                last[key] = lo

        def place(g):
            if g == NBLK:
                return (B - 1) % 2, 0, 2
            return (g // 8) % 2, g % 8, 1 if g % 8 == 0 else 0

        def scores(g):
            G, (par, i, mask) = g // GRP, place(g)
            qc, kcols = slice((g % GRP) * P, (g % GRP + 1) * P), slice(i * P, (i + 2) * P)

            def emit(e):
                for c2 in range(2):
                    for n in range(3):
                        for half in range(2):
                            r = slice(half * DH, (half + 1) * DH)
                            a = q_slot(G, n == 0)[r, c2, qc]
                            b = (kl if n == 1 else kh)[par][r, c2, kcols]
                            x = e.matmul(ps_s[:, half, c2], a, b, start=n == 0, stop=n == 2)
                return x
            need = [s for t in range(4) for s in qk_ready[G, t]]
            need += [s for t in (2, 3) for s in qk_ready[NGRP, t]]
            if g % GRP == 0 and g % 8 and g < NBLK:
                need += [s for t in (2, 3) for s in qk_ready[G - 1, t]]
            sc = c.pe(emit, need + [last.get("ps_s")])
            last["score", g] = sc
            p, sm = pr[g % NPR], small[g % NPR]
            for h in range(HEADS):
                mx = c.dve(lambda e, h=h: e.tensor_tensor_reduce(
                    out=p[:, h], in0=ps_s[:, h % 2, h // 2], in1=masks[:, mask], scale=1.0, scalar=-3.0e38,
                    op0=ALU.add, op1=ALU.max, accum_out=sm[:, 0, h:h + 1]),
                    [sc, ld_masks, ws[3], last.get(("pt_pe", g - NPR)), last.get(("exp", g - NPR))])
            last["ps_s"] = mx
            last["max", g] = c.dve(lambda e: e.tensor_scalar(sm[:, 1], sm[:, 0], -1.0 / DH ** 0.5, None, ALU.mult), [mx, last.get(("exp", g - NPR))])

        def soft(g):
            p, sm = pr[g % NPR], small[g % NPR]
            for h in range(HEADS):
                ex = c.act(lambda e, h=h: e.activation(p[:, h], p[:, h], ACTF.Exp, bias=sm[:, 1, h:h + 1],
                                                       scale=1.0 / DH ** 0.5, accum_out=sm[:, 2, h:h + 1]),
                           [last["max", g], last.get(("prob", g - NPR))])
            last["exp", g] = ex

        def normalise(g):
            p, sm = pr[g % NPR], small[g % NPR]
            rc = c.dve(lambda e: e.reciprocal(sm[:, 3], sm[:, 2]), [last["exp", g], last.get(("prob", g - NPR))])
            last["prob", g] = c.pool(lambda e: e.tensor_tensor(p[:], p[:], sm[:, 3].unsqueeze(2).broadcast_to([P, HEADS, 2 * P]), ALU.mult), [rc])

        def transpose_p(g):
            p = pr[g % NPR]

            def emit(e):
                for kb in range(2):
                    for h in range(HEADS):
                        x = e.transpose(ps_pt[:, kb, h], p[:, h, kb * P:(kb + 1) * P], ident[:])
                return x
            t = c.pe(emit, [last["prob", g], last.get("ps_pt")])
            last["pt_pe", g] = t
            hi = c.act(act_copy(pth[g % 2][:], ps_pt[:]), [t, last.get(("av", g - 2))])
            lo = c.dve(sub(ptl[g % 2][:], ps_pt[:], pth[g % 2][:]), [hi, last.get(("av", g - 2))])
            last["ps_pt"] = last["pt", g] = lo

        def attend(g):
            par, i, _ = place(g)
            G = g // GRP
            cols = slice((g % GRP) * P, (g % GRP + 1) * P)

            def emit(e):
                for c2 in range(KC):
                    vc = slice(c2 * P, (c2 + 1) * P)
                    x = matmul_split(ps_av[:, c2], [(vh[par][:, i + kb, vc], vl[par][:, i + kb, vc]) for kb in range(2)],
                                     [(pth[g % 2][:, kb, 2 * c2:2 * c2 + 2], ptl[g % 2][:, kb, 2 * c2:2 * c2 + 2])
                                      for kb in range(2)])(e)
                return x
            need = [last["pt", g], last.get("ps_av")] + [s for k in v_ready if k[0] in (G, G - 1, NGRP) for s in v_ready[k]]
            av = c.pe(emit, need)
            last["av", g] = av
            for half in range(2):
                r, src = slice(half * DH, (half + 1) * DH), slice(half * P, (half + 1) * P)
                hi = c.act(act_copy(ah[G % 2][r, :, cols], ps_av[r, :, src]), [av, last.get(("wo", G - 2))])
            for half in range(2):
                r, src = slice(half * DH, (half + 1) * DH), slice(half * P, (half + 1) * P)
                lo = c.dve(sub(al[G % 2][r, :, cols], ps_av[r, :, src], ah[G % 2][r, :, cols]), [hi, last.get(("wo", G - 2))])
            last["ps_av"] = last["attn", g] = lo

        def out_project(G, m):
            n = blocks(G) * P
            wh, wl = w["wo"]
            mc = slice(m * P, (m + 1) * P)
            ps_j, key = bank()
            mm = c.pe(matmul_split(ps_j[:, 0:n], [(wh[:, k, mc], wl[:, k, mc]) for k in range(KC)],
                                   [(ah[G % 2][:, k, 0:n], al[G % 2][:, k, 0:n]) for k in range(KC)]),
                      [last["attn", 4 * G + blocks(G) - 1], last.get(key), ws[3]])
            last[key] = ev = c.act(act_copy(oT[:, m, 0:n], ps_j[:, 0:n]), [mm, last.get(("oT_st", G - 1))])
            if m == KC - 1:
                last["wo", G] = mm
                for h in range((blocks(G) + 1) // 2):
                    k = min(2, blocks(G))
                    last["oT_st", G] = c.dma(c.sync, "oT_st", io["oT_d"][2 * G + h][:, :, 0:k * P],
                                             oT[:, :, 2 * h * P:(2 * h + k) * P], [ev])

        def prep(G, n):
            if n < 2:
                if G < NGRP or n == 0:
                    transpose_x(G, n)
            elif n in (5, 7):
                if G < NGRP or n == 5:
                    project_v(G, (n - 5) // 2)
            else:
                project_qk(G, {2: 0, 3: 2, 4: 1, 6: 3}[n])

        def load_next():
            w1_v = io["w1T"].rearrange("(c p) n -> p c n", p=P)
            for k in range(KC):
                last["ld_w1", k] = c.dma(c.sync, f"g_w1_{k}", shared.x[k][:], w1_v[:, k], [last["ln", NGRP - 2 + k]])
            free = [[last["xT_st", G], last["xTl", G]] for G in (NGRP - 2, NGRP - 1)]
            last["next_xT"] = c.dma(c.sync, "g_xT0", shared.pair_xT(0), io["xT_d"][0], free[0])
            last["next_b1"] = c.dma(c.sync, "g_b1", shared.xT[1][:], io["b1"], free[1])

        def split_next(n):
            k, cols = n // 2, slice((n % 2) * (HID // 2), (n % 2 + 1) * (HID // 2))
            hi = c.act(act_copy(w1h[:, k, cols], shared.x[k][:, cols]), [last["ld_w1", k], last["xT_use", NGRP - 2 + k]])
            c.dve(sub(w1l[:, k, cols], shared.x[k][:, cols], w1h[:, k, cols]), [hi, last["xT_use", NGRP - 2 + k]])

        load_x(0)
        take_memory()
        staged = []
        for n, (k, (hi, lo)) in enumerate(w.items()):
            full = pr[n // 2][:, 2 * (n % 2):2 * (n % 2) + 2]
            staged.append((full, c.dma(c.sync, k, full, io[k + "T"].rearrange("(c p) n -> p c n", p=P)), hi, lo))
        load_x(1)
        ld_masks = c.dma(c.sync, "a_masks", masks[:], io["masks"].rearrange("m p k -> p m k"))

        def norm(G):
            for step in (norm_stats, norm_apply):
                for part in range(2):
                    step(G, part)
            load_x(G + 2)

        norm(0)
        for full, ld, hi, lo in staged:
            h = c.dve(copy(hi[:], full), [ld])
            ws.append(c.dve(sub(lo[:], full, hi[:]), [h]))
        for G in (NGRP, 0):
            prep(G, 0)
            prep(G, 1)
        norm(1)
        for G in (NGRP, 0, 1):
            for n in range(2, 8):
                prep(G, n)
                if G == 0 and n == 3:
                    prep(1, 0)
                    prep(1, 1)
                    norm(2)
        for a in range(NBLK + 6):
            G, j = a // GRP + 2, a % GRP
            if a <= NBLK:
                scores(a)
            if 1 <= a <= NBLK + 1:
                normalise(a - 1)
            if G < NGRP:
                prep(G, 2 * j)
                if j == 0:
                    prep(G, 1)
            if 2 <= a <= NBLK + 2:
                transpose_p(a - 2)
            if a <= NBLK:
                soft(a)
            if 3 <= a <= NBLK + 3:
                attend(a - 3)
            if G < NGRP and j:
                prep(G, 2 * j + 1)
            if G + 1 < NGRP and j == 0:
                norm_stats(G + 1, 0)
                norm_stats(G + 1, 1)
            elif G + 1 < NGRP and j < 3:
                norm_apply(G + 1, j - 1)
            if G + 3 < NGRP and j == 3:
                load_x(G + 3)
            if j == 3 and 1 <= a // GRP <= NGRP:
                out_project(a // GRP - 1, 0)
            if j == 0 and 2 <= a // GRP <= NGRP + 1:
                out_project(a // GRP - 2, 1)
            if a == NBLK - GRP:
                load_next()
            if NBLK - GRP < a <= NBLK:
                split_next(a - NBLK + GRP - 1)
        for m in range(KC):
            out_project(NGRP, m)
        stores = [last["xn_st", G] for G in (NGRP - 1, NGRP - 2)]
        stores += [last["xT_st", G] for G in (NGRP - 1, NGRP - 2)] + [last["oT_st", NGRP]]
        c.sync(lambda e: e.nop(), stores)
        c.run()
    return last["next_xT"], last["next_b1"]


def load_chunk(c, io, shared, C, free):
    xT = shared.xT[C % 2][:].rearrange("p (k t) -> p k t", k=KC)
    for h in range(2):
        step = c.dma(c.sync, f"m_xT{C % 2}", xT[:, :, 2 * h * P:(2 * h + 2) * P], io["xT_d"][2 * C + h], free)
    return step


def gradient_phase(c, io, shared, halves, g1, g2, b1n, b2n, ld_xT0, ld_b1):
    nc = c.nc
    with ExitStack() as ctx:
        def sb(name, shape, dt=F32):
            return ctx.enter_context(nc.sbuf_tensor(name, shape, dt))

        def ps(name, shape, dt=F32):
            return ctx.enter_context(nc.psum_tensor(name, shape, dt))

        hf = [sb(f"h_full{i}", [P, HID]) for i in range(2)]
        qf = sb("silu_q", [P, HID])
        sp = shared.x + [sb(f"silu_slope{i}", [P, HID]) for i in (2, 3)]
        w1h, w1l = shared.w1
        w2Th, w2Tl = sb("w2T_h", [P, HC, D], F32R), sb("w2T_l", [P, HC, D], F32R)
        w2h, w2l = sb("w2_h", [P, KC, HID], F32R), sb("w2_l", [P, KC, HID], F32R)
        w1_v = io["w1T"].rearrange("(c p) n -> p c n", p=P)
        w2T_v = io["w2T"].rearrange("(c p) n -> p c n", p=P)
        w2_v = io["w2"].rearrange("(c p) n -> p c n", p=P)
        last, w_ready = {}, {}

        def load_weight(name, k, full, dram):
            last["ld", name, k] = c.dma(c.sync, f"g_{name}_{k}", full, dram)

        def split_weight(name, k, full, high, low):
            h = c.act(act_copy(high, full), [last["ld", name, k]])
            w_ready[name] = last["split", name, k] = c.dve(sub(low, full, high), [h])

        ident = sb("g_ident", [P, P])
        ld_ident = c.dma(c.sync, "g_ident", ident[:], io["ident"])
        row_scale = sb("mem_row_scale", [P, P])
        ld_scale = c.dma(c.sync, "g_scale", row_scale[:], io["mem_scale"])
        b2c = sb("b2_col", [P, KC])
        ld_b2 = c.dma(c.sync, "g_b2", b2c[:], io["b2c"])
        b1 = shared.xT[1]
        dz_sum = sb("dz_sum", [P, HID])
        db2 = sb("db2_parts", [P, KC, NPAIR + 1])
        zero_g1 = c.pool(lambda e: e.memset(g1[:], 0.0))
        zero_dz = c.pool(lambda e: e.memset(dz_sum[:], 0.0))

        xn_f = [sb(f"xn_f{i}", [P, 2, D]) for i in range(2)]
        xT_f = [shared.pair_xT(i) for i in range(2)]
        oT_f = [sb(f"oT_f{i}", [P, KC, 2 * P]) for i in range(2)]
        xnh = [sb(f"xn_h{i}", [P, 2, D], F32R) for i in range(2)]
        xnl = [sb(f"xn_l{i}", [P, 2, D], F32R) for i in range(2)]
        xTh = sb("g_xTh", [P, KC, 2 * P], F32R)
        xTl = sb("g_xTl", [P, KC, 2 * P], F32R)
        hh = [sb(f"h_h{i}", [P, HID], F32R) for i in range(4)]
        hl = [sb(f"h_l{i}", [P, HID], F32R) for i in range(4)]
        hTh, hTl = (t[:].rearrange("p (k t) -> p k t", k=HC) for t in halves)
        dzh = [sb(f"dz_h{i}", [P, HID], F32R) for i in range(2)]
        dzl = [sb(f"dz_l{i}", [P, HID], F32R) for i in range(2)]
        dpf = sb("dpredT", [P, KC, 2 * P])
        dTh, dTl = sb("dpredT_h", [P, KC, 2 * P], F32R), sb("dpredT_l", [P, KC, 2 * P], F32R)
        dth, dtl = sb("dpred_h", [P, 2, D], F32R), sb("dpred_l", [P, 2, D], F32R)

        banks = [ps(f"g_bank{i}", [P, 512]) for i in range(8)]
        turn = [0]

        def bank():
            turn[0] += 1
            return banks[turn[0] % 8], ("bank", turn[0] % 8)

        def n_of(p):
            return 2 if p < NPAIR else 1

        def load(p):
            n, s = n_of(p), p % 2
            last["ld", p] = [
                c.dma(c.sync, f"g_xT{s}", xT_f[s][:, :, 0:n * P], io["xT_d"][p][:, :, 0:n * P], [last.get(("xTl", p - 2))]) if p else ld_xT0,
                c.dma(c.sync, f"g_xn{s}", xn_f[s][:, 0:n], io["xn_d"][p][:, 0:n], [last.get(("xnl", p - 2))]),
                c.dma(c.sync, f"g_oT{s}", oT_f[s][:, :, 0:n * P], io["oT_d"][p][:, :, 0:n * P], [last.get(("dp", p - 2))])]

        def split_xT(p):
            n, s = n_of(p), p % 2
            ld = last["ld", p]
            h = c.act(act_copy(xTh[:, :, 0:n * P], xT_f[s][:, :, 0:n * P]), [ld[0], last.get(("z", p - 1))])
            last["xTl", p] = c.dve(sub(xTl[:, :, 0:n * P], xT_f[s][:, :, 0:n * P], xTh[:, :, 0:n * P]), [h, last.get(("z", p - 1))])

        def split_xn(p):
            n, s = n_of(p), p % 2
            ld = last["ld", p]
            h = c.act(act_copy(xnh[s][:, 0:n], xn_f[s][:, 0:n]), [ld[1], last.get(("gw1", p - 2))])
            last["xnl", p] = c.dve(sub(xnl[s][:, 0:n], xn_f[s][:, 0:n], xnh[s][:, 0:n]), [h, last.get(("gw1", p - 2))])

        def forward(p, b):
            g = 2 * p + b
            cols = slice(b * P, (b + 1) * P)
            t, hfull = sp[g % 4], hf[g % 2]
            free = [last.get(("hT_pe", g - 2)), last.get(("hl", g - 2)), last.get(("q", g - 2))]
            halves = [slice(0, 512), slice(512, 1024)]
            zs = []
            for hc in halves:
                acc, key = bank()
                z = c.pe(matmul_split(acc[:], [(xTh[:, k, cols], xTl[:, k, cols]) for k in range(KC)],
                                      [(w1h[:, k, hc], w1l[:, k, hc]) for k in range(KC)]),
                         [last["xTl", p], last.get(key)])
                last[key] = zb = c.dve(add(hfull[:, hc], acc[:], b1[:, hc]), [z, ld_b1] + free)
                zs.append(zb)
            for hc, zb in zip(halves, zs):
                s = c.act(lambda e, hc=hc: e.activation(t[:, hc], hfull[:, hc], ACTF.Sigmoid), [zb, last.get(("dzs", g - 4)), staged.get(g)])
                h = c.dve(lambda e, hc=hc: e.tensor_tensor(hfull[:, hc], hfull[:, hc], t[:, hc], ALU.mult), [s])
            last["z", p] = z
            last["h", g] = h
            q = c.dve(lambda e: e.scalar_tensor_tensor(qf[:], t[:], 1.0, hfull[:], ALU.subtract, ALU.mult), [h, last.get(("sp", g - 1))])
            last["q", g] = q
            hi = c.act(act_copy(hh[g % 4][:], hfull[:]), [h, last.get(("gw2", p - 2))])
            last["sp", g] = c.pool(sub(t[:], t[:], qf[:]), [q])
            last["hl", g] = c.pool(sub(hl[g % 4][:], hfull[:], hh[g % 4][:]), [hi, last.get(("gw2", p - 2))])

        def transpose_h(p, b):
            g = 2 * p + b
            cols = slice(b * P, (b + 1) * P)
            for half in range(2):
                ks = slice(4 * half, 4 * half + 4)
                acc, key = bank()

                def emit(e, half=half, acc=acc):
                    for k in range(4):
                        i = e.transpose(acc[:, k * P:(k + 1) * P], hf[g % 2][:, (4 * half + k) * P:(4 * half + k + 1) * P], ident[:])
                    return i
                t = c.pe(emit, [last["h", g], ld_ident, last.get(key)])
                src = acc[:].rearrange("p (k t) -> p k t", k=4)
                hi = c.act(act_copy(hTh[:, ks, cols], src), [t, last.get(("pred", p - 1))])
                lo = c.dve(sub(hTl[:, ks, cols], src, hTh[:, ks, cols]), [hi, last.get(("pred", p - 1))])
                last[key] = lo
            last["hT_pe", g] = t
            last["hT", g] = lo

        def predict(p):
            n, s = n_of(p), p % 2
            N = n * P
            acc, key = bank()

            def emit(e):
                for m in range(KC):
                    mc = slice(m * P, (m + 1) * P)
                    i = matmul_split(acc[:, m * 2 * P:m * 2 * P + N], [(w2Th[:, k, mc], w2Tl[:, k, mc]) for k in range(HC)],
                                     [(hTh[:, k, 0:N], hTl[:, k, 0:N]) for k in range(HC)])(e)
                return i
            mm = c.pe(emit, [last["hT", 2 * p + n - 1], w_ready["w2T"], last.get(key)])
            last["pred", p] = mm
            free = [last.get(("dT_pe", p - 1)), last.get(("dTl", p - 1))]
            for m in range(KC):
                d = c.dve(lambda e, m=m: e.scalar_tensor_tensor(
                    dpf[:, m, 0:N], acc[:, m * 2 * P:m * 2 * P + N], b2c[:, m:m + 1], oT_f[s][:, m, 0:N],
                    ALU.add, ALU.subtract, accum_out=db2[:, m, p:p + 1]), [mm, ld_b2, last["ld", p][2]] + free)
            last[key] = last["dp", p] = d
            if p == NPAIR:
                for m in range(KC):
                    d = c.dve(lambda e, m=m: e.tensor_tensor(dpf[:, m, 0:N], dpf[:, m, 0:N], row_scale[:], ALU.mult), [d, ld_scale])
                for m in range(KC):
                    d2 = c.dve(lambda e, m=m: e.tensor_reduce(db2[:, m, p:p + 1], dpf[:, m, 0:N], AX.X, ALU.add), [d])
                last["db2"] = d2
            hi = c.act(act_copy(dTh[:, :, 0:N], dpf[:, :, 0:N]), [d, last.get(("dh", p - 1))])
            last["dTl", p] = c.dve(sub(dTl[:, :, 0:N], dpf[:, :, 0:N], dTh[:, :, 0:N]), [hi, last.get(("dh", p - 1))])
            last["dpf", p] = d

        def transpose_d(p):
            n = n_of(p)
            acc, key = bank()

            def emit(e):
                for b in range(n):
                    for m in range(KC):
                        i = e.transpose(acc[:, (2 * b + m) * P:(2 * b + m + 1) * P], dpf[:, m, b * P:(b + 1) * P], ident[:])
                return i
            t = c.pe(emit, [last["dpf", p], last.get(key)])
            last["dT_pe", p] = t
            src = acc[:, 0:n * D].rearrange("p (b d) -> p b d", b=n)
            hi = c.act(act_copy(dth[:, 0:n], src), [t, last.get(("gw2", p - 1))])
            lo = c.dve(sub(dtl[:, 0:n], src, dth[:, 0:n]), [hi, last.get(("gw2", p - 1))])
            last[key] = last["dtok", p] = lo

        def backward(p, b):
            g = 2 * p + b
            cols = slice(b * P, (b + 1) * P)
            t = sp[g % 4]
            for half in range(2):
                hc = slice(half * 512, (half + 1) * 512)
                acc, key = bank()
                mm = c.pe(matmul_split(acc[:], [(dTh[:, k, cols], dTl[:, k, cols]) for k in range(KC)],
                                       [(w2h[:, k, hc], w2l[:, k, hc]) for k in range(KC)]),
                          [last["dTl", p], w_ready["w2"], last.get(key)])
                last[key] = dz = c.dve(lambda e, hc=hc, acc=acc: e.tensor_tensor(t[:, hc], acc[:], t[:, hc], ALU.mult), [mm, last["sp", g]])
            last["dh", p] = mm
            hi = c.act(act_copy(dzh[b][:], t[:]), [dz, last.get(("gw1", p - 1))])
            last["dz", g] = c.pool(sub(dzl[b][:], t[:], dzh[b][:]), [hi, last.get(("gw1", p - 1))])
            last["dzs", g] = c.pool(add(dz_sum[:], dz_sum[:], t[:]), [dz, last.get(("dzs", g - 1)), zero_dz])

        def accumulate_w2(p, tiles):
            n = n_of(p)
            for t in tiles:
                acc, key = bank()

                def emit(e, t=t, acc=acc):
                    for u in range(2):
                        hc = slice((2 * t + u) * P, (2 * t + u + 1) * P)
                        i = matmul_split(acc[:, u * D:(u + 1) * D], [(hh[(2 * p + b) % 4][:, hc], hl[(2 * p + b) % 4][:, hc]) for b in range(n)],
                                         [(dth[:, b], dtl[:, b]) for b in range(n)])(e)
                    return i
                mm = c.pe(emit, [last["dtok", p], last["hl", 2 * p + n - 1], last.get(key)])
                dst = g2[:, 2 * t:2 * t + 2].rearrange("p a b -> p (a b)")
                last[key] = last["g2", t] = c.dve(add(dst, acc[:], dst), [mm, last["zero_g2"], last.get(("g2", t))])
            last["gw2", p] = mm

        def accumulate_w1(p, tiles):
            n, s = n_of(p), p % 2
            for t in tiles:
                k, hc = t // 2, slice((t % 2) * 512, (t % 2 + 1) * 512)
                acc, key = bank()
                mm = c.pe(matmul_split(acc[:], [(xnh[s][:, b, k * P:(k + 1) * P], xnl[s][:, b, k * P:(k + 1) * P]) for b in range(n)],
                                       [(dzh[b][:, hc], dzl[b][:, hc]) for b in range(n)]),
                          [last["dz", 2 * p + n - 1], last["xnl", p], last.get(key)])
                last[key] = last["g1", t] = c.dve(add(g1[:, k, hc], acc[:], g1[:, k, hc]), [mm, last["rows_cleared"], last.get(("g1", t))])
            last["gw1", p] = mm

        pairs = NPAIR + 1
        load(0)
        for k in range(2):
            load_weight("w2T", k, g2[:, 4 * k:4 * k + 4], w2T_v[:, 4 * k:4 * k + 4])
            load_weight("w2", k, sp[2 + k][:], w2_v[:, k])
        load(1)
        split_xT(0)
        staged = {}
        xbuf_rows = io["xbuf_d"].rearrange("(p a) d -> p (a d)", p=P)
        width = CLEAR * ROW
        for n in range(SLOTS // P // CLEAR):
            last["rows_cleared"] = c.dma(c.sync, "zero_rows", xbuf_rows[:, n * width:(n + 1) * width],
                                         g1[:].rearrange("p a b -> p (a b)")[:, 0:width], [zero_g1, last["ld", 1][2]])
        rates, b1c = sb("g_rates_sb", [P, 4]), sb("b1_col", [P, HC])
        ld_r = c.dma(c.sync, "g_rates", rates[:, 0:2], io["rates"])
        ld_b1c = c.dma(c.sync, "g_b1c", b1c[:], io["b1c"])

        def old_weights():
            out = []
            parts = [(g1[:, k], w1_v[:, k]) for k in range(2)] + [(g2[:, 4 * k:4 * k + 4], w2T_v[:, 4 * k:4 * k + 4]) for k in range(2)]
            free = [[last["sp", 2 * NPAIR]]] + [[last["dzs", g], last["dz", g]] for g in range(2 * NPAIR - 3, 2 * NPAIR)]
            for n, ((gt, view), t) in enumerate(zip(parts, [qf, sp[1], sp[2], sp[3]])):
                w = t[:] if n < 2 else t[:].rearrange("p (a b) -> p a b", b=D)
                ld = c.dma(c.sync, f"g_old{n}", w, view, free[n])
                out.append((ld, gt, w))
            return out

        def load_chunks():
            free = [[last["xTl", NPAIR - 1], last["xTl", NPAIR]], [last["h", 2 * NPAIR]]]
            for C in range(2):
                last["ld_chunk", C] = load_chunk(c, io, shared, C, free[C])

        def split_chunk():
            (high, low), n = halves, KC * T
            hi = c.act(act_copy(high[:, 0:n], shared.xT[0][:]), [last["ld_chunk", 0], last["pred", NPAIR]])
            c.dve(sub(low[:, 0:n], shared.xT[0][:], high[:, 0:n]), [hi, last["pred", NPAIR]])

        for p in range(pairs + 1):
            now, both = p < pairs, p < NPAIR
            before = p >= 1
            if now:
                forward(p, 0)
            if before:
                backward(p - 1, 0)
            if both:
                forward(p, 1)
            if p == 0:
                for k in range(2):
                    r = slice(4 * k, 4 * k + 4)
                    split_weight("w2T", k, g2[:, r], w2Th[:, r], w2Tl[:, r])
                last["zero_g2"] = c.pool(lambda e: e.memset(g2[:], 0.0), [last["split", "w2T", 0], last["split", "w2T", 1]])
            if before and n_of(p - 1) == 2:
                backward(p - 1, 1)
            if before:
                accumulate_w2(p - 1, [0])
            if now:
                transpose_h(p, 0)
            if before:
                accumulate_w2(p - 1, [1])
            if both:
                transpose_h(p, 1)
            if p + 1 < pairs:
                split_xT(p + 1)
            if before:
                accumulate_w2(p - 1, [2, 3])
            if now:
                predict(p)
            if before:
                accumulate_w1(p - 1, [0, 1])
            if p == pairs:
                split_chunk()
            if now:
                transpose_d(p)
            if p == pairs - 1:
                old = old_weights()
                load_chunks()
            if before:
                accumulate_w1(p - 1, [2, 3])
            if p == 0:
                for k in range(KC):
                    split_weight("w2", k, sp[2 + k][:], w2h[:, k], w2l[:, k])
                    staged[2 + k] = last["split", "w2", k]
                split_xn(0)
            if p + 1 < pairs:
                split_xn(p + 1)
            if p + 2 < pairs:
                load(p + 2)

        keep = c.dve(lambda e: e.tensor_scalar(rates[:, 2:3], rates[:, 0:1], -1.0, 1.0, ALU.mult, ALU.add), [ld_r])
        step = c.dve(lambda e: e.tensor_scalar(rates[:, 3:4], rates[:, 1:2], -1.0, None, ALU.mult), [ld_r])
        ones = c.dve(lambda e: e.memset(rates[:, 0:1], 1.0), [keep])
        sums, key = bank()

        def emit(e):
            for k in range(HC):
                i = e.matmul(sums[:, k:k + 1], dz_sum[:, k * P:(k + 1) * P], rates[:, 0:1], start=True, stop=True)
            return i
        mm = c.pe(emit, [last["dzs", 2 * NPAIR], last.get(key), ones])
        done = [last["g1", t] for t in range(4)] + [last["g2", t] for t in range(4)]
        kept = [c.dve(lambda e, w=w: e.tensor_scalar(w, w, rates[:, 2:3], None, ALU.mult), [ld, keep]) for ld, gt, w in old]
        new = [c.dve(lambda e, w=w, gt=gt: e.scalar_tensor_tensor(gt, gt, rates[:, 3:4], w, ALU.mult, ALU.add), [a, step] + done)
               for a, (ld, gt, w) in zip(kept, old)]
        for k in range(KC):
            hi = c.act(act_copy(w1h[:, k], g1[:, k]), [new[k], last["z", NPAIR]])
            c.dve(sub(w1l[:, k], g1[:, k], w1h[:, k]), [hi, last["z", NPAIR]])
        red = c.dve(lambda e: e.tensor_reduce(b2n[:], db2[:], AX.X, ALU.add), [last["db2"]])
        a = c.dve(lambda e: e.tensor_scalar(b2c[:], b2c[:], rates[:, 2:3], None, ALU.mult), [last["dp", NPAIR], keep])
        c.dve(lambda e: e.scalar_tensor_tensor(b2n[:], b2n[:], rates[:, 3:4], b2c[:], ALU.mult, ALU.add), [a, red])
        a = c.dve(lambda e: e.tensor_scalar(b1c[:], b1c[:], rates[:, 2:3], None, ALU.mult), [ld_b1c, keep])
        c.dve(lambda e: e.scalar_tensor_tensor(b1n[:], sums[:, 0:HC], rates[:, 3:4], b1c[:], ALU.mult, ALU.add), [mm, step, a])
        c.run()
    return last["ld_chunk", 1]


def merge_phase(c, io, shared, halves, g1, g2, b1n, b2n, ld_chunk1):
    nc = c.nc
    with ExitStack() as ctx:
        def sb(name, shape, dt=F32):
            return ctx.enter_context(nc.sbuf_tensor(name, shape, dt))

        def ps(name, shape, dt=F32):
            return ctx.enter_context(nc.psum_tensor(name, shape, dt))

        last = {}
        w1h, w1l = shared.w1
        w2h, w2l = sb("m_w2_h", [P, HC, D], F32R), sb("m_w2_l", [P, HC, D], F32R)
        lin, lin_ready = {}, {}
        lin_f = [sb(f"lin_f{i}", [P, KC, D]) for i in range(2)]
        for n, k in enumerate(("lin1", "lin2")):
            lin[k] = sb(k + "_h", [P, KC, D], F32R), sb(k + "_l", [P, KC, D], F32R)
        gate = sb("gate_w", [P, KC, E])
        gate_b = sb("gate_bias", [P, E])
        ident, before_f = sb("m_ident", [P, P]), sb("m_before_f", [P, P])
        before, ones = sb("m_before", [P, P], BF16), sb("m_ones", [P, P], BF16)
        set_ones = c.pool(lambda e: e.memset(ones[:], 1.0))
        experts = sb("expert_ids", [P, E])
        neg_half = sb("m_neg_half", [P, GRP])
        set_half = c.pool(lambda e: e.memset(neg_half[:], -0.5))
        counts = sb("expert_counts", [P, TOPK, E])
        set_counts = c.pool(lambda e: e.memset(counts[:], 0.0))

        xT_f = [t[:].rearrange("p (k t) -> p k t", k=KC) for t in shared.xT]
        oT = [sb(f"m_oT{i}", [P, KC, T]) for i in range(2)]
        x_t = [t[:].rearrange("p (j d) -> p j d", j=GRP) for t in shared.x]
        (xTh, oTh), (xTl, oTl) = ([t[:, i * KC * T:(i + 1) * KC * T].rearrange("p (k t) -> p k t", k=KC)
                                   for i in range(2)] for t in halves)
        sig = [sb(f"m_sig{i}", [P, T]) for i in range(NZ)]
        hf = [sb(f"m_hf{i}", [P, T]) for i in range(NZ)]
        hh, hl = sb("m_hh", [P, HC, T], F32R), sb("m_hl", [P, HC, T], F32R)
        om, omh, oml = sb("memT", [P, KC, T]), sb("memT_h", [P, KC, T], F32R), sb("memT_l", [P, KC, T], F32R)
        ga, gb = sb("gate1", [P, KC, T]), sb("gate2", [P, KC, T])
        x1 = [sb(f"x1_{i}", [P, GRP, D]) for i in range(2)]
        x2 = [sb(f"xn2_{i}", [P, GRP, ROW]) for i in range(3)]
        x2T = sb("xn2T", [P, KC, T])
        stats, mv, rstd = sb("m_stats", [P, GRP, 6]), sb("m_mv", [P, GRP, 2]), sb("m_rstd", [P, 2, GRP])
        lg = sb("logits", [P, GRP, E])
        pr = sb("router_probs", [P, GRP, E])
        mx, sm = sb("router_max", [P, GRP]), sb("router_sum", [P, 2, GRP])
        top = sb("router_top", [P, GRP, 8])
        idx = sb("router_idx", [P, GRP, 8], mybir.dt.uint32)
        idf = sb("router_idf", [P, TOPK, GRP])
        hot = sb("router_hot", [P, TOPK, GRP, E], BF16)
        pos_e, pos = sb("router_pos_e", [P, TOPK, GRP, E]), sb("router_pos", [P, TOPK, GRP])
        keep = sb("router_keep", [P, TOPK, GRP])
        slot, slot2 = sb("router_slot", [P, TOPK, GRP]), sb("router_slot2", [P, TOPK, GRP])
        sidx = [sb(f"scatter_rows{i}", [P, TOPK, GRP], I32) for i in range(2)]

        tokens = sb("token_numbers", [P, NBLK])
        clear_x2 = [c.pool(lambda e, t=t: e.memset(t[:, :, D:], 0.0)) for t in x2][-1]

        ps_z = [ps(f"m_ps_z{i}", [P, T]) for i in range(NZ)]
        ps_o = [ps(f"m_ps_o{i}", [P, T]) for i in range(2)]
        ps_r = ps("m_ps_r", [P, GRP, D])
        ps_s = ps("m_ps_s", [P, 512])
        ps_l, ps_c = ps_s[:, 0:GRP * E], ps_s[:, GRP * E:]
        x_v = io["x"].rearrange("(g j p) d -> g p j d", j=GRP, p=P)
        x1_v = io["out"].rearrange("(g j p) d -> g p j d", j=GRP, p=P)
        turn = [0]

        def load_xT(C):
            last["ld_xT", C] = load_chunk(c, io, shared, C, [last["xTl", C - 2]])

        def load_oT(C):
            s = C % 2
            for h in range(2):
                t = slice(2 * h * P, (2 * h + 2) * P)
                last["ld_oT", C] = c.dma(c.sync, f"m_oT{s}", oT[s][:, :, t], io["oT_d"][2 * C + h], [last.get(("merge", C - 2))])

        def load_x(C):
            s = C % 2
            last["ld_x", C] = c.dma(c.sync, f"m_x{s}", x_t[s][:], x_v[C], [last.get(("x1", C - 2))])

        def split_xT(C):
            s = C % 2
            h = c.act(act_copy(xTh[:], xT_f[s][:]), [last["ld_xT", C], last.get(("z", C - 1))])
            last["xTl", C] = c.dve(sub(xTl[:], xT_f[s][:], xTh[:]), [h, last.get(("z", C - 1))])

        def split_oT(C):
            s = C % 2
            h = c.act(act_copy(oTh[:], oT[s][:]), [last["ld_oT", C], last.get(("g1", C - 1))])
            last["oTl", C] = c.dve(sub(oTl[:], oT[s][:], oTh[:]), [h, last.get(("g1", C - 1))])

        def hidden(C, t):
            r, mc = (HC * C + t) % NZ, slice(t * P, (t + 1) * P)
            acc, key = ps_z[r], ("ps_z", r)
            z = c.pe(matmul_split(acc[:], [(w1h[:, k, mc], w1l[:, k, mc]) for k in range(KC)],
                                  [(xTh[:, k], xTl[:, k]) for k in range(KC)]), [last["xTl", C], last.get(key)])
            last["z", C] = z
            s = c.act(lambda e: e.activation(sig[r][:], acc[:], ACTF.Sigmoid, bias=b1n[:, t:t + 1]), [z, last.get(("hf", r))])
            h = c.dve(lambda e: e.scalar_tensor_tensor(hf[r][:], acc[:], b1n[:, t:t + 1], sig[r][:], ALU.add, ALU.mult),
                      [s, last.get(("hl", r))])
            last[key] = last["hf", r] = last["h", C, t] = h

        def split_hidden(C, t):
            r = (HC * C + t) % NZ
            h = last["h", C, t]
            hi = c.act(act_copy(hh[:, t], hf[r][:]), [h, last.get(("om", C - 1))])
            last["hl", r] = last["hl", C, t] = (c.dve if t == HC - 1 else c.pool)(sub(hl[:, t], hf[r][:], hh[:, t]), [hi, last.get(("om", C - 1))])

        def bank():
            turn[0] += 1
            return ps_o[turn[0] % 2], ("ps_o", turn[0] % 2)

        def linear_gate(C, name, dst, high, low, ready, free):
            wh, wl = lin[name]
            for m in range(KC):
                acc, key = bank()
                mc = slice(m * P, (m + 1) * P)
                mm = c.pe(matmul_split(acc[:], [(wh[:, k, mc], wl[:, k, mc]) for k in range(KC)],
                                       [(high[:, k], low[:, k]) for k in range(KC)]), [ready, lin_ready[name], last.get(key)])
                last[key] = a = c.act(lambda e, m=m, acc=acc: e.activation(dst[:, m], acc[:], ACTF.Sigmoid), [mm] + free)
            return mm, a

        def memory_out(C, m, half):
            if half == 0:
                last["acc", m] = bank()
            acc, key = last["acc", m]
            mc, ks = slice(m * P, (m + 1) * P), range(4 * half, 4 * half + 4)
            mm = c.pe(matmul_split(acc[:], [(w2h[:, k, mc], w2l[:, k, mc]) for k in ks],
                                   [(hh[:, k], hl[:, k]) for k in ks], first=half == 0, last=half == 1),
                      [last["hl", C, k] for k in ks] + [last["w2"], last.get(key)])
            last["om", C] = mm
            if half:
                f = c.act(lambda e: e.activation(om[:, m], acc[:], ACTF.Identity, bias=b2n[:, m:m + 1]),
                          [mm, last.get(("merge_om", C - 1)), last.get(("oml", C - 1, m))])
                hi = c.act(lambda e: e.activation(omh[:, m], acc[:], ACTF.Identity, bias=b2n[:, m:m + 1]), [mm, last.get(("g2", C - 1))])
                last[key] = hi
                last["oml", C, m] = c.dve(sub(oml[:, m], om[:, m], omh[:, m]), [f, hi, last.get(("g2", C - 1))])

        def gate1(C):
            mm, last["ga", C] = linear_gate(C, "lin1", ga, oTh, oTl, last["oTl", C], [last.get(("merge", C - 1)), last.get(("mergeT", C - 1))])
            last["g1", C] = mm

        def gate2(C):
            mm, g = linear_gate(C, "lin2", gb, omh, oml, last["oml", C, 1], [last.get(("merge", C - 1))])
            last["g2", C] = mm
            s = C % 2
            a = c.dve(lambda e: e.tensor_tensor(ga[:], ga[:], oT[s][:], ALU.mult), [last["ga", C]])
            last["merge_om", C] = b = c.dve(lambda e: e.tensor_tensor(gb[:], gb[:], om[:], ALU.mult), [g, last["oml", C, 0]])
            last["merge", C] = c.dve(add(ga[:], ga[:], gb[:]), [a, b])

        def residual(C):
            def emit(e):
                for j in range(GRP):
                    for m in range(KC):
                        i = e.transpose(ps_r[:, j, m * P:(m + 1) * P], ga[:, m, j * P:(j + 1) * P], ident[:])
                return i
            t = c.pe(emit, [last["merge", C], ld_ident, last.get("ps_r")])
            last["mergeT", C] = t
            y = x1[C % 2]
            a = c.dve(add(y[:], ps_r[:], x_t[C % 2][:]), [t, last["ld_x", C], last.get(("x1_st", C - 2)), last.get(("ln2", C - 2))])
            last["ps_r"] = last["x1", C] = a
            last["x1_st", C] = c.dma(c.sync, f"x1_st{C % 2}", x1_v[C], y[:], [a])

        def norm_stats(C):
            y, a = x1[C % 2], last["x1", C]
            for j in range(GRP):
                b = c.dve(lambda e, j=j: e.bn_stats(stats[:, j], y[:, j]), [a, last.get("mv")])
            for j in range(GRP):
                g = c.dve(lambda e, j=j: e.bn_aggr(mv[:, j], stats[:, j]), [b, last.get(("ln2", C - 1))])
            last["mv"] = g
            v = c.dve(lambda e: e.tensor_scalar(rstd[:, 0], mv[:, :, 1], EPS, None, ALU.add), [g, last.get("rstd")])
            r = c.pool(lambda e: e.tensor_tensor(rstd[:, 1], rstd[:, 0], neg_half[:], ALU.pow), [v, set_half, last.get(("ln2", C - 1))])
            last["rstd"] = r

        def norm_apply(C):
            y, z, r = x1[C % 2], x2[C % 3], last["rstd"]
            for j in range(GRP):
                n = c.dve(lambda e, j=j: e.tensor_scalar(z[:, j, 0:D], y[:, j], mv[:, j, 0:1], rstd[:, 1, j:j + 1], ALU.subtract, ALU.mult),
                          [r] + last.get(("scatter", C - 3), []))
            last["ln2", C] = n
            last["numbered"] = c.dve(copy(z[:, :, D], tokens[:, C * GRP:(C + 1) * GRP]), [ld_tokens, clear_x2] + last.get(("scatter", C - 3), []))

        def transpose_x2(C):
            z = x2[C % 3]

            def emit(e):
                for m in range(KC):
                    for j in range(GRP):
                        i = e.transpose(ps_r[:, 2 * m + j // 2, (j % 2) * P:(j % 2 + 1) * P], z[:, j, m * P:(m + 1) * P], ident[:])
                return i
            t = c.pe(emit, [last["ln2", C], last.get("ps_r")])
            last["x2T", C] = last["ps_r"] = c.act(act_copy(x2T[:].rearrange("p m t -> p (m t)"), ps_r[:].rearrange("p a b -> p (a b)")),
                                                  [t, last.get(("logits", C - 1))])

        def router(C):
            def emit(e):
                for j in range(GRP):
                    for k in range(KC):
                        i = e.matmul(ps_l[:, j * E:(j + 1) * E], x2T[:, k, j * P:(j + 1) * P], gate[:, k], start=k == 0, stop=k == KC - 1)
                return i
            mm = c.pe(emit, [last["x2T", C], ld_gate, last.get("ps_s")])
            last["logits", C] = mm
            wide = [P, GRP, E]
            src = ps_l.rearrange("p (j x) -> p j x", x=E)
            a = c.dve(add(lg[:], src, gate_b[:].unsqueeze(1).broadcast_to(wide)), [mm, ld_gb, last.get("sh")])
            last["ps_s"] = a
            m = c.dve(lambda e: e.tensor_reduce(mx[:], lg[:], AX.X, ALU.max), [a, last.get("sh")])
            s = c.dve(sub(lg[:], lg[:], mx[:].unsqueeze(2).broadcast_to(wide)), [m, last.get("ex")])
            last["sh"] = s
            x = c.act(lambda e: e.activation(pr[:], lg[:], ACTF.Exp), [s, last.get("find")])
            last["ex"] = x

        def choose(C):
            wide, x = [P, GRP, E], last["ex"]
            r = c.dve(lambda e: e.tensor_reduce(sm[:, 0], pr[:], AX.X, ALU.add), [x, last.get("probs")])
            r = c.dve(lambda e: e.reciprocal(sm[:, 1], sm[:, 0]), [r])
            q = c.dve(lambda e: e.tensor_tensor(pr[:], pr[:], sm[:, 1].unsqueeze(2).broadcast_to(wide), ALU.mult), [r])
            last["probs"] = q
            for j in range(GRP):
                t = c.dve(lambda e, j=j: e.max(top[:, j], pr[:, j]), [q, last.get("weights")])
            for j in range(GRP):
                f = c.dve(lambda e, j=j: e.max_index(idx[:, j], top[:, j], pr[:, j]), [t, last.get("idf")])
            last["find"] = f
            d = c.dve(copy(idf[:], idx[:, :, 0:TOPK].rearrange("p j k -> p k j")), [f, last.get("slots")])
            last["idf"] = d
            for k in range(TOPK):
                o = c.dve(lambda e, k=k: e.tensor_tensor(hot[:, k], experts[:].unsqueeze(1).broadcast_to(wide),
                                                         idf[:, k].unsqueeze(2).broadcast_to(wide), ALU.is_equal),
                          [d, ld_exp, last.get("pos_e"), last.get("count_pe")])
            last["hot", C] = o

        def dispatch(C):
            n = TOPK * E

            def emit(e):
                for j in range(GRP + 1):
                    out = ps_c[:, j * n:(j + 1) * n].rearrange("p (k x) -> p k x", x=E)
                    for i in range(min(j, GRP - 1) + 1):
                        lhs = before if i == j else ones
                        x = e.matmul(out, lhs[:], hot[:, :, i], start=i == 0, stop=i == min(j, GRP - 1))
                return x
            mm = c.pe(emit, [last["hot", C], before_ready, set_ones, last.get("ps_s")])
            last["count_pe"] = mm
            wide = [P, GRP, E]
            for k in range(TOPK):
                src = ps_c[:, 0:GRP * n].rearrange("p (j k x) -> p j k x", k=TOPK, x=E)[:, :, k]
                a = c.dve(add(pos_e[:, k], src, counts[:, k].unsqueeze(1).broadcast_to(wide)), [mm, set_counts, last.get("counts"), last.get("pos")])
            cn = c.dve(add(counts[:], counts[:], ps_c[:, GRP * n:(GRP + 1) * n].rearrange("p (k x) -> p k x", x=E)), [a, mm])
            last["ps_s"] = last["counts"] = cn
            b = c.dve(lambda e: e.tensor_tensor(pos_e[:], pos_e[:], hot[:], ALU.mult), [a])
            last["pos_e"] = b
            p = c.dve(lambda e: e.tensor_reduce(pos[:], pos_e[:], AX.X, ALU.add), [b, last.get("slots")])
            last["pos"] = p
            k1 = c.dve(lambda e: e.tensor_scalar(keep[:], pos[:], float(CAP), None, ALU.is_lt), [p, last.get("slots")])
            s = c.dve(lambda e: e.scalar_tensor_tensor(slot[:], idf[:], float(CAP), pos[:], ALU.mult, ALU.add), [p, last.get("slots")])
            s = c.dve(lambda e: e.tensor_scalar(slot[:, 1], slot[:, 1], float(NSLOT), None, ALU.add), [s])
            u = c.dve(lambda e: e.tensor_scalar(slot2[:], keep[:], -OUTSIDE, OUTSIDE, ALU.mult, ALU.add), [k1, last.get("slots")])
            sc = c.dve(add(sidx[C % 2][:], slot[:], slot2[:]), [s, u] + last.get(("scatter", C - 2), []))
            w = c.dve(lambda e: e.tensor_tensor(x2[C % 3][:, :, D + 1:D + 1 + TOPK], top[:, :, 0:TOPK],
                                                keep[:].rearrange("p k j -> p j k"), ALU.mult), [k1, clear_x2] + last.get(("scatter", C - 3), []))
            last["weights"] = w
            last["slots"] = sc
            last["sidx", C] = sc

        def scatter(C):
            for k in range(TOPK):
                for j in range(GRP):
                    st = c.scatter(f"scatter{C % 3}", io["xbuf_d"], sidx[C % 2][:, k, j:j + 1], x2[C % 3][:, j], SLOTS,
                                   [last["sidx", C], last["weights"], last["numbered"]])
            last["scatter", C] = [st]

        last["xTl", 0], last["ld_xT", 1] = None, ld_chunk1
        load_oT(0)
        load_x(0)
        ld_gate = c.dma(c.sync, "gate_w", gate[:], io["gateT"].rearrange("(c p) n -> p c n", p=P))
        ld_gb = c.dma(c.sync, "gate_b", gate_b[:], io["gate_b"])
        ld_ident = c.dma(c.sync, "m_ident", ident[:], io["ident"])
        ld_before = c.dma(c.sync, "m_before", before_f[:], io["before"])
        ld_exp = c.dma(c.sync, "m_experts", experts[:], io["experts"])
        ld_tokens = c.dma(c.sync, "m_tokens", tokens[:], io["tokens"])
        for n, k in enumerate(("lin1", "lin2")):
            last["ld", k] = c.dma(c.sync, k, lin_f[n][:], io[k + "T"].rearrange("(c p) n -> p c n", p=P))

        def split_lin(n):
            k = ("lin1", "lin2")[n]
            hi = c.act(act_copy(lin[k][0][:], lin_f[n][:]), [last["ld", k]])
            lin_ready[k] = c.dve(sub(lin[k][1][:], lin_f[n][:], lin[k][0][:]), [hi])

        def split_w2(k):
            r = slice(4 * k, 4 * k + 4)
            hi = c.act(act_copy(w2h[:, r], g2[:, r]))
            last["w2"] = c.dve(sub(w2l[:, r], g2[:, r], w2h[:, r]), [hi])

        begin = {3: lambda: split_oT(0), 4: lambda: split_lin(0), 5: lambda: split_w2(0), 6: lambda: split_w2(1),
                 7: lambda: split_lin(1)}
        for C in range(NCH):
            tail, sent = C >= 1, C >= 2
            hidden(C, 0)
            hidden(C, 1)
            split_hidden(C, 0)
            if tail:
                gate2(C - 1)
            if C + 1 < NCH:
                load_oT(C + 1)
            hidden(C, 2)
            split_hidden(C, 1)
            if sent:
                choose(C - 2)
            for t in (3, 4, 5):
                hidden(C, t)
                split_hidden(C, t - 1)
                if C == 0:
                    begin[t]()
            if tail:
                residual(C - 1)
            if C + 1 < NCH:
                load_x(C + 1)
            hidden(C, 6)
            split_hidden(C, 5)
            if C == 0:
                begin[6]()
            if sent:
                dispatch(C - 2)
            hidden(C, 7)
            gate1(C)
            split_hidden(C, 6)
            split_hidden(C, 7)
            if C == 0:
                begin[7]()
                before_ready = c.dve(copy(before[:], before_f[:]), [ld_before])
                first_w1 = c.dma(c.sync, "e_w1", g1[:], io["W1"][0].rearrange("(c p) n -> p c n", p=P))
                first_w2 = c.dma(c.sync, "e_w2", g2[:], io["W2"][0].rearrange("(c p) n -> p c n", p=P), [last["w2"]])
            if tail:
                norm_stats(C - 1)
                norm_apply(C - 1)
            if sent:
                scatter(C - 2)
            if C + 1 < NCH:
                split_xT(C + 1)
            memory_out(C, 0, 0)
            memory_out(C, 0, 1)
            if C + 1 < NCH:
                split_oT(C + 1)
            memory_out(C, 1, 0)
            if tail:
                transpose_x2(C - 1)
            memory_out(C, 1, 1)
            if tail:
                router(C - 1)
            if C + 2 < NCH:
                load_xT(C + 2)
        C = NCH - 1
        choose(C - 1)
        gate2(C)
        residual(C)
        norm_stats(C)
        norm_apply(C)
        transpose_x2(C)
        dispatch(C - 1)
        scatter(C - 1)
        router(C)
        choose(C)
        dispatch(C)
        scatter(C)
        ends = [last["x1_st", C] for C in (NCH - 1, NCH - 2)]
        for C in range(NCH - 3, NCH):
            ends += last["scatter", C][-1:]
        c.sync(lambda e: e.nop(), ends)
        c.run()
    return first_w1, first_w2


def expert_phase(c, io, shared, s1, s2, first_w1, first_w2):
    nc = c.nc
    with ExitStack() as ctx:
        def sb(name, shape, dt=F32):
            return ctx.enter_context(nc.sbuf_tensor(name, shape, dt))

        def ps(name, shape, dt=F32):
            return ctx.enter_context(nc.psum_tensor(name, shape, dt))

        last = {}
        ident = sb("e_ident", [P, P])
        b1, b2 = sb("e_b1", [P, E, HC]), sb("e_b2", [P, E, KC])
        w1h, w1l = shared.w1
        w2h, w2l = sb("e_w2_h", [P, HC, D], F32R), sb("e_w2_l", [P, HC, D], F32R)
        xs = [sb(f"slots{i}", [P, SB, ROW]) for i in range(2)]
        xh, xl = sb("slotsT_h", [P, KC, CAP], F32R), sb("slotsT_l", [P, KC, CAP], F32R)
        hf = [sb(f"e_hf{i}", [P, CAP]) for i in range(NHF)]
        hh, hl = sb("e_hh", [P, HC, CAP], F32R), sb("e_hl", [P, HC, CAP], F32R)
        yT = sb("e_yT", [P, KC, CAP])
        ys = sb("e_ys", [P, SB, D])
        base = sb("token_rows", [P, SB, D])
        clear = c.pool(lambda e: e.memset(base[:], 0.0))
        empty = sb("slot_empty", [P, SB])
        token = [sb(f"slot_token{i}", [P, SB], I32) for i in range(2)]
        prob = [sb(f"slot_prob{i}", [P, SB]) for i in range(2)]
        ps_z = [ps(f"e_ps_z{i}", [P, 2, 512]) for i in range(2)]
        ps_x = ps("e_ps_x", [P, 4 * D])
        ps_t = ps("e_ps_t", [P, 4, D])
        x_v = io["xbuf_d"].rearrange("(i b p) d -> i p b d", b=SB, p=P)
        N = TOPK * E

        def load_slots(i):
            last["xs", i] = c.dma(c.sync, f"slots{i % 2}", xs[i % 2][:], x_v[i], [last.get(("xT_pe", i - 2)), last.get(("meta", i - 2))])

        def slot_tokens(i):
            x, t = xs[i % 2], token[i % 2]
            a = c.dve(lambda e: e.tensor_scalar(empty[:], x[:, :, D], 0.0, OUTSIDE, ALU.is_equal, ALU.mult), [last["xs", i], last.get(("token", i - 1))])
            last["token", i] = c.dve(lambda e: e.scalar_tensor_tensor(t[:], x[:, :, D], -1.0, empty[:], ALU.add, ALU.add), [a] + last.get(("scatter", i - 2), []))
            last["meta", i] = c.dve(copy(prob[i % 2][:], x[:, :, D + 1 + i // E]), [last["xs", i], last.get(("sum", i - 2))])

        def load_w1(i):
            last["ld_w1", i] = c.dma(c.sync, "e_w1", s1[:], io["W1"][i % E].rearrange("(c p) n -> p c n", p=P), [last.get(("w1", i - 1))])

        def load_w2(i):
            last["ld_w2", i] = c.dma(c.sync, "e_w2", s2[:], io["W2"][i % E].rearrange("(c p) n -> p c n", p=P), [last.get(("w2", i - 1))])

        def split_w1(i):
            for k in range(KC):
                hi = c.act(act_copy(w1h[:, k], s1[:, k]), [last["ld_w1", i], last.get(("h", i - 1))])
                last["w1", i] = c.dve(sub(w1l[:, k], s1[:, k], w1h[:, k]), [hi, last.get(("h", i - 1))])

        def split_w2(i, k):
            r = slice(4 * k, 4 * k + 4)
            hi = c.act(act_copy(w2h[:, r], s2[:, r]), [last["ld_w2", i], last.get(("y", i - 1))])
            last["w2", i] = c.dve(sub(w2l[:, r], s2[:, r], w2h[:, r]), [hi, last.get(("y", i - 1))])

        def transpose_slots(i, blocks):
            n = len(blocks)

            def emit(e):
                for m in range(KC):
                    for a, b in enumerate(blocks):
                        x = e.transpose(ps_x[:, (m * n + a) * P:(m * n + a + 1) * P], xs[i % 2][:, b, m * P:(m + 1) * P], ident[:])
                return x
            t = c.pe(emit, [last["xs", i], ld_ident, last.get("ps_x")])
            last["xT_pe", i] = t
            cols = slice(blocks[0] * P, (blocks[-1] + 1) * P)
            src = ps_x[:, 0:KC * n * P].rearrange("p (m t) -> p m t", m=KC)
            hi = c.act(act_copy(xh[:, :, cols], src), [t, last.get(("h", i - 1))])
            last["ps_x"] = last["xT", i] = c.dve(sub(xl[:, :, cols], src, xh[:, :, cols]), [hi, last.get(("h", i - 1))])

        turn = [0]

        def bank():
            turn[0] += 1
            return ps_z[turn[0] % 2], ("ps_z", turn[0] % 2)

        def product(out, lhs, rhs, after, first=True, last=True):
            def emit(e):
                for s in range(2):
                    cols = slice(s * HALF, (s + 1) * HALF)
                    x = matmul_split(out[:, s, 0:HALF], lhs, [(h[:, cols], l[:, cols]) for h, l in rhs], first, last)(e)
                return x
            return c.pe(emit, after)

        def up(i, t):
            e_, mc, (out, key), r = i % E, slice(t * P, (t + 1) * P), bank(), t % NHF
            mm = product(out, [(w1h[:, k, mc], w1l[:, k, mc]) for k in range(KC)],
                         [(xh[:, k], xl[:, k]) for k in range(KC)], [last["xT", i], last["w1", i], last.get(key)])
            last["h", i] = mm
            f = c.act(lambda e: e.activation(hf[r][:].rearrange("p (s n) -> p s n", s=2), out[:, :, 0:HALF], ACTF.Relu, bias=b1[:, e_, t:t + 1]),
                      [mm, ld_b1, last.get(("hl_buf", r))])
            last[key] = f
            hi = c.dve(copy(hh[:, t], hf[r][:]), [f, last.get(("y", i - 1))])
            last["hl_buf", r] = last["hl", t] = (c.dve if t % 4 == 3 else c.pool)(sub(hl[:, t], hf[r][:], hh[:, t]), [hi, last.get(("y", i - 1))])

        def down(i, m, half):
            if half == 0:
                last["acc", m] = bank()
            out, key = last["acc", m]
            mc, ks = slice(m * P, (m + 1) * P), range(4 * half, 4 * half + 4)
            mm = product(out, [(w2h[:, k, mc], w2l[:, k, mc]) for k in ks], [(hh[:, k], hl[:, k]) for k in ks],
                         [last["hl", k] for k in ks] + [last["w2", i], last.get(key)], half == 0, half == 1)
            last["y", i] = mm
            if half:
                last[key] = last["yT", i] = c.act(
                    lambda e: e.activation(yT[:, m].rearrange("p (s n) -> p s n", s=2), out[:, :, 0:HALF], ACTF.Identity, bias=b2[:, i % E, m:m + 1]),
                    [mm, ld_b2, last.get(("yT_pe", i - 1))])

        def transpose_y(i, blocks):
            def emit(e):
                for a, b in enumerate(blocks):
                    for m in range(KC):
                        x = e.transpose(ps_t[:, a, m * P:(m + 1) * P], yT[:, m, b * P:(b + 1) * P], ident[:])
                return x
            t = c.pe(emit, [last["yT", i], last.get("ps_t")])
            last["yT_pe", i] = t
            for a, b in enumerate(blocks):
                d = c.dve(lambda e, a=a, b=b: e.scalar_tensor_tensor(ys[:, b], ps_t[:, a], prob[i % 2][:, b:b + 1], base[:, b], ALU.mult, ALU.add),
                          [t, last["gather", i], last["meta", i]] + last.get(("scatter", i - 1), []))
            last["ps_t"] = last["sum", i] = d

        def gather(i):
            for b in range(SB):
                st = c.gather("gather", base[:, b], io["out"], token[i % 2][:, b:b + 1], NT,
                              [last["token", i], clear, last.get(("sum", i - 1))] + last.get(("scatter", i - 1), []))
            last["gather", i] = st

        def scatter(i, blocks):
            for b in blocks:
                st = c.scatter("scatter", io["out"], token[i % 2][:, b:b + 1], ys[:, b], NT, [last["sum", i]])
            last["scatter", i] = [st]

        load_slots(0)
        ld_ident = c.dma(c.sync, "e_ident", ident[:], io["ident"])
        ld_b1 = c.dma(c.sync, "e_b1", b1[:], io["eb1"])
        ld_b2 = c.dma(c.sync, "e_b2", b2[:], io["eb2"])
        load_slots(1)
        last["ld_w1", 0], last["ld_w2", 0] = first_w1, first_w2
        split_w1(0)
        slot_tokens(0)
        transpose_slots(0, [0, 1, 2, 3])
        transpose_slots(0, [4])
        split_w2(0, 0)
        split_w2(0, 1)
        load_w1(1)
        load_w2(1)
        for i in range(N):
            for t in range(HC):
                up(i, t)
                if i and t in (1, 3):
                    split_w2(i, t // 2)
                if i and t == 2:
                    transpose_y(i - 1, [0, 1, 2, 3])
                if i and t == 3:
                    scatter(i - 1, [0, 1])
                if i and t == 4:
                    transpose_y(i - 1, [4])
                    if i + 1 < N:
                        load_w2(i + 1)
                if i and t == 5:
                    scatter(i - 1, [2])
            if i:
                scatter(i - 1, [3, 4])
            if i + 1 < N:
                split_w1(i + 1)
            down(i, 0, 0)
            gather(i)
            if i + 1 < N:
                slot_tokens(i + 1)
                transpose_slots(i + 1, [0, 1, 2, 3])
            down(i, 0, 1)
            down(i, 1, 0)
            if i + 1 < N:
                transpose_slots(i + 1, [4])
            down(i, 1, 1)
            if i + 2 < N:
                load_w1(i + 2)
                load_slots(i + 2)
        for blocks in ([0, 1, 2, 3], [4]):
            transpose_y(N - 1, blocks)
            scatter(N - 1, blocks)
        c.sync(lambda e: e.nop(), last["scatter", N - 1])
        c.run()


def build(nc, io):
    io["xn_d"] = nc.dram_tensor("xn_d", [NPAIR + 1, P, 2, D], F32).ap()
    io["xT_d"] = nc.dram_tensor("xT_d", [NPAIR + 1, P, KC, 2 * P], F32).ap()
    io["oT_d"] = nc.dram_tensor("oT_d", [NPAIR + 1, P, KC, 2 * P], F32).ap()
    io["xbuf_d"] = nc.dram_tensor("xbuf_d", [SLOTS, ROW], F32).ap()
    with ExitStack() as ctx:
        def sb(name, shape, dt=F32):
            return ctx.enter_context(nc.sbuf_tensor(name, shape, dt))

        c = Core(nc, ctx)
        shared = Shared(sb)
        prepared = attention_phase(c, io, shared)
        g1, g2 = sb("new_w1T", [P, KC, HID]), sb("new_w2T", [P, HC, D])
        b1n, b2n = sb("new_b1", [P, HC]), sb("new_b2", [P, KC])
        halves = [sb(f"halves_{k}", [P, HC * 2 * P], F32R) for k in ("h", "l")]
        ld_chunk1 = gradient_phase(c, io, shared, halves, g1, g2, b1n, b2n, *prepared)
        first_w1, first_w2 = merge_phase(c, io, shared, halves, g1, g2, b1n, b2n, ld_chunk1)
        expert_phase(c, io, shared, g1, g2, first_w1, first_w2)


def window_masks():
    q, k = np.arange(P)[:, None], np.arange(P)[None]
    masks = np.full((3, P, 2 * P), -1e30, np.float32)
    masks[0, :, :P][k > q] = 0
    masks[0, :, P:][k <= q] = 0
    masks[1] = masks[0]
    masks[1, :, :P - NMEM] = -1e30
    masks[2, :, :P][(k >= P - NMEM) & (k <= q)] = 0
    return masks


def layouts(a):
    t = np.ascontiguousarray
    io = {"x": a["L0_attn_x"].reshape(NT, D), "memp": np.zeros((P, D), np.float32)}
    io["memp"][P - NMEM:] = a["L0_attn_mem"]
    for k in ("wq", "wk", "wv", "wo", "w1", "w2", "lin1", "lin2"):
        io[k + "T"] = t(a["L0_attn_" + k].T)
    io["w2"], io["b1"] = a["L0_attn_w2"], t(np.broadcast_to(a["L0_attn_b1"], (P, HID)))
    io["b1c"] = t(a["L0_attn_b1"].reshape(HC, P).T)
    io["b2c"] = t(a["L0_attn_b2"].reshape(KC, P).T)
    io["rates"] = np.empty((P, 2), np.float32)
    io["rates"][:, 0], io["rates"][:, 1] = a["L0_attn_alpha"], a["L0_attn_theta"]
    io["gateT"] = t(a["L0_ffn_gate_w"].T)
    io["gate_b"] = t(np.broadcast_to(a["L0_ffn_gate_b"], (P, E)))
    io["W1"], io["W2"] = a["L0_ffn_W1"], a["L0_ffn_W2"]
    io["eb1"] = t(a["L0_ffn_b1"].reshape(E, HC, P).transpose(2, 0, 1))
    io["eb2"] = t(a["L0_ffn_b2"].reshape(E, KC, P).transpose(2, 0, 1))
    io["ident"] = np.eye(P, dtype=np.float32)
    io["masks"] = window_masks()
    io["before"] = np.triu(np.ones((P, P), np.float32), 1)
    io["tokens"] = t(1 + np.arange(NT, dtype=np.float32).reshape(NBLK, P).T)
    io["experts"] = t(np.broadcast_to(np.arange(E, dtype=np.float32), (P, E)))
    io["mem_scale"] = np.zeros((P, P), np.float32)
    io["mem_scale"][:, P - NMEM:] = B
    return io


def kernel(**inputs):
    import concourse.bacc as bacc
    from concourse.bass_utils import run_bass_kernel_spmd

    arrays = layouts({k: np.asarray(v) for k, v in inputs.items()})
    nc = bacc.Bacc("TRN2", target_bir_lowering=False, num_devices=1)
    io = {k: nc.dram_tensor("in_" + k, v.shape, F32, kind="ExternalInput").ap() for k, v in arrays.items()}
    io["out"] = nc.dram_tensor("out", [NT, D], F32, kind="ExternalOutput").ap()
    build(nc, io)
    r = run_bass_kernel_spmd(nc, [{"in_" + k: v for k, v in arrays.items()}], core_ids=[0])
    return r.results[0]["out"].reshape(B, S, D)
```
